# Optimizing a Trainium2 kernel written in Bass

```python
import numpy as np
import jax
import jax.numpy as jnp

def _softmax(x, axis=-1):
    return jax.nn.softmax(x, axis=axis)

def _gelu(x):
    return jax.nn.gelu(x, approximate=True)

def _silu(x):
    return jax.nn.silu(x)

def _sigmoid(x):
    return jax.nn.sigmoid(x)

def _layernorm(x, axis=-1, eps=1e-05):
    m = jnp.mean(x, axis=axis, keepdims=True)
    v = jnp.var(x, axis=axis, keepdims=True)
    return (x - m) / jnp.sqrt(v + eps)

def _scatter_add(tgt, idx, src, axis=0):
    return tgt.at[idx].add(src)

def _segment_sum(src, seg, n):
    return jax.ops.segment_sum(src, seg, n)
kernel_name = 'mk_adaln_d2_jaxref_r8_e0170f'

def setup_inputs(seed: int=0):
    np.random.seed(seed)
    _w = jnp.asarray

    def _L0_attn_setup():
        import jax, jax.numpy as jnp
        import numpy as np
        DIM = 128
        HEADS = 16
        DIM_HEAD = DIM // HEADS
        LATENT = DIM // 4
        SCALE = DIM_HEAD ** (-0.5)
        key = jax.random.key(seed)
        ks = jax.random.split(key, 8)
        B, S = (2, 256)
        init = lambda k, shape, fan_in: jax.random.normal(k, shape, jnp.float32) * fan_in ** (-0.5)
        return {'x': jax.random.normal(ks[0], (B, S, DIM), jnp.float32), 'Wq': init(ks[1], (DIM, DIM), DIM), 'bq': jnp.zeros((DIM,), jnp.float32), 'Wl': init(ks[2], (DIM, LATENT), DIM), 'bl': jnp.zeros((LATENT,), jnp.float32), 'Wk': init(ks[3], (LATENT, DIM), LATENT), 'bk': jnp.zeros((DIM,), jnp.float32), 'Wv': init(ks[4], (LATENT, DIM), LATENT), 'bv': jnp.zeros((DIM,), jnp.float32), 'Wo': init(ks[5], (DIM, DIM), DIM), 'bo': jnp.zeros((DIM,), jnp.float32)}
    _L0_attn_in = _L0_attn_setup()

    def _L0_ffn_setup():
        import jax, jax.numpy as jnp
        import numpy as np
        D_IN, D_HID = (128, 512)

        def _ternary(key, shape):
            return jax.random.randint(key, shape, -1, 2).astype(jnp.float32)

        def _tlin(x, w, s):
            return jnp.einsum('bsi,oi->bso', x, w) * s
        key = jax.random.key(seed)
        ks = jax.random.split(key, 12)
        inv = lambda fan: 1.0 / np.sqrt(fan).astype(np.float32)
        return {'x': jax.random.normal(ks[0], (4, 256, D_IN), dtype=jnp.float32), 'w1_w': _ternary(ks[1], (D_HID, D_IN)), 'w1_s': jax.random.uniform(ks[2], (D_HID,), dtype=jnp.float32) * inv(D_IN), 'w2_w': _ternary(ks[3], (D_HID, D_IN)), 'w2_s': jax.random.uniform(ks[4], (D_HID,), dtype=jnp.float32) * inv(D_IN), 'h1_w': _ternary(ks[5], (D_HID, D_HID)), 'h1_s': jax.random.uniform(ks[6], (D_HID,), dtype=jnp.float32) * inv(D_HID), 'h2_w': _ternary(ks[7], (D_HID, D_HID)), 'h2_s': jax.random.uniform(ks[8], (D_HID,), dtype=jnp.float32) * inv(D_HID), 'w3_w': _ternary(ks[9], (D_IN, D_HID)), 'w3_s': jax.random.uniform(ks[10], (D_IN,), dtype=jnp.float32) * inv(D_HID)}
    _L0_ffn_in = _L0_ffn_setup()
    _L0_c = _w((lambda *s: np.random.randn(*s).astype(np.float32) * 0.05)(16, 128))
    _L0_wmod = _w((lambda *s: np.random.randn(*s).astype(np.float32) * 0.05)(128, 6 * 128) * 128 ** (-0.5))

    def _L1_attn_setup():
        import jax, jax.numpy as jnp
        import numpy as np
        B, S, D, H = (4, 256, 128, 4)
        HD = D // H

        def _reference_tuple_inner(hidden_states, Wq, Wk, Wv, Wo, bo, betas, mem, z):
            b, s, d = hidden_states.shape
            h = betas.shape[1]
            hd = d // h

            def split(x):
                return x.reshape(b, s, h, hd).transpose(0, 2, 1, 3)
            q = split(hidden_states @ Wq.T)
            k = split(hidden_states @ Wk.T)
            v = split(hidden_states @ Wv.T)
            aw = jnp.einsum('bhqd,bhkd->bhqk', q, k)
            causal = jnp.tril(jnp.ones((s, s), bool))
            aw = jnp.where(causal, aw, jnp.finfo(aw.dtype).min)
            p = jax.nn.softmax(aw, axis=-1)
            attn = jnp.einsum('bhqk,bhkd->bhqd', p, v)
            sq = jax.nn.elu(q) + 1.0
            sk = jax.nn.elu(k) + 1.0
            A_mem = jnp.einsum('bhsd,hde->bhse', sq, mem) / (jnp.einsum('bhsd,hdo->bhso', sq, z) + 1e-06)
            g = jax.nn.sigmoid(betas)
            out = g * A_mem + (1.0 - g) * attn
            delta = jnp.einsum('bhsd,hde->bhse', sk, mem) / (jnp.einsum('bhsd,hdo->bhso', sk, z) + 1e-06)
            mem_new = mem + jnp.einsum('bhsd,bhse->hde', sk, v - delta) / b
            z_new = z + jnp.mean(jnp.sum(sk, axis=2), axis=0)[:, :, None]
            out = out.transpose(0, 2, 1, 3).reshape(b, s, d)
            out = out @ Wo.T + bo
            return (out, mem_new, z_new)
        key = jax.random.key(seed)
        ks = jax.random.split(key, 6)
        s = 0.02
        return {'hidden_states': jax.random.normal(ks[0], (B, S, D), jnp.float32), 'Wq': jax.random.normal(ks[1], (D, D), jnp.float32) * s, 'Wk': jax.random.normal(ks[2], (D, D), jnp.float32) * s, 'Wv': jax.random.normal(ks[3], (D, D), jnp.float32) * s, 'Wo': jax.random.normal(ks[4], (D, D), jnp.float32) * s, 'bo': jnp.zeros((D,), jnp.float32), 'betas': jax.random.normal(ks[5], (1, H, 1, 1), jnp.float32), 'mem': jnp.zeros((H, HD, HD), jnp.float32), 'z': jnp.zeros((H, HD, 1), jnp.float32)}
    _L1_attn_in = _L1_attn_setup()

    def _L1_ffn_setup():
        import jax, jax.numpy as jnp
        import numpy as np
        E = 8
        K = 2
        DIM = 128
        DFF = 256

        def _moe(x, Wg, bg, w1, w2):
            B, S, D = x.shape
            t = x.reshape(-1, D)
            logits = t @ Wg.T + bg
            probs = jax.nn.softmax(logits, axis=-1)
            topw, topi = jax.lax.top_k(probs, K)
            topw = topw / jnp.sum(topw, axis=-1, keepdims=True)
            combine = jnp.sum(jax.nn.one_hot(topi, E, dtype=t.dtype) * topw[..., None], axis=1)

            def body(acc, packed):
                w1e, w2e, ce = packed
                h = t @ w1e.T
                gate, up = jnp.split(h, 2, axis=-1)
                a = jax.nn.silu(gate) * up
                o = a @ w2e.T
                return (acc + ce[:, None] * o, None)
            out, _ = jax.lax.scan(body, jnp.zeros_like(t), (w1, w2, combine.T))
            return out.reshape(B, S, D)
        key = jax.random.key(seed)
        ks = jax.random.split(key, 5)
        B, S = (4, 256)
        x = jax.random.normal(ks[0], (B, S, DIM), dtype=jnp.float32)
        Wg = jax.random.normal(ks[1], (E, DIM), dtype=jnp.float32) * 0.02
        bg = jax.random.normal(ks[2], (E,), dtype=jnp.float32) * 0.02
        w1 = jax.random.normal(ks[3], (E, DFF, DIM), dtype=jnp.float32) * 0.02
        w2 = jax.random.normal(ks[4], (E, DIM, DFF // 2), dtype=jnp.float32) * 0.02
        return {'x': x, 'Wg': Wg, 'bg': bg, 'w1': w1, 'w2': w2}
    _L1_ffn_in = _L1_ffn_setup()
    _L1_c = _w((lambda *s: np.random.randn(*s).astype(np.float32) * 0.05)(16, 128))
    _L1_wmod = _w((lambda *s: np.random.randn(*s).astype(np.float32) * 0.05)(128, 6 * 128) * 128 ** (-0.5))
    _d = {'L0_attn_x': _L0_attn_in['x'], 'L0_attn_Wq': _L0_attn_in['Wq'], 'L0_attn_bq': _L0_attn_in['bq'], 'L0_attn_Wl': _L0_attn_in['Wl'], 'L0_attn_bl': _L0_attn_in['bl'], 'L0_attn_Wk': _L0_attn_in['Wk'], 'L0_attn_bk': _L0_attn_in['bk'], 'L0_attn_Wv': _L0_attn_in['Wv'], 'L0_attn_bv': _L0_attn_in['bv'], 'L0_attn_Wo': _L0_attn_in['Wo'], 'L0_attn_bo': _L0_attn_in['bo'], 'L0_ffn_w1_w': _L0_ffn_in['w1_w'], 'L0_ffn_w1_s': _L0_ffn_in['w1_s'], 'L0_ffn_w2_w': _L0_ffn_in['w2_w'], 'L0_ffn_w2_s': _L0_ffn_in['w2_s'], 'L0_ffn_h1_w': _L0_ffn_in['h1_w'], 'L0_ffn_h1_s': _L0_ffn_in['h1_s'], 'L0_ffn_h2_w': _L0_ffn_in['h2_w'], 'L0_ffn_h2_s': _L0_ffn_in['h2_s'], 'L0_ffn_w3_w': _L0_ffn_in['w3_w'], 'L0_ffn_w3_s': _L0_ffn_in['w3_s'], 'L0_c': _L0_c, 'L0_wmod': _L0_wmod, 'L1_attn_Wq': _L1_attn_in['Wq'], 'L1_attn_Wk': _L1_attn_in['Wk'], 'L1_attn_Wv': _L1_attn_in['Wv'], 'L1_attn_Wo': _L1_attn_in['Wo'], 'L1_attn_bo': _L1_attn_in['bo'], 'L1_attn_betas': _L1_attn_in['betas'], 'L1_attn_mem': _L1_attn_in['mem'], 'L1_attn_z': _L1_attn_in['z'], 'L1_ffn_Wg': _L1_ffn_in['Wg'], 'L1_ffn_bg': _L1_ffn_in['bg'], 'L1_ffn_w1': _L1_ffn_in['w1'], 'L1_ffn_w2': _L1_ffn_in['w2'], 'L1_c': _L1_c, 'L1_wmod': _L1_wmod}
    _x0 = _d['L0_attn_x']
    _d['L0_attn_x'] = jax.random.normal(jax.random.fold_in(jax.random.key(seed), 1), (16, 256, 128), dtype=_x0.dtype)
    del _x0
    return _d

def reference(L0_attn_x, L0_attn_Wq, L0_attn_bq, L0_attn_Wl, L0_attn_bl, L0_attn_Wk, L0_attn_bk, L0_attn_Wv, L0_attn_bv, L0_attn_Wo, L0_attn_bo, L0_ffn_w1_w, L0_ffn_w1_s, L0_ffn_w2_w, L0_ffn_w2_s, L0_ffn_h1_w, L0_ffn_h1_s, L0_ffn_h2_w, L0_ffn_h2_s, L0_ffn_w3_w, L0_ffn_w3_s, L0_c, L0_wmod, L1_attn_Wq, L1_attn_Wk, L1_attn_Wv, L1_attn_Wo, L1_attn_bo, L1_attn_betas, L1_attn_mem, L1_attn_z, L1_ffn_Wg, L1_ffn_bg, L1_ffn_w1, L1_ffn_w2, L1_c, L1_wmod):

    def _L0_attn_ref(x, Wq, bq, Wl, bl, Wk, bk, Wv, bv, Wo, bo):
        import jax, jax.numpy as jnp
        import numpy as np
        DIM = 128
        HEADS = 16
        DIM_HEAD = DIM // HEADS
        LATENT = DIM // 4
        SCALE = DIM_HEAD ** (-0.5)
        B, S, D = x.shape
        H, Dh = (HEADS, DIM_HEAD)
        q = (x @ Wq + bq).reshape(B, S, H, Dh)
        latent = x @ Wl + bl
        k = (latent @ Wk + bk).reshape(B, S, H, Dh)
        v = (latent @ Wv + bv).reshape(B, S, H, Dh)
        scores = jnp.einsum('bihd,bjhd->bhij', q, k) * SCALE
        attn = jax.nn.softmax(scores, axis=-1)
        out = jnp.einsum('bhij,bjhd->bihd', attn, v).reshape(B, S, D)
        out = out @ Wo + bo
        return out

    def _L0_ffn_ref(x, w1_w, w1_s, w2_w, w2_s, h1_w, h1_s, h2_w, h2_s, w3_w, w3_s):
        import jax, jax.numpy as jnp
        import numpy as np
        D_IN, D_HID = (128, 512)

        def _ternary(key, shape):
            return jax.random.randint(key, shape, -1, 2).astype(jnp.float32)

        def _tlin(x, w, s):
            return jnp.einsum('bsi,oi->bso', x, w) * s
        h = jax.nn.silu(_tlin(x, w1_w, w1_s)) * _tlin(x, w2_w, w2_s)
        h = jax.nn.gelu(_tlin(h, h1_w, h1_s), approximate=False)
        h = jax.nn.gelu(_tlin(h, h2_w, h2_s), approximate=False)
        return _tlin(h, w3_w, w3_s)

    def _L1_attn_ref(hidden_states, Wq, Wk, Wv, Wo, bo, betas, mem, z):
        import jax, jax.numpy as jnp
        import numpy as np
        B, S, D, H = (4, 256, 128, 4)
        HD = D // H

        def _reference_tuple_inner(hidden_states, Wq, Wk, Wv, Wo, bo, betas, mem, z):
            b, s, d = hidden_states.shape
            h = betas.shape[1]
            hd = d // h

            def split(x):
                return x.reshape(b, s, h, hd).transpose(0, 2, 1, 3)
            q = split(hidden_states @ Wq.T)
            k = split(hidden_states @ Wk.T)
            v = split(hidden_states @ Wv.T)
            aw = jnp.einsum('bhqd,bhkd->bhqk', q, k)
            causal = jnp.tril(jnp.ones((s, s), bool))
            aw = jnp.where(causal, aw, jnp.finfo(aw.dtype).min)
            p = jax.nn.softmax(aw, axis=-1)
            attn = jnp.einsum('bhqk,bhkd->bhqd', p, v)
            sq = jax.nn.elu(q) + 1.0
            sk = jax.nn.elu(k) + 1.0
            A_mem = jnp.einsum('bhsd,hde->bhse', sq, mem) / (jnp.einsum('bhsd,hdo->bhso', sq, z) + 1e-06)
            g = jax.nn.sigmoid(betas)
            out = g * A_mem + (1.0 - g) * attn
            delta = jnp.einsum('bhsd,hde->bhse', sk, mem) / (jnp.einsum('bhsd,hdo->bhso', sk, z) + 1e-06)
            mem_new = mem + jnp.einsum('bhsd,bhse->hde', sk, v - delta) / b
            z_new = z + jnp.mean(jnp.sum(sk, axis=2), axis=0)[:, :, None]
            out = out.transpose(0, 2, 1, 3).reshape(b, s, d)
            out = out @ Wo.T + bo
            return (out, mem_new, z_new)
        return _reference_tuple_inner(hidden_states, Wq, Wk, Wv, Wo, bo, betas, mem, z)[0]

    def _L1_ffn_ref(x, Wg, bg, w1, w2):
        import jax, jax.numpy as jnp
        import numpy as np
        E = 8
        K = 2
        DIM = 128
        DFF = 256

        def _moe(x, Wg, bg, w1, w2):
            B, S, D = x.shape
            t = x.reshape(-1, D)
            logits = t @ Wg.T + bg
            probs = jax.nn.softmax(logits, axis=-1)
            topw, topi = jax.lax.top_k(probs, K)
            topw = topw / jnp.sum(topw, axis=-1, keepdims=True)
            combine = jnp.sum(jax.nn.one_hot(topi, E, dtype=t.dtype) * topw[..., None], axis=1)

            def body(acc, packed):
                w1e, w2e, ce = packed
                h = t @ w1e.T
                gate, up = jnp.split(h, 2, axis=-1)
                a = jax.nn.silu(gate) * up
                o = a @ w2e.T
                return (acc + ce[:, None] * o, None)
            out, _ = jax.lax.scan(body, jnp.zeros_like(t), (w1, w2, combine.T))
            return out.reshape(B, S, D)
        return _moe(x, Wg, bg, w1, w2)
    x = L0_attn_x
    mod = (_silu(L0_c) @ L0_wmod).reshape(L0_c.shape[0], 6, 1, -1)
    sa, ca, ga, sb, cb, gb = (mod[:, 0], mod[:, 1], mod[:, 2], mod[:, 3], mod[:, 4], mod[:, 5])
    ga = (2 * (ga >= 0) - 1) * jnp.maximum(jnp.abs(ga), 0.25)
    gb = (2 * (gb >= 0) - 1) * jnp.maximum(jnp.abs(gb), 0.25)
    h = _layernorm(x, axis=-1) * (1 + ca) + sa
    x = x + ga * _L0_attn_ref(h, L0_attn_Wq, L0_attn_bq, L0_attn_Wl, L0_attn_bl, L0_attn_Wk, L0_attn_bk, L0_attn_Wv, L0_attn_bv, L0_attn_Wo, L0_attn_bo)
    h = _layernorm(x, axis=-1) * (1 + cb) + sb
    x = x + gb * _L0_ffn_ref(h, L0_ffn_w1_w, L0_ffn_w1_s, L0_ffn_w2_w, L0_ffn_w2_s, L0_ffn_h1_w, L0_ffn_h1_s, L0_ffn_h2_w, L0_ffn_h2_s, L0_ffn_w3_w, L0_ffn_w3_s)
    mod = (_silu(L1_c) @ L1_wmod).reshape(L1_c.shape[0], 6, 1, -1)
    sa, ca, ga, sb, cb, gb = (mod[:, 0], mod[:, 1], mod[:, 2], mod[:, 3], mod[:, 4], mod[:, 5])
    ga = (2 * (ga >= 0) - 1) * jnp.maximum(jnp.abs(ga), 0.25)
    gb = (2 * (gb >= 0) - 1) * jnp.maximum(jnp.abs(gb), 0.25)
    h = _layernorm(x, axis=-1) * (1 + ca) + sa
    x = x + ga * _L1_attn_ref(h, L1_attn_Wq, L1_attn_Wk, L1_attn_Wv, L1_attn_Wo, L1_attn_bo, L1_attn_betas, L1_attn_mem, L1_attn_z)
    h = _layernorm(x, axis=-1) * (1 + cb) + sb
    x = x + gb * _L1_ffn_ref(h, L1_ffn_Wg, L1_ffn_bg, L1_ffn_w1, L1_ffn_w2)
    return x

_drawn_inputs = setup_inputs


def setup_inputs(seed=0):
    import zlib

    import numpy as np

    out = dict(_drawn_inputs(seed))
    spreads = {'L0_attn_bq': (0.0, 0.1),
     'L0_attn_bl': (0.0, 0.1),
     'L0_attn_bk': (0.0, 2.0),
     'L0_attn_bv': (0.0, 0.1),
     'L0_attn_bo': (0.0, 0.1),
     'L1_attn_bo': (0.0, 0.8),
     'L1_attn_mem': (0.0, 0.1),
     'L1_attn_z': (0.0, 0.1)}
    factors = {'L1_attn_Wk': 64.0,
     'L1_attn_Wv': 64.0,
     'L1_ffn_Wg': 8.0,
     'L1_ffn_bg': 31.079,
     'L1_ffn_w1': 8.0,
     'L1_ffn_w2': 8.0}
    for name, (base, spread) in spreads.items():
        noise = np.random.default_rng([zlib.crc32(name.encode()), seed]).standard_normal(out[name].shape)
        drawn = base * np.exp(spread * noise) if base else spread * noise
        out[name] = jnp.asarray(drawn.astype(out[name].dtype))
    for name, factor in factors.items():
        out[name] = (out[name] * factor).astype(out[name].dtype)
    return out
```

```python
from contextlib import ExitStack

import concourse.bass as bass
from concourse import mybir

F32 = mybir.dt.float32
F32R = mybir.dt.float32r
BF16 = mybir.dt.bfloat16
ALU = mybir.AluOpType
ACT = mybir.ActivationFunctionType
AX = mybir.AxisListType

P = 128
B = 16
S = 256
D = 128
NT = S // P
EPS = 1e-5
SA, CA, GA, SB, CB, GB = range(6)

H0 = 16
DH0 = D // H0
LAT = D // 4
SCALE0 = DH0 ** -0.5
PAIRS = H0 // 2
HROWS = P // 2
TERMS = [(0, 0), (0, 1), (0, 2), (1, 0), (1, 1), (2, 0)]
TROWS = 2 * DH0
NB = 4
MAXROW = len(TERMS) * TROWS
PES = {"ln": 0, "max_turn": 1, "qk": 3, "O0": 5, "v": 8, "O1": 9, "back": 11, "out": 12, "turn_y": 14,
       "pv_s": (11, 15), "pv_t": (3, 7)}
DVE = {"negmax": 0, "stats": 2, "parts": 6, "O0": 6, "parts2": 10, "normalise": 11, "O1": 10, "add": 15}
ACTS = {"hT": 0, "maxT": 0, "qk": 3, "part1": 7, "v": 7, "OTn": 11, "y": 12, "OT_s": (11, 15), "OT_t": (3, 6)}


X_LOADS = 4
X_LOADED = 16 * X_LOADS


class Names:
    pass


def batch_valid(b):
    return not isinstance(b, int) or 0 <= b < B


def at_least(eng, sem, value):
    if isinstance(value, int) and value <= 0:
        return
    eng.wait_ge(sem, value)


def wait_apart(eng, k, sem, value):
    eng.wait_ge(sem, value)
    eng.sem_inc(k.waits_passed, 1)


def tensors(nc, ctx, tag):
    def sb(name, shape, dt=F32):
        return ctx.enter_context(nc.sbuf_tensor(f"{tag}_{name}", shape, dt))

    def ps(name, shape, dt=F32):
        return ctx.enter_context(nc.psum_tensor(f"{tag}_{name}", shape, dt))

    mine = []

    def clear():
        if mine:
            nc.clear_and_free_semaphores(mine)
            nc.all_engine_barrier()

    ctx.callback(clear)

    def sem(name):
        mine.append(nc.alloc_semaphore(f"{tag}_s_{name}"))
        return mine[-1]

    return sb, ps, sem


def prepare(nc, k, a):
    with ExitStack() as ctx:
        sb, ps, sem = tensors(nc, ctx, "prep")
        c_nat = sb("c_nat", [B, 2, D])
        wmod = sb("wmod", [P, 2, 6 * D])
        wl = sb("wl", [P, LAT])
        wk = sb("wk", [LAT, D])
        wv = sb("wv", [LAT, D])
        wq = sb("wq", [P, D])
        lat_bias = sb("lat_bias", [LAT, 1])
        cols = sb("cols", [P, 4])
        tanh_c = sb("tanh_c", [P, 2 * B])
        half_c = sb("half_c", [P, 2 * B])
        silu_c = sb("silu_c", [P, 2 * B])
        wlT = sb("wlT", [LAT, P])
        wk_perm = sb("wk_perm", [LAT, D])
        bv_col = sb("bv_col", [P, 1])
        gate_sign = sb("gate_sign", [P, 2, 2, B])
        gate_abs = sb("gate_abs", [P, 2, 2, B])

        p_c = ps("p_c", [P, 512])
        p_mod = ps("p_mod", [P, 512])
        p_w = ps("p_w", [P, 512])
        p_v = ps("p_v", [P, 512])
        p_b = ps("p_b", [P, 512])

        zeroed = sem("zeroed")
        ident_ready = sem("ident_ready")
        small_loaded = sem("small_loaded")
        wmod_loaded = sem("wmod_loaded")
        c_turned = sem("c_turned")
        c_tanh = sem("c_tanh")
        c_half = sem("c_half")
        c_silu = sem("c_silu")
        wl_turned = sem("wl_turned")
        wlT_ready = sem("wlT_ready")
        perm_ready = sem("perm_ready")
        w_made = sem("w_made")
        mod_made = sem("mod_made")
        modT_ready = sem("modT_ready")
        bias_made = sem("bias_made")
        bv_ready = sem("bv_ready")
        bo_made = sem("bo_made")
        gate_step = sem("gate_step")

        x_view = a["L0_attn_x"].rearrange("b (i p) d -> p (b i) d", p=P)
        small = 0

        block = ctx.enter_context(nc.Block())

        @block.sync
        def _(sp):
            loads = [
                (c_nat[:, 0, :], a["L0_c"]), (c_nat[:, 1, :], a["L1_c"]),
                (wl[:], a["L0_attn_Wl"]), (wk[:], a["L0_attn_Wk"]), (wv[:], a["L0_attn_Wv"]),
                (wq[:], a["L0_attn_Wq"]), (k.wo0[:], a["L0_attn_Wo"]),
                (lat_bias[:], a["L0_attn_bl"].rearrange("(l o) -> l o", o=1)),
            ]
            for to, of in loads:
                sp.dma_start(to, of).then_inc(small_loaded, 16)
            for half in range(2):
                rows = slice(half * HROWS, (half + 1) * HROWS)
                for n, name in enumerate(("L0_attn_bq", "L0_attn_bk")):
                    sp.dma_start(cols[rows, n:n + 1],
                                 a[name].rearrange("(g w d o) -> w d g o", w=2, d=DH0, o=1)[half],
                                 allow_slow_non_contiguous=True).then_inc(small_loaded, 16)
            for n, name in ((2, "L0_attn_bv"), (3, "L0_attn_bo")):
                sp.dma_start(cols[:, n:n + 1], a[name].rearrange("(d o) -> d o", o=1)).then_inc(small_loaded, 16)
            for n, name in enumerate(("L0_wmod", "L1_wmod")):
                sp.dma_start(wmod[:, n, :], a[name]).then_inc(wmod_loaded, 16)
            per = B * NT // X_LOADS
            for n in range(X_LOADS):
                part = slice(n * per, (n + 1) * per)
                sp.dma_start(k.X[:, part, :], x_view[:, part, :]).then_inc(k.x_loaded, 16)
            sp.wait_ge(k.x_loaded, X_LOADED)

        SMALL = 16 * 14

        @block.gpsimd
        def _(pool):
            pool.memset(k.ident[:], 0.0).then_inc(zeroed, 1)
            pool.wait_ge(zeroed, 1)
            pool.affine_select(out=k.ident[:], in_=k.ident[:], compare_op=ALU.not_equal, fill=1.0, base=0,
                               pattern=[[-1, P]], channel_multiplier=1).then_inc(ident_ready, 1)
            pool.wait_ge(ident_ready, 1)
            pool.tensor_copy(k.ident16[:], k.ident[:]).then_inc(ident_ready, 1)
            pool.memset(k.minus_half[:], -0.5)
            for r in range(NB):
                pool.memset(k.V[r][:, :, :, DH0 + 1:], 0.0)
                if r >= 2:
                    pool.memset(k.Q[r][:], 0.0)
                    pool.memset(k.K[r][:], 1.0)

        @block.tensor
        def _(pe):
            pe.wait_ge(ident_ready, 1)
            pe.wait_ge(small_loaded, SMALL)
            for n in range(2):
                mm = pe.transpose(p_c[:, n * B:(n + 1) * B], c_nat[:, n, :], k.ident[0:B, 0:B])
            mm.then_inc(c_turned, 1)
            pe.transpose(p_w[0:LAT, 0:P], wl[:], k.ident[:]).then_inc(wl_turned, 1)
            pe.wait_ge(wlT_ready, 1)
            pe.wait_ge(perm_ready, 2)
            pe.matmul(p_v[:, 0:D], wlT[:], wk_perm[:], start=True, stop=True)
            pe.matmul(p_v[:, D:2 * D], wlT[:], wv[:], start=True, stop=True).then_inc(w_made, 1)
            pe.matmul(p_b[:, 0:1], wk_perm[:], lat_bias[:], start=True, stop=True)
            pe.matmul(p_b[:, 1:2], wv[:], lat_bias[:], start=True, stop=True).then_inc(bias_made, 1)
            pe.wait_ge(c_silu, 1)
            pe.wait_ge(wmod_loaded, 32)
            for n in range(2):
                for j in range(6):
                    at = (n * 6 + j) * B
                    mm = pe.matmul(p_mod[:, at:at + B], wmod[:, n, j * D:(j + 1) * D],
                                   silu_c[:, n * B:(n + 1) * B], start=True, stop=True)
            mm.then_inc(mod_made, 1)
            pe.wait_ge(bv_ready, 1)
            pe.matmul(p_c[:, 0:1], k.wo0[:], bv_col[:], start=True, stop=True).then_inc(bo_made, 1)

        @block.scalar
        def _(act):
            act.wait_ge(c_turned, 1)
            act.activation(tanh_c[:], p_c[:, 0:2 * B], ACT.Tanh, scale=0.5).then_inc(c_tanh, 1)

        @block.vector
        def _(dve):
            for r in range(NB):
                dve.memset(k.V[r][:, :, :, DH0:DH0 + 1], 1.0)
                if r < 2:
                    dve.memset(k.Q[r][:], 0.0)
                    dve.memset(k.K[r][:], 1.0)
            dve.wait_ge(small_loaded, SMALL)
            dve.wait_ge(ident_ready, 1)
            dve.tensor_reduce(k.parity[:], k.ident[:].rearrange("p (t w d) -> p w t d", w=2, d=DH0), AX.XY, ALU.add)
            for to, of in ((k.wq0[:], wq[:]), (wk_perm[:], wk[:])):
                dve.tensor_copy(to.rearrange("p (w d g) -> p w d g", w=2, d=DH0),
                                of.rearrange("p (g w d) -> p w d g", w=2, d=DH0)).then_inc(perm_ready, 1)
            dve.wait_ge(wl_turned, 1)
            dve.tensor_copy(wlT[:], p_w[0:LAT, 0:P]).then_inc(wlT_ready, 1)
            dve.wait_ge(c_tanh, 1)
            dve.tensor_scalar(half_c[:], p_c[:, 0:2 * B], 0.5, None, ALU.mult).then_inc(c_half, 1)
            dve.wait_ge(c_half, 1)
            dve.scalar_tensor_tensor(out=silu_c[:], in0=tanh_c[:], scalar=1.0, in1=half_c[:],
                                     op0=ALU.add, op1=ALU.mult).then_inc(c_silu, 1)
            dve.wait_ge(w_made, 1)
            dve.tensor_copy(k.wk0[:], p_v[:, 0:D])
            dve.tensor_copy(k.wv0[:], p_v[:, D:2 * D])
            dve.wait_ge(bias_made, 1)
            dve.tensor_scalar(k.bq0[:], cols[:, 0:1], SCALE0, None, ALU.mult)
            dve.tensor_tensor(k.bk0[:], p_b[:, 0:1], cols[:, 1:2], ALU.add)
            dve.tensor_tensor(bv_col[:], p_b[:, 1:2], cols[:, 2:3], ALU.add).then_inc(bv_ready, 1)
            dve.wait_ge(bo_made, 1)
            dve.tensor_tensor(k.bo0[:], p_c[:, 0:1], cols[:, 3:4], ALU.add).then_inc(gate_step, 1)
            dve.wait_ge(mod_made, 1)
            dve.tensor_copy(k.mod[:], p_mod[:, 0:2 * 6 * B].rearrange("p (n j b) -> p n j b", n=2, j=6)).then_inc(gate_step, 1)
            dve.wait_ge(gate_step, 2)
            one_plus = k.mod[:, :, CA::CB - CA, :]
            dve.tensor_scalar(one_plus, one_plus, 1.0, None, ALU.add)
            g = k.mod[:, :, GA::GB - GA, :]
            dve.tensor_scalar(gate_sign[:], g, 0.0, 2.0, ALU.is_ge, ALU.mult)
            dve.scalar_tensor_tensor(out=gate_abs[:], in0=g, scalar=-1.0, in1=g, op0=ALU.mult, op1=ALU.max
                                     ).then_inc(gate_step, 1)
            dve.wait_ge(gate_step, 3)
            dve.tensor_scalar(gate_abs[:], gate_abs[:], 0.25, None, ALU.max).then_inc(gate_step, 1)
            dve.wait_ge(gate_step, 4)
            dve.scalar_tensor_tensor(out=g, in0=gate_sign[:], scalar=-1.0, in1=gate_abs[:],
                                     op0=ALU.add, op1=ALU.mult).then_inc(gate_step, 1)
            dve.wait_ge(gate_step, 5)
            dve.tensor_scalar(k.gbo0[:], k.mod[:, 0, GA, :], k.bo0[:, 0:1], None, ALU.mult)


def attention0(nc, k):
    with ExitStack() as ctx:
        sb, ps, sem = tensors(nc, ctx, "att0")
        Q, K, V = k.Q, k.K, k.V
        stats = sb("stats", [P, NT, 6])
        meanvar = sb("meanvar", [P, NT, 2])
        var_eps = sb("var_eps", [P, NT])
        rstd = sb("rstd", [P, NT])
        xn = sb("xn", [P, NT, D])
        hT = sb("hT", [P, S])
        qk = sb("qk", [P, 2, S])
        rest = sb("rest", [P, 2, S])
        parts = sb("parts", [P, 3, 2, S], BF16)
        Qall = sb("Qall", [P, PAIRS, S], BF16)
        rowmax = sb("rowmax", [P, NT, PAIRS, 2])
        negmax = sb("negmax", [P, NT, 2, PAIRS])
        negrest = sb("negrest", [P, NT, 2, PAIRS])
        negparts = sb("negparts", [P, NT, 2, 3, PAIRS], BF16)
        maxT = sb("maxT", [2 * 3 * PAIRS, S], BF16)
        probs = [sb(f"probs{n}", [P, 2, 2, NT, S]) for n in range(2)]
        OT = [sb(f"OT{n}", [P, S]) for n in range(4)]
        recip = sb("recip", [P, 2, NT, 4])
        O = sb("O", [P, NT, H0, DH0])
        OTn = sb("OTn", [P, S])
        yT = sb("yT", [P, S])

        p_max = [ps(f"p_max{n}", [P, 2, S]) for n in range(2)]
        p_sT = [ps(f"p_sT{n}", [P, 2, NT, S]) for n in range(2)]
        p_o = ps("p_o", [P, 512])
        p_m = ps("p_m", [P, 512])
        p_m16 = p_m[:].bitcast(BF16)

        stats_step = sem("stats_step")
        var_ready = sem("var_ready")
        rstd_ready = sem("rstd_ready")
        xn_ready = sem("xn_ready")
        xn_turned = sem("xn_turned")
        hT_ready = sem("hT_ready")
        qk_made = sem("qk_made")
        qk_ready = sem("qk_ready")
        part0_ready = sem("part0_ready")
        rest_ready = sem("rest_ready")
        part1_ready = sem("part1_ready")
        part2_ready = sem("part2_ready")
        v_made = sem("v_made")
        v_ready = sem("v_ready")
        stacked = sem("stacked")
        Q_ready = sem("Q_ready")
        scored = sem("scored")
        maxed = sem("maxed")
        negmax_ready = sem("negmax_ready")
        neg_step = sem("neg_step")
        neg_ready = sem("neg_ready")
        max_turned = sem("max_turned")
        maxT_ready = sem("maxT_ready")
        max_stacked = sem("max_stacked")
        scoredT = sem("scoredT")
        exped = sem("exped")
        pv_made = sem("pv_made")
        OT_ready = sem("OT_ready")
        O_turned = sem("O_turned")
        recip_ready = sem("recip_ready")
        O_ready = sem("O_ready")
        OTn_turned = sem("OTn_turned")
        OTn_ready = sem("OTn_ready")
        y_made = sem("y_made")
        yT_ready = sem("yT_ready")
        y_turned = sem("y_turned")
        x_added = sem("x_added")

        TILES = 2 * PAIRS
        STACK_DMAS = 2 * len(TERMS)

        def pe_ln(pe, b):
            pe.wait_ge(xn_ready, b + 1)
            at_least(pe, v_ready, b)
            at_least(pe, x_added, b - 4)
            for i in range(NT):
                mm = pe.transpose(p_m[:, i * P:(i + 1) * P], xn[:, i, :], k.ident[:])
            mm.then_inc(xn_turned, 1)

        def pe_qk(pe, b):
            pe.wait_ge(hT_ready, b + 1)
            at_least(pe, maxT_ready, b - 2)
            pe.matmul(p_m[:, 0:S], k.wq0[:], hT[:], start=True, stop=True)
            pe.matmul(p_m[:, S:2 * S], k.wk0[:], hT[:], start=True, stop=True).then_inc(qk_made, 1)

        def pe_v(pe, b):
            pe.wait_ge(qk_ready, b + 1)
            at_least(pe, O_ready, 2 * (b - 4) + 1)
            for i in range(NT):
                mm = pe.matmul(p_m[:, i * D:(i + 1) * D], hT[:, i * P:(i + 1) * P], k.wv0[:], start=True, stop=True)
            mm.then_inc(v_made, 1)

        def pe_max_tile(pe, b, r, t):
            if t == 0:
                pe.wait_ge(stacked, 16 * STACK_DMAS * (b + 1))
                pe.wait_ge(Q_ready, b + 1)
            at_least(pe, maxed, TILES * b + t - 1)
            pair, i = t // NT, t % NT
            for w in range(2):
                mm = pe.matmul(p_max[t % 2][:, w, :], Q[r][0:MAXROW, 2 * pair + w, i * P:(i + 1) * P],
                               K[r][0:MAXROW, pair, :],
                               start=True, stop=True)
            mm.then_inc(scored, 1)

        def pe_max_turn(pe, b):
            pe.wait_ge(neg_ready, b + 1)
            if not isinstance(b, int) or b + 3 < B:
                wait_apart(pe, k, hT_ready, b + 4)
            else:
                at_least(pe, x_added, b - 1)
            for i in range(NT):
                mm = pe.transpose(p_m16[0:6 * PAIRS, i * P:(i + 1) * P],
                                  negparts[:, i].rearrange("p w t g -> p (w t g)"), k.ident16[:])
            mm.then_inc(max_turned, 1)

        def pe_scoreT(pe, b, r, t):
            if t == 0:
                pe.wait_ge(max_stacked, 32 * (b + 1))
            at_least(pe, exped, PAIRS * b + t - 1)
            for w in range(2):
                for j in range(NT):
                    mm = pe.matmul(p_sT[t % 2][:, w, j, :], K[r][:, t, j * P:(j + 1) * P], Q[r][:, 2 * t + w, :],
                                   start=True, stop=True)
            mm.then_inc(scoredT, 1)

        def pe_pv(pe, b, r, g):
            if g == 0:
                pe.wait_ge(v_ready, b + 1)
            pe.wait_ge(exped, PAIRS * b + 2 * g + 2)
            at_least(pe, OT_ready, 4 * b + g)
            for j in range(NT):
                for h in range(4):
                    mm = pe.matmul(p_o[32 * h:32 * h + 32, 0:S], V[r][:, j, 4 * g + h, :],
                                   probs[g % 2][:, h // 2, h % 2, j, :], start=(j == 0), stop=(j == NT - 1))
            mm.then_inc(pv_made, 1)

        def pe_turn_O(pe, b, u, p_m_free):
            p_m_free()
            pe.wait_ge(OT_ready, 4 * b + 2 * u + 2)
            for g in range(2):
                for i in range(NT):
                    at = (g * NT + i) * P
                    mm = pe.transpose(p_m[:, at:at + P], OT[2 * u + g][:, i * P:(i + 1) * P], k.ident[:])
            mm.then_inc(O_turned, 1)

        def pe_turn_back(pe, b):
            pe.wait_ge(O_ready, 2 * b + 2)
            for i in range(NT):
                mm = pe.transpose(p_m[:, i * P:(i + 1) * P], O[:, i].rearrange("p h d -> p (h d)"), k.ident[:])
            mm.then_inc(OTn_turned, 1)

        def pe_out(pe, b):
            pe.wait_ge(OTn_ready, b + 1)
            pe.matmul(p_m[:, 0:S], k.wo0[:], OTn[:], start=True, stop=True).then_inc(y_made, 1)

        def pe_turn_y(pe, b):
            pe.wait_ge(yT_ready, b + 1)
            for i in range(NT):
                mm = pe.transpose(p_m[:, i * P:(i + 1) * P], yT[:, i * P:(i + 1) * P], k.ident[:])
            mm.then_inc(y_turned, 1)

        def pe_step(pe, n, r):
            f, m, s, t = n, n - 2, n - 3, n - 4
            rm, rs, rt = (r - 2) % NB, (r - 3) % NB, r
            for slot in range(TILES):
                if slot == PES["ln"] and batch_valid(f):
                    pe_ln(pe, f)
                if slot == PES["max_turn"] and batch_valid(s):
                    pe_max_turn(pe, s)
                if slot == PES["qk"] and batch_valid(f):
                    pe_qk(pe, f)
                if slot == PES["v"] and batch_valid(f):
                    pe_v(pe, f)
                if batch_valid(m):
                    pe_max_tile(pe, m, rm, slot)
                if slot >= 6 and slot % 2 == 0 and batch_valid(s):
                    pe_scoreT(pe, s, rs, (slot - 6) // 2)
                if slot in (0, 2, 4) and batch_valid(t):
                    pe_scoreT(pe, t, rt, 5 + slot // 2)
                if slot in PES["pv_s"] and batch_valid(s):
                    pe_pv(pe, s, rs, PES["pv_s"].index(slot))
                if slot in PES["pv_t"] and batch_valid(t):
                    pe_pv(pe, t, rt, 2 + PES["pv_t"].index(slot))
                if slot == PES["O0"] and batch_valid(t):
                    def after_qk():
                        if batch_valid(f):
                            pe.wait_ge(qk_ready, f + 1)
                        elif batch_valid(s):
                            pe.wait_ge(maxT_ready, s + 1)
                        at_least(pe, x_added, t)
                    pe_turn_O(pe, t, 0, after_qk)
                if slot == PES["O1"] and batch_valid(t):
                    def after_v():
                        if batch_valid(f):
                            pe.wait_ge(v_ready, f + 1)
                        pe.wait_ge(O_ready, 2 * t + 1)
                    pe_turn_O(pe, t, 1, after_v)
                if slot == PES["back"] and batch_valid(t):
                    pe_turn_back(pe, t)
                if slot == PES["out"] and batch_valid(t):
                    pe_out(pe, t)
                if slot == PES["turn_y"] and batch_valid(t):
                    pe_turn_y(pe, t)

        def dve_stats(dve, b):
            at_least(dve, xn_ready, b)
            for i in range(NT):
                dve.bn_stats(stats[:, i, :], k.X[:, bass.ds(b * NT + i, 1), :]).then_inc(stats_step, 1)
            wait_apart(dve, k, stats_step, 3 * b + 2)
            for i in range(NT):
                ins = dve.bn_aggr(meanvar[:, i, :], stats[:, i, :])
            ins.then_inc(stats_step, 1)
            dve.wait_ge(stats_step, 3 * b + 3)
            at_least(dve, rstd_ready, b)
            dve.tensor_scalar(var_eps[:], meanvar[:, :, 1], EPS, None, ALU.add).then_inc(var_ready, 1)

        def dve_normalise(dve, b):
            dve.wait_ge(rstd_ready, b + 1)
            at_least(dve, xn_turned, b)
            for i in range(NT):
                ins = dve.tensor_scalar(xn[:, i, :], k.X[:, bass.ds(b * NT + i, 1), :].rearrange("p o d -> p (o d)"),
                                        meanvar[:, i, 0:1], rstd[:, i:i + 1], ALU.subtract, ALU.mult)
            ins.then_inc(xn_ready, 1)

        def dve_parts(dve, b):
            dve.wait_ge(part0_ready, b + 1)
            dve.tensor_tensor(rest[:], qk[:], parts[:, 0], ALU.subtract).then_inc(rest_ready, 1)

        def dve_parts2(dve, b):
            dve.wait_ge(part1_ready, b + 1)
            dve.tensor_tensor(parts[:, 2], rest[:], parts[:, 1], ALU.subtract).then_inc(part2_ready, 1)

        def dve_max_tile(dve, b, t):
            pair, i = t // NT, t % NT
            if t == 0:
                at_least(dve, negmax_ready, b)
            dve.wait_ge(scored, TILES * b + t + 1)
            dve.tensor_reduce(rowmax[:, i, pair, :], p_max[t % 2][:], AX.X, ALU.max).then_inc(maxed, 1)

        def dve_negmax(dve, b):
            dve.wait_ge(maxed, TILES * (b + 1))
            dve.tensor_scalar(negmax[:].rearrange("p i w g -> p i g w"), rowmax[:], -1.0, None, ALU.mult
                              ).then_inc(negmax_ready, 1)
            dve.wait_ge(negmax_ready, b + 1)
            at_least(dve, max_turned, b)
            dve.tensor_copy(negparts[:, :, :, 0, :], negmax[:]).then_inc(neg_step, 1)
            dve.wait_ge(neg_step, 3 * b + 1)
            dve.tensor_tensor(negrest[:], negmax[:], negparts[:, :, :, 0, :], ALU.subtract).then_inc(neg_step, 1)
            dve.wait_ge(neg_step, 3 * b + 2)
            dve.tensor_copy(negparts[:, :, :, 1, :], negrest[:]).then_inc(neg_step, 1)
            dve.wait_ge(neg_step, 3 * b + 3)
            dve.tensor_tensor(negparts[:, :, :, 2, :], negrest[:], negparts[:, :, :, 1, :], ALU.subtract
                              ).then_inc(neg_ready, 1)

        def dve_normalise_O(dve, b, u):
            dve.wait_ge(O_turned, 2 * b + u + 1)
            if u == 0:
                at_least(dve, OTn_turned, b)
            heads = p_m[:].rearrange("p (g i h c) -> p g i h c", g=2, i=NT, h=4)
            at_least(dve, O_ready, 2 * b + u)
            dve.reciprocal(recip[:].rearrange("p g i h -> p (g i h)"),
                           p_m[:].rearrange("p (n c) -> p n c", c=32)[:, :, DH0]).then_inc(recip_ready, 1)
            dve.wait_ge(recip_ready, 2 * b + u + 1)
            for i in range(NT):
                ins = dve.tensor_tensor(O[:, i, 8 * u:8 * u + 8, :].rearrange("p (g h) d -> p g h d", g=2),
                                        heads[:, :, i, :, 0:DH0],
                                        recip[:, :, i, :].unsqueeze(3).to_broadcast([P, 2, 4, DH0]), ALU.mult)
            ins.then_inc(O_ready, 1)

        def dve_add(dve, b):
            dve.wait_ge(y_turned, b + 1)
            x = k.X[:, bass.ds(b * NT, NT), :]
            dve.tensor_tensor(x, x, p_m[:, 0:S].rearrange("p (i d) -> p i d", i=NT), ALU.add).then_inc(x_added, 1)

        def dve_step(dve, n):
            f, m, s, t = n, n - 2, n - 3, n - 4
            for slot in range(TILES):
                if slot == DVE["negmax"] and batch_valid(s):
                    dve_negmax(dve, s)
                if slot == DVE["O0"] and batch_valid(t):
                    dve_normalise_O(dve, t, 0)
                if slot == DVE["O1"] and batch_valid(t):
                    dve_normalise_O(dve, t, 1)
                if slot == DVE["parts"] and batch_valid(f):
                    dve_parts(dve, f)
                if slot == DVE["parts2"] and batch_valid(f):
                    dve_parts2(dve, f)
                if batch_valid(m):
                    dve_max_tile(dve, m, slot)
                if slot == DVE["stats"] and batch_valid(f + 1):
                    dve_stats(dve, f + 1)
                if slot == DVE["normalise"] and batch_valid(f + 1):
                    dve_normalise(dve, f + 1)
                if slot == DVE["add"] and batch_valid(t):
                    dve_add(dve, t)

        def act_hT(act, b):
            act.wait_ge(xn_turned, b + 1)
            at_least(act, v_made, b)
            act.activation(hT[:], p_m[:, 0:S], ACT.Identity, bias=k.mod[:, 0, SA, bass.ds(b, 1)],
                           scale=k.mod[:, 0, CA, bass.ds(b, 1)]).then_inc(hT_ready, 1)

        def act_qk(act, b):
            act.wait_ge(qk_made, b + 1)
            at_least(act, rest_ready, b)
            act.activation(qk[:, 0, :], p_m[:, 0:S], ACT.Identity, bias=k.bq0[:, 0:1], scale=SCALE0)
            act.activation(qk[:, 1, :], p_m[:, S:2 * S], ACT.Identity, bias=k.bk0[:, 0:1]).then_inc(qk_ready, 1)
            act.wait_ge(qk_ready, b + 1)
            at_least(act, stacked, 16 * STACK_DMAS * b)
            act.activation(parts[:, 0], qk[:], ACT.Copy).then_inc(part0_ready, 1)

        def act_part1(act, b):
            act.wait_ge(rest_ready, b + 1)
            act.activation(parts[:, 1], rest[:], ACT.Copy).then_inc(part1_ready, 1)

        def act_v(act, b, r):
            act.wait_ge(v_made, b + 1)
            at_least(act, pv_made, 4 * (b - NB) + 4)
            act.activation(V[r][:, :, :, 0:DH0], p_m[:, 0:NT * D].rearrange("p (i h d) -> p i h d", i=NT, h=H0),
                           ACT.Copy).then_inc(v_ready, 1)

        def act_maxT(act, b):
            act.wait_ge(max_turned, b + 1)
            at_least(act, max_stacked, 32 * b)
            act.activation(maxT[:], p_m16[0:6 * PAIRS, 0:S], ACT.Copy).then_inc(maxT_ready, 1)

        def act_exp(act, b, t):
            g = t // 2
            act.wait_ge(scoredT, PAIRS * b + t + 1)
            if t % 2 == 0:
                at_least(act, pv_made, 4 * b + g - 1)
            act.activation(probs[g % 2][:, t % 2], p_sT[t % 2][:], ACT.Exp).then_inc(exped, 1)

        def act_OT(act, b, g):
            act.wait_ge(pv_made, 4 * b + g + 1)
            at_least(act, O_turned, 2 * (b - 1) + g // 2 + 1)
            act.activation(OT[g][:], p_o[:, 0:S], ACT.Copy).then_inc(OT_ready, 1)

        def act_OTn(act, b):
            act.wait_ge(OTn_turned, b + 1)
            at_least(act, y_made, b)
            act.activation(OTn[:], p_m[:, 0:S], ACT.Copy).then_inc(OTn_ready, 1)

        def act_y(act, b):
            act.wait_ge(y_made, b + 1)
            at_least(act, y_turned, b)
            act.activation(yT[:], p_m[:, 0:S], ACT.Identity, bias=k.gbo0[:, bass.ds(b, 1)],
                           scale=k.mod[:, 0, GA, bass.ds(b, 1)]).then_inc(yT_ready, 1)

        def act_step(act, n, r):
            f, m, s, t = n, n - 2, n - 3, n - 4
            for slot in range(TILES):
                if slot == ACTS["hT"] and batch_valid(f):
                    act_hT(act, f)
                if slot == ACTS["maxT"] and batch_valid(s):
                    act_maxT(act, s)
                if slot == ACTS["qk"] and batch_valid(f):
                    act_qk(act, f)
                if slot == ACTS["part1"] and batch_valid(f):
                    act_part1(act, f)
                if slot == ACTS["v"] and batch_valid(f):
                    act_v(act, f, r)
                if slot == ACTS["OTn"] and batch_valid(t):
                    act_OTn(act, t)
                if slot == ACTS["y"] and batch_valid(t):
                    act_y(act, t)
                if slot >= 6 and slot % 2 == 0 and batch_valid(s):
                    act_exp(act, s, (slot - 6) // 2)
                if slot in (0, 2, 4) and batch_valid(t):
                    act_exp(act, t, 5 + slot // 2)
                if slot in ACTS["OT_s"] and batch_valid(s):
                    act_OT(act, s, ACTS["OT_s"].index(slot))
                if slot in ACTS["OT_t"] and batch_valid(t):
                    act_OT(act, t, 2 + ACTS["OT_t"].index(slot))

        def sp_max(sp, b, r):
            wait_apart(sp, k, maxT_ready, b + 1)
            wait_apart(sp, k, scored, TILES * (b + 1))
            for w in range(2):
                sp.dma_start(Q[r][MAXROW:MAXROW + 3, w::2, :], maxT[w * 3 * PAIRS:(w + 1) * 3 * PAIRS, :]
                             ).then_inc(max_stacked, 16)

        def sp_stack(sp, b, r):
            if not isinstance(b, int) or b >= NB:
                wait_apart(sp, k, scoredT, PAIRS * (b - NB + 1))
            at_least(sp, stacked, 16 * STACK_DMAS * b)
            if not isinstance(b, int) or b >= 1:
                wait_apart(sp, k, Q_ready, b)
            for part, ready in enumerate((part0_ready, part1_ready, part2_ready)):
                sp.wait_ge(ready, b + 1)
                for n, (q_part, k_part) in enumerate(TERMS):
                    rows = slice(n * TROWS, (n + 1) * TROWS)
                    if q_part == part:
                        sp.dma_start(Qall[rows, :, :], parts[:, part, 0, :]).then_inc(stacked, 16)
                    if k_part == part:
                        sp.dma_start(K[r][rows, :, :], parts[:, part, 1, :]).then_inc(stacked, 16)

        def sp_step(sp, n, r):
            if batch_valid(n - 3):
                sp_max(sp, n - 3, (r - 3) % NB)
            if batch_valid(n):
                sp_stack(sp, n, r)

        def pool_rstd(pool, b):
            pool.wait_ge(var_ready, b + 1)
            at_least(pool, xn_ready, b)
            pool.tensor_tensor(rstd[:], var_eps[:], k.minus_half[:, 0:NT], ALU.pow).then_inc(rstd_ready, 1)

        def pool_Q(pool, b, r):
            pool.wait_ge(stacked, 16 * STACK_DMAS * (b + 1))
            if not isinstance(b, int) or b >= NB:
                wait_apart(pool, k, scoredT, PAIRS * (b - NB + 1))
            for w in range(2):
                ins = pool.tensor_scalar(Q[r][0:MAXROW, w::2, :], Qall[0:MAXROW], k.parity[0:MAXROW, w:w + 1], 0.0,
                                         ALU.mult, ALU.add)
            ins.then_inc(Q_ready, 1)

        def pool_step(pool, n, r):
            if batch_valid(n + 1):
                pool_rstd(pool, n + 1)
            pool_Q(pool, n, r)

        LOOPS = (B - 1 - 4) // NB
        WHOLE = range(4, 4 + NB * LOOPS)
        LAST = B + 4

        block = ctx.enter_context(nc.Block())

        @block.sync
        def _(sp):
            for n in range(WHOLE.start):
                sp_step(sp, n, n % NB)
            with sp.Fori(0, LOOPS) as turn:
                for r in range(NB):
                    sp_step(sp, turn * NB + (WHOLE.start + r), r)
            for n in range(WHOLE.stop, LAST):
                sp_step(sp, n, n % NB)

        @block.gpsimd
        def _(pool):
            pool_rstd(pool, 0)
            for n in range(WHOLE.start):
                pool_step(pool, n, n % NB)
            with pool.Fori(0, LOOPS) as turn:
                for r in range(NB):
                    pool_step(pool, turn * NB + (WHOLE.start + r), r)
            for n in range(WHOLE.stop, B):
                pool_step(pool, n, n % NB)

        @block.tensor
        def _(pe):
            for n in range(WHOLE.start):
                pe_step(pe, n, n % NB)
            with pe.Fori(0, LOOPS) as turn:
                for r in range(NB):
                    pe_step(pe, turn * NB + (WHOLE.start + r), r)
            for n in range(WHOLE.stop, LAST):
                pe_step(pe, n, n % NB)

        @block.scalar
        def _(act):
            for n in range(WHOLE.start):
                act_step(act, n, n % NB)
            with act.Fori(0, LOOPS) as turn:
                for r in range(NB):
                    act_step(act, turn * NB + (WHOLE.start + r), r)
            for n in range(WHOLE.stop, LAST):
                act_step(act, n, n % NB)

        @block.vector
        def _(dve):
            dve_stats(dve, 0)
            dve_normalise(dve, 0)
            for n in range(WHOLE.start):
                dve_step(dve, n)
            with dve.Fori(0, LOOPS) as turn:
                for r in range(NB):
                    dve_step(dve, turn * NB + (WHOLE.start + r))
            for n in range(WHOLE.stop, LAST):
                dve_step(dve, n)


F = 512
FB = F // P


def ffn_weights(nc, k, a, sb):
    for name, blocks, width in (("w1", 1, F), ("w2", 1, F), ("h1", FB, F), ("h2", FB, F), ("w3", FB, D)):
        for part in ("hi", "lo"):
            k.w[f"{name}_{part}"] = sb(f"{name}_{part}", [P, blocks, width], F32R)
    k.rows_inexact = sb("rows_inexact", [1, 1], mybir.dt.int32)
    with ExitStack() as ctx:
        sbt, ps, sem = tensors(nc, ctx, "ffn0w")
        lo_abs = sbt("lo_abs", [P, F])
        lo_sums = sbt("lo_sums", [P, 11])
        lo_sum = sbt("lo_sum", [P, 1])
        inexact = sbt("inexact", [P, 1])
        ones = sbt("ones", [P, 1])
        p_count = ps("p_count", [P, 512])
        ones_ready = sem("ones_ready")
        lo_summed = sem("lo_summed")
        inexact_step = sem("inexact_step")
        counted = sem("counted")
        raw = sbt("raw_ffn", [P, 44, D])
        scales = k.ffn_scales
        p_t = [ps(f"p_t{n}", [P, 4, P]) for n in range(4)]
        loaded = [sem(f"ffn_loaded{n}") for n in range(5)]
        turned = sem("turned")
        hi_ready = sem("hi_ready")
        lo_ready = sem("lo_ready")
        scales_loaded = sem("scales_loaded")
        scales_ready = sem("scales_ready")

        plan = [("w1", FB, 1, 0), ("w2", FB, 1, FB), ("h1", FB, FB, 2 * FB), ("h2", FB, FB, 2 * FB + FB * FB),
                ("w3", 1, FB, 2 * FB + 2 * FB * FB)]
        groups = []
        for n, (name, ob, ib, at) in enumerate(plan):
            if name == "w3":
                groups.append((n, [at + i for i in range(FB)], name, None))
            else:
                for i in range(ib):
                    groups.append((n, [at + o * ib + i for o in range(FB)], name, i))

        def dest(name, i, part):
            w = k.w[f"{name}_{part}"]
            return w[:, :, :].rearrange("p i d -> p (i d)") if i is None else w[:, i, :]

        block = ctx.enter_context(nc.Block())

        @block.sync
        def _(sp):
            for n, (name, ob, ib, at) in enumerate(plan):
                sp.dma_start(raw[:, at:at + ob * ib, :].rearrange("p (o i) d -> p o (i d)", o=ob),
                             a[f"L0_ffn_{name}_w"].rearrange("(o p) i -> p o i", p=P)).then_inc(loaded[n], 16)
            for n, name in enumerate(("w1", "w2", "h1", "h2")):
                sp.dma_start(scales[:, n, :], a[f"L0_ffn_{name}_s"].rearrange("(m p) -> p m", p=P),
                             allow_slow_non_contiguous=True).then_inc(scales_loaded, 16)
            sp.dma_start(k.w3_scale[:], a["L0_ffn_w3_s"].rearrange("(p o) -> p o", o=1)).then_inc(scales_loaded, 16)

        @block.tensor
        def _(pe):
            for g, (n, of, name, i) in enumerate(groups):
                pe.wait_ge(loaded[n], 16)
                at_least(pe, lo_ready, g - 3)
                for j, o in enumerate(of):
                    mm = pe.transpose(p_t[g % 4][:, j, :], raw[:, o, :], k.ident[:])
                mm.then_inc(turned, 1)
            pe.wait_ge(ones_ready, 1)
            pe.wait_ge(inexact_step, 2)
            pe.matmul(p_count[0:1, 0:1], inexact[:], ones[:], start=True, stop=True).then_inc(counted, 1)

        @block.gpsimd
        def _(pool):
            pool.memset(ones[:], 1.0).then_inc(ones_ready, 1)

        @block.scalar
        def _(act):
            def sum_lo(g):
                n, of, name, i = groups[g]
                act.wait_ge(lo_ready, g + 1)
                at_least(act, lo_summed, g)
                act.activation(lo_abs[:], dest(name, i, "lo").bitcast(F32), ACT.Abs, accum_out=lo_sums[:, g:g + 1]
                               ).then_inc(lo_summed, 1)

            for g, (n, of, name, i) in enumerate(groups):
                act.wait_ge(turned, g + 1)
                act.activation(dest(name, i, "hi"), p_t[g % 4][:].rearrange("p j d -> p (j d)"), ACT.Copy
                               ).then_inc(hi_ready, 1)
                if g >= 1:
                    sum_lo(g - 1)
            sum_lo(len(groups) - 1)

        @block.vector
        def _(dve):
            for g, (n, of, name, i) in enumerate(groups):
                dve.wait_ge(hi_ready, g + 1)
                dve.tensor_tensor(dest(name, i, "lo"), p_t[g % 4][:].rearrange("p j d -> p (j d)"),
                                  dest(name, i, "hi").bitcast(F32), ALU.subtract).then_inc(lo_ready, 1)
            dve.wait_ge(lo_summed, len(groups))
            dve.tensor_reduce(lo_sum[:], lo_sums[:], AX.X, ALU.add).then_inc(inexact_step, 1)
            dve.wait_ge(inexact_step, 1)
            dve.tensor_scalar(inexact[:], lo_sum[:], 0.0, None, ALU.not_equal).then_inc(inexact_step, 1)
            dve.wait_ge(counted, 1)
            dve.tensor_copy(k.rows_inexact[:], p_count[0:1, 0:1])
            dve.wait_ge(scales_loaded, 16 * 5)
            dve.scalar_tensor_tensor(out=k.ab_scale[:], in0=scales[:, 0, :], scalar=0.5, in1=scales[:, 1, :],
                                     op0=ALU.mult, op1=ALU.mult)
            dve.tensor_scalar(k.half_s1[:], scales[:, 0, :], 0.5, None, ALU.mult)
            dve.tensor_scalar(k.w3_gate[:], k.mod[:, 0, GB, :], k.w3_scale[:, 0:1], None, ALU.mult)


def split_product(pe, out, hi_lo_w, hi_lo_x, first, last, w_lo_is_zero=False):
    (w_hi, w_lo), (x_hi, x_lo) = hi_lo_w, hi_lo_x
    pe.matmul(out, w_hi, x_hi, start=first, stop=False)
    mm = pe.matmul(out, w_hi, x_lo, start=False, stop=last and w_lo_is_zero)
    if w_lo_is_zero:
        return mm
    return pe.matmul(out, w_lo, x_hi, start=False, stop=last)


def layer_norm_steps(nc, k, sb, sem, x_added=None):
    n = Names()
    n.stats = sb("stats", [P, NT, 6])
    n.meanvar = sb("meanvar", [P, NT, 2])
    n.var_eps = sb("var_eps", [P, NT])
    n.rstd = sb("rstd", [P, NT])
    n.xn = sb("xn", [P, NT, D])
    n.stats_step = sem("stats_step")
    n.var_ready = sem("var_ready")
    n.rstd_ready = sem("rstd_ready")
    n.xn_ready = sem("xn_ready")
    n.xn_turned = sem("xn_turned")

    def dve_stats(dve, b):
        at_least(dve, n.xn_ready, b)
        for i in range(NT):
            dve.bn_stats(n.stats[:, i, :], k.X[:, bass.ds(b * NT + i, 1), :]).then_inc(n.stats_step, 1)
        wait_apart(dve, k, n.stats_step, 3 * b + 2)
        for i in range(NT):
            ins = dve.bn_aggr(n.meanvar[:, i, :], n.stats[:, i, :])
        ins.then_inc(n.stats_step, 1)
        dve.wait_ge(n.stats_step, 3 * b + 3)
        at_least(dve, n.rstd_ready, b)
        dve.tensor_scalar(n.var_eps[:], n.meanvar[:, :, 1], EPS, None, ALU.add).then_inc(n.var_ready, 1)

    def dve_normalise(dve, b):
        dve.wait_ge(n.rstd_ready, b + 1)
        at_least(dve, n.xn_turned, b)
        for i in range(NT):
            ins = dve.tensor_scalar(n.xn[:, i, :], k.X[:, bass.ds(b * NT + i, 1), :].rearrange("p o d -> p (o d)"),
                                    n.meanvar[:, i, 0:1], n.rstd[:, i:i + 1], ALU.subtract, ALU.mult)
        ins.then_inc(n.xn_ready, 1)

    def pool_rstd(pool, b):
        pool.wait_ge(n.var_ready, b + 1)
        at_least(pool, n.xn_ready, b)
        pool.tensor_tensor(n.rstd[:], n.var_eps[:], k.minus_half[:, 0:NT], ALU.pow).then_inc(n.rstd_ready, 1)

    def pe_turn(pe, b, p_m):
        pe.wait_ge(n.xn_ready, b + 1)
        for i in range(NT):
            mm = pe.transpose(p_m[:, i * P:(i + 1) * P], n.xn[:, i, :], k.ident[:])
        mm.then_inc(n.xn_turned, 1)

    n.dve_stats, n.dve_normalise, n.pool_rstd, n.pe_turn = dve_stats, dve_normalise, pool_rstd, pe_turn
    return n


def ffn0(nc, k):
    with ExitStack() as ctx:
        sb, ps, sem = tensors(nc, ctx, "ffn0s")
        ln = layer_norm_steps(nc, k, sb, sem)
        HB = FB // 2
        hT = sb("hT", [P, S])
        h_hi = [sb(f"h_hi{n}", [P, S], F32R) for n in range(2)]
        h_lo = [sb(f"h_lo{n}", [P, S], F32R) for n in range(2)]
        tanh_a = [sb(f"tanh_a{n}", [P, 2, S]) for n in range(HB)]
        gated = [sb(f"gated{n}", [P, 2, S]) for n in range(HB)]
        u = [sb(f"u{n}", [P, 2, S]) for n in range(2)]
        u_hi, u_lo, g1_hi, g1_lo, g2_hi, g2_lo = (
            [sb(f"{name}{n}", [P, FB, S], F32R) for n in range(2)]
            for name in ("u_hi", "u_lo", "g1_hi", "g1_lo", "g2_hi", "g2_lo"))
        g = [sb(f"g{n}", [P, 2, S]) for n in range(2)]
        yT = sb("yT", [P, S])

        p_a = [ps(f"p_a{n}", [P, 2, S]) for n in range(HB)]
        p_b = [ps(f"p_b{n}", [P, 2, S]) for n in range(HB)]
        p_h = [ps(f"p_h{n}", [P, 2, S]) for n in range(HB)]
        p_m = ps("p_m", [P, 512])
        p_y = ps("p_y", [P, 512])

        hT_ready = sem("hT_ready")
        h_hi_ready = sem("h_hi_ready")
        h_lo_ready = sem("h_lo_ready")
        a_made = sem("a_made")
        b_made = sem("b_made")
        tanh_ready = sem("tanh_ready")
        gated_ready = sem("gated_ready")
        u_ready = sem("u_ready")
        u_hi_ready = sem("u_hi_ready")
        u_lo_ready = sem("u_lo_ready")
        h1_made = sem("h1_made")
        g1_ready = sem("g1_ready")
        g1_lo_ready = sem("g1_lo_ready")
        h2_made = sem("h2_made")
        g2_ready = sem("g2_ready")
        g2_lo_ready = sem("g2_lo_ready")
        y_made = sem("y_made")
        yT_ready = sem("yT_ready")
        y_turned = sem("y_turned")
        x_added = sem("x_added")

        def pe_ab(pe, b, r, exact):
            pe.wait_ge(h_lo_ready, b + 1)
            for q in range(HB):
                for bank, name, made in ((p_a[q], "w1", a_made), (p_b[q], "w2", b_made)):
                    at_least(pe, u_ready, HB * (b - 1) + q + 1)
                    w = k.w[name + "_hi"], k.w[name + "_lo"]
                    for m in range(2):
                        cols = slice((2 * q + m) * P, (2 * q + m + 1) * P)
                        mm = split_product(pe, bank[:, m, :], [x[:, 0, cols] for x in w], (h_hi[r][:], h_lo[r][:]),
                                           True, True, exact)
                    mm.then_inc(made, 1)

        def pe_hidden(pe, b, r, exact, name, x_hi, x_lo, x_ready, before, made):
            w = k.w[name + "_hi"], k.w[name + "_lo"]
            for q in range(HB):
                before(q)
                for m in range(2):
                    cols = slice((2 * q + m) * P, (2 * q + m + 1) * P)
                    for i in range(FB):
                        if q == m == 0 and i % 2 == 0:
                            pe.wait_ge(x_ready, HB * b + i // 2 + 1)
                        mm = split_product(pe, p_h[q][:, m, :], [x[:, i, cols] for x in w],
                                           (x_hi[r][:, i, :], x_lo[r][:, i, :]), i == 0, i == FB - 1, exact)
                mm.then_inc(made, 1)

        def pe_w3(pe, b, r, exact):
            pe.wait_ge(g2_lo_ready, HB * (b + 1))
            at_least(pe, yT_ready, b)
            for i in range(FB):
                mm = split_product(pe, p_y[:, 0:S], (k.w["w3_hi"][:, i, :], k.w["w3_lo"][:, i, :]),
                                   (g2_hi[r][:, i, :], g2_lo[r][:, i, :]), i == 0, i == FB - 1, exact)
            mm.then_inc(y_made, 1)

        def pe_step(pe, n, r, exact):
            if batch_valid(n - 2):
                def free1(q):
                    at_least(pe, g2_ready, HB * (n - 4) + q + 1)
                pe_hidden(pe, n - 2, r, exact, "h1", u_hi, u_lo, u_lo_ready, free1, h1_made)
            if batch_valid(n - 5):
                pe.wait_ge(yT_ready, n - 4)
                if batch_valid(n - 1):
                    pe.wait_ge(h_hi_ready, n)
                at_least(pe, x_added, n - 5)
                for i in range(NT):
                    mm = pe.transpose(p_m[:, i * P:(i + 1) * P], yT[:, i * P:(i + 1) * P], k.ident[:])
                mm.then_inc(y_turned, 1)
            if batch_valid(n - 1):
                pe_ab(pe, n - 1, (r + 1) % 2, exact)
            if batch_valid(n - 4):
                pe_w3(pe, n - 4, r, exact)
            if batch_valid(n):
                at_least(pe, x_added, n - 4)
                ln.pe_turn(pe, n, p_m)
            if batch_valid(n - 3):
                def free2(q):
                    if batch_valid(n - 2):
                        pe.wait_ge(g1_ready, HB * (n - 2) + q + 1)
                    else:
                        at_least(pe, g2_ready, HB * (n - 4) + q + 1)
                pe_hidden(pe, n - 3, (r + 1) % 2, exact, "h2", g1_hi, g1_lo, g1_lo_ready, free2, h2_made)

        def act_h(act, b, r):
            act.wait_ge(ln.xn_turned, b + 1)
            at_least(act, h_lo_ready, b)
            scale, bias = k.mod[:, 0, CB, bass.ds(b, 1)], k.mod[:, 0, SB, bass.ds(b, 1)]
            act.activation(hT[:], p_m[:, 0:S], ACT.Identity, bias=bias, scale=scale).then_inc(hT_ready, 1)
            if not isinstance(b, int) or b >= 2:
                wait_apart(act, k, b_made, HB * (b - 1))
            act.activation(h_hi[r][:], p_m[:, 0:S], ACT.Identity, bias=bias, scale=scale).then_inc(h_hi_ready, 1)

        def act_tanh(act, b, q):
            act.wait_ge(a_made, HB * b + q + 1)
            at_least(act, gated_ready, HB * (b - 1) + q + 1)
            for m in range(2):
                ins = act.activation(tanh_a[q][:, m, :], p_a[q][:, m, :], ACT.Tanh,
                                     scale=k.half_s1[:, 2 * q + m:2 * q + m + 1])
            ins.then_inc(tanh_ready, 1)

        def act_u_hi(act, b, r, q):
            act.wait_ge(u_ready, HB * b + q + 1)
            at_least(act, h1_made, HB * (b - 1))
            act.activation(u_hi[r][:, 2 * q:2 * q + 2, :], u[q][:], ACT.Copy).then_inc(u_hi_ready, 1)

        def act_gelu(act, b, r, q, layer, made, g_hi, g_ready, g_lo_ready, g_read, g_used):
            act.wait_ge(made, HB * b + q + 1)
            g_used(q)
            for m in range(2):
                act.activation(g[q][:, m, :], p_h[q][:, m, :], ACT.Gelu,
                               scale=k.ffn_scales[:, layer, 2 * q + m:2 * q + m + 1])
            at_least(act, g_read, (b - 1) * HB if layer == 2 else b - 1)
            for m in range(2):
                ins = act.activation(g_hi[r][:, 2 * q + m, :], p_h[q][:, m, :], ACT.Gelu,
                                     scale=k.ffn_scales[:, layer, 2 * q + m:2 * q + m + 1])
            ins.then_inc(g_ready, 1)

        def act_step(act, n, r):
            if batch_valid(n - 2):
                def used1(q):
                    at_least(act, g2_lo_ready, HB * (n - 4) + q + 1)
                for q in range(HB):
                    act_gelu(act, n - 2, r, q, 2, h1_made, g1_hi, g1_ready, g1_lo_ready, h2_made, used1)
            if batch_valid(n - 1):
                for q in range(HB):
                    act_tanh(act, n - 1, q)
            if batch_valid(n - 1):
                act_u_hi(act, n - 1, (r + 1) % 2, 0)
            if batch_valid(n - 3):
                def used2(q):
                    if batch_valid(n - 2):
                        act.wait_ge(g1_lo_ready, HB * (n - 2) + q + 1)
                    else:
                        at_least(act, g2_lo_ready, HB * (n - 4) + q + 1)
                act_gelu(act, n - 3, (r + 1) % 2, 0, 3, h2_made, g2_hi, g2_ready, g2_lo_ready, y_made, used2)
            if batch_valid(n - 1):
                act_u_hi(act, n - 1, (r + 1) % 2, 1)
            if batch_valid(n):
                act_h(act, n, r)
            if batch_valid(n - 3):
                act_gelu(act, n - 3, (r + 1) % 2, 1, 3, h2_made, g2_hi, g2_ready, g2_lo_ready, y_made, used2)
            if batch_valid(n - 4):
                act.wait_ge(y_made, n - 3)
                at_least(act, y_turned, n - 4)
                act.activation(yT[:], p_y[:, 0:S], ACT.Copy, scale=k.w3_gate[:, bass.ds(n - 4, 1)]
                               ).then_inc(yT_ready, 1)

        def dve_u(dve, b, r, q):
            dve.wait_ge(tanh_ready, HB * b + q + 1)
            at_least(dve, u_ready, HB * (b - 1) + q + 1)
            dve.scalar_tensor_tensor(out=gated[q][:], in0=tanh_a[q][:], scalar=1.0, in1=p_a[q][:],
                                     op0=ALU.add, op1=ALU.mult).then_inc(gated_ready, 1)
            dve.wait_ge(gated_ready, HB * b + q + 1)
            dve.wait_ge(b_made, HB * b + q + 1)
            at_least(dve, u_lo_ready, HB * (b - 1) + q + 1)
            for m in range(2):
                ins = dve.scalar_tensor_tensor(out=u[q][:, m, :], in0=p_b[q][:, m, :],
                                               scalar=k.ab_scale[:, 2 * q + m:2 * q + m + 1], in1=gated[q][:, m, :],
                                               op0=ALU.mult, op1=ALU.mult)
            ins.then_inc(u_ready, 1)

        def dve_lo(dve, b, r, q, ready, read, read_at, lo, hi, g_buf, lo_ready):
            dve.wait_ge(ready, HB * b + q + 1)
            at_least(dve, read, read_at)
            dve.tensor_tensor(lo[r][:, 2 * q:2 * q + 2, :], g_buf[q][:], hi[r][:, 2 * q:2 * q + 2, :].bitcast(F32),
                              ALU.subtract).then_inc(lo_ready, 1)

        def dve_step(dve, n, r):
            o = (r + 1) % 2
            if batch_valid(n + 1):
                ln.dve_stats(dve, n + 1)
            if batch_valid(n - 2):
                for q in range(HB):
                    dve_lo(dve, n - 2, r, q, g1_ready, h2_made, HB * (n - 3), g1_lo, g1_hi, g, g1_lo_ready)
            if batch_valid(n - 5):
                dve.wait_ge(y_turned, n - 4)
                x = k.X[:, bass.ds((n - 5) * NT, NT), :]
                dve.tensor_tensor(x, x, p_m[:, 0:S].rearrange("p (i d) -> p i d", i=NT), ALU.add
                                  ).then_inc(x_added, 1)
            if batch_valid(n - 1):
                for q in range(HB):
                    dve_u(dve, n - 1, o, q)
                for q in range(HB):
                    dve_lo(dve, n - 1, o, q, u_hi_ready, h1_made, HB * (n - 2), u_lo, u_hi, u, u_lo_ready)
            if batch_valid(n):
                dve.wait_ge(h_hi_ready, n + 1)
                dve.wait_ge(hT_ready, n + 1)
                at_least(dve, b_made, HB * (n - 1))
                dve.tensor_tensor(h_lo[r][:], hT[:], h_hi[r][:].bitcast(F32), ALU.subtract).then_inc(h_lo_ready, 1)
            if batch_valid(n + 1):
                ln.dve_normalise(dve, n + 1)
            if batch_valid(n - 3):
                for q in range(HB):
                    dve_lo(dve, n - 3, o, q, g2_ready, y_made, n - 4, g2_lo, g2_hi, g, g2_lo_ready)

        WHOLE0, LOOPS, LAST = 5, 5, B + 5

        block = ctx.enter_context(nc.Block())

        @block.gpsimd
        def _(pool):
            ln.pool_rstd(pool, 0)
            with pool.Fori(1, B) as b:
                ln.pool_rstd(pool, b)

        def pe_program(pe, exact):
            for n in range(WHOLE0):
                pe_step(pe, n, n % 2, exact)
            with pe.Fori(0, LOOPS) as turn:
                for r in range(2):
                    pe_step(pe, turn * 2 + (WHOLE0 + r), (WHOLE0 + r) % 2, exact)
            for n in range(WHOLE0 + 2 * LOOPS, LAST):
                pe_step(pe, n, n % 2, exact)

        @block.tensor
        def _(pe):
            rows_inexact = pe.value_load(k.rows_inexact[0:1, 0:1], min_val=0, max_val=P)
            with pe.If(rows_inexact == 0):
                pe_program(pe, exact=True)
            with pe.Else():
                pe_program(pe, exact=False)

        @block.scalar
        def _(act):
            for n in range(WHOLE0):
                act_step(act, n, n % 2)
            with act.Fori(0, LOOPS) as turn:
                for r in range(2):
                    act_step(act, turn * 2 + (WHOLE0 + r), (WHOLE0 + r) % 2)
            for n in range(WHOLE0 + 2 * LOOPS, LAST):
                act_step(act, n, n % 2)

        @block.vector
        def _(dve):
            ln.dve_stats(dve, 0)
            ln.dve_normalise(dve, 0)
            for n in range(WHOLE0):
                dve_step(dve, n, n % 2)
            with dve.Fori(0, LOOPS) as turn:
                for r in range(2):
                    dve_step(dve, turn * 2 + (WHOLE0 + r), (WHOLE0 + r) % 2)
            for n in range(WHOLE0 + 2 * LOOPS, LAST):
                dve_step(dve, n, n % 2)


H1 = 4
DH1 = D // H1
MASKED = -1e30


def attention1_weights(nc, k, a, wsb):
    for name in ("wq1", "wk1", "wv1", "wo1"):
        k.w[name] = wsb(name, [P, D])
    k.memz = wsb("memz", [P, D + H1])
    k.gate_m = wsb("gate_m", [P, 1])
    k.gate_a = wsb("gate_a", [P, 1])
    k.gbo1 = wsb("gbo1", [P, B])
    k.mask16 = wsb("mask16", [P, P], BF16)
    with ExitStack() as ctx:
        sb, ps, sem = tensors(nc, ctx, "att1w")
        raw = sb("raw", [P, 4, D])
        beta = sb("beta", [P, 1])
        tanh_b = sb("tanh_b", [P, 1])
        bo = sb("bo", [P, 1])
        p_t = ps("p_t", [P, 4, D])
        loaded = sem("loaded")
        cleared = sem("cleared")
        mem_loaded = sem("mem_loaded")
        turned = sem("turned")
        tanh_ready = sem("tanh_ready")
        gate_ready = sem("gate_ready")
        mask_ready = sem("mask_ready")
        names = ("Wq", "Wk", "Wv", "Wo")
        block = ctx.enter_context(nc.Block())

        @block.sync
        def _(sp):
            for n, name in enumerate(names):
                sp.dma_start(raw[:, n, :], a[f"L1_attn_{name}"]).then_inc(loaded, 16)
            sp.dma_start(bo[:], a["L1_attn_bo"].rearrange("(d o) -> d o", o=1)).then_inc(loaded, 16)
            for h in range(H1):
                rows = slice(h * DH1, (h + 1) * DH1)
                sp.dma_start(beta[rows, :], a["L1_attn_betas"][0, h].to_broadcast([DH1, 1])).then_inc(loaded, 16)
            sp.wait_ge(cleared, 1)
            for h in range(H1):
                rows = slice(h * DH1, (h + 1) * DH1)
                sp.dma_start(k.memz[rows, rows], a["L1_attn_mem"][h]).then_inc(mem_loaded, 16)
                sp.dma_start(k.memz[rows, D + h:D + h + 1], a["L1_attn_z"][h]).then_inc(mem_loaded, 16)
            sp.wait_ge(mem_loaded, 16 * 2 * H1)

        @block.gpsimd
        def _(pool):
            pool.memset(k.memz[:], 0.0).then_inc(cleared, 1)
            pool.memset(k.mask16[:], 0.0).then_inc(mask_ready, 1)
            pool.wait_ge(mask_ready, 1)
            pool.affine_select(out=k.mask16[:], in_=k.mask16[:], compare_op=ALU.is_ge, fill=MASKED, base=0,
                               pattern=[[-1, P]], channel_multiplier=1).then_inc(mask_ready, 1)

        @block.tensor
        def _(pe):
            pe.wait_ge(loaded, 16 * 9)
            for n in range(4):
                mm = pe.transpose(p_t[:, n, :], raw[:, n, :], k.ident[:])
            mm.then_inc(turned, 1)

        @block.scalar
        def _(act):
            act.wait_ge(loaded, 16 * 9)
            act.activation(tanh_b[:], beta[:], ACT.Tanh, scale=0.5).then_inc(tanh_ready, 1)

        @block.vector
        def _(dve):
            dve.wait_ge(tanh_ready, 1)
            dve.tensor_scalar(k.gate_m[:], tanh_b[:], 0.5, 0.5, ALU.mult, ALU.add).then_inc(gate_ready, 1)
            dve.tensor_scalar(k.gate_a[:], tanh_b[:], -0.5, 0.5, ALU.mult, ALU.add)
            dve.wait_ge(mem_loaded, 16 * 2 * H1)
            dve.wait_ge(gate_ready, 1)
            dve.tensor_scalar(k.memz[:, 0:D], k.memz[:, 0:D], k.gate_m[:, 0:1], None, ALU.mult)
            dve.tensor_scalar(k.gbo1[:], k.mod[:, 1, GA, :], bo[:, 0:1], None, ALU.mult)
            dve.wait_ge(turned, 1)
            for n, name in enumerate(("wq1", "wk1", "wv1", "wo1")):
                dve.tensor_copy(k.w[name][:], p_t[:, n, :])


def attention1(nc, k):
    with ExitStack() as ctx:
        sb, ps, sem = tensors(nc, ctx, "att1")
        ln = layer_norm_steps(nc, k, sb, sem)
        hT = [sb(f"hT{n}", [P, S]) for n in range(2)]
        qT = sb("qT", [P, S])
        kT = sb("kT", [P, S])
        q_hi = [sb(f"q_hi{n}", [P, H1, S], F32R) for n in range(2)]
        q_lo = [sb(f"q_lo{n}", [P, H1, S], F32R) for n in range(2)]
        k_hi = [sb(f"k_hi{n}", [P, S], F32R) for n in range(2)]
        k_lo = [sb(f"k_lo{n}", [P, S], F32R) for n in range(2)]
        q_min = sb("q_min", [P, S])
        q_exp = sb("q_exp", [P, S])
        sq = [sb(f"sq{n}", [P, S]) for n in range(2)]
        V = [sb(f"V{n}", [P, NT, D]) for n in range(2)]
        rowmax = sb("rowmax", [P, NT, H1])
        negmax = sb("negmax", [P, NT, H1])
        sums = sb("sums", [P, NT, H1])
        rsums = sb("rsums", [P, NT, H1])
        prob0 = [sb(f"prob0_{n}", [P, H1, P]) for n in range(2)]
        prob1 = [sb(f"prob1_{n}", [P, H1, S]) for n in range(2)]
        probT0 = sb("probT0", [P, H1, S])
        probT1 = sb("probT1", [P, H1, P])
        den = sb("den", [P, NT, H1])
        rden = sb("rden", [P, NT, H1])
        A = [sb(f"A{n}", [P, NT, H1, DH1]) for n in range(2)]
        OT = sb("OT", [P, S])
        OTA = sb("OTA", [P, S])
        yT = sb("yT", [P, S])

        p_s0 = ps("p_s0", [P, H1, P])
        p_s1 = ps("p_s1", [P, H1, S])
        p_t = [ps(f"p_t{n}", [P, 512]) for n in range(2)]
        p_o = ps("p_o", [P, 512])
        p_m = ps("p_m", [P, 512])
        p_n = ps("p_n", [P, 512])

        cleared = sem("cleared")
        hT_ready = sem("hT_ready")
        qk_made = sem("qk_made")
        qT_ready = sem("qT_ready")
        kT_ready = sem("kT_ready")
        k_hi_ready = sem("k_hi_ready")
        k_lo_ready = sem("k_lo_ready")
        q_hi_ready = sem("q_hi_ready")
        q_lo_ready = sem("q_lo_ready")
        q_min_ready = sem("q_min_ready")
        q_exp_ready = sem("q_exp_ready")
        sq_ready = sem("sq_ready")
        v_made = sem("v_made")
        v_ready = sem("v_ready")
        scored = sem("scored")
        maxed = sem("maxed")
        negmax_ready = sem("negmax_ready")
        exped = sem("exped")
        rsums_ready = sem("rsums_ready")
        probs_ready = sem("probs_ready")
        probs_turned = sem("probs_turned")
        probT_ready = sem("probT_ready")
        pv_made = sem("pv_made")
        a_made = sem("a_made")
        den_ready = sem("den_ready")
        rden_ready = sem("rden_ready")
        A_ready = sem("A_ready")
        A_turned = sem("A_turned")
        OT_ready = sem("OT_ready")
        OTA_ready = sem("OTA_ready")
        y_made = sem("y_made")
        yT_ready = sem("yT_ready")
        y_turned = sem("y_turned")
        x_added = sem("x_added")

        def pe_step(pe, n, r):
            f, m, t, y = n, n - 1, n - 2, n - 3
            o = (r + 1) % 2
            if batch_valid(f):
                at_least(pe, v_ready, m)
                at_least(pe, OTA_ready, t)
                ln.pe_turn(pe, f, p_m)
            if batch_valid(m):
                for i, (bank, keys) in enumerate(((p_s0, P), (p_s1, S))):
                    pe.wait_ge(k_lo_ready, n)
                    pe.wait_ge(q_lo_ready, n)
                    at_least(pe, exped, 2 * m - 1 + i)
                    rows = slice(i * P, (i + 1) * P)
                    for h in range(H1):
                        out = bank[:, h, :]
                        pe.matmul(out, q_hi[o][:, h, rows], k_hi[o][:, 0:keys], start=True, stop=False,
                                  skip_group_check=True)
                        pe.matmul(out, q_hi[o][:, h, rows], k_lo[o][:, 0:keys], start=False, stop=False,
                                  skip_group_check=True)
                        pe.matmul(out, q_lo[o][:, h, rows], k_hi[o][:, 0:keys], start=False, stop=False,
                                  skip_group_check=True)
                        mm = pe.matmul(bank[:, h, keys - P:keys], k.ident16[:], k.mask16[:], start=False, stop=True,
                                       skip_group_check=True)
                    mm.then_inc(scored, 1)
            if batch_valid(y):
                if batch_valid(f):
                    pe.wait_ge(hT_ready, f + 1)
                pe.wait_ge(OTA_ready, t)
                pe.wait_ge(yT_ready, y + 1)
                for i in range(NT):
                    mm = pe.transpose(p_m[:, i * P:(i + 1) * P], yT[:, i * P:(i + 1) * P], k.ident[:])
                mm.then_inc(y_turned, 1)
            if batch_valid(f):
                pe.wait_ge(hT_ready, f + 1)
                at_least(pe, A_ready, m)
                at_least(pe, yT_ready, t)
                pe.matmul(p_n[:, 0:S], k.w["wq1"][:], hT[r][:], start=True, stop=True)
                pe.matmul(p_n[:, S:2 * S], k.w["wk1"][:], hT[r][:], start=True, stop=True).then_inc(qk_made, 1)
            if batch_valid(m):
                if batch_valid(f):
                    pe.wait_ge(hT_ready, f + 1)
                at_least(pe, x_added, t)
                at_least(pe, OTA_ready, t)
                for i in range(NT):
                    mm = pe.matmul(p_m[:, i * D:(i + 1) * D], hT[o][:, i * P:(i + 1) * P], k.w["wv1"][:],
                                   start=True, stop=True)
                mm.then_inc(v_made, 1)
            if batch_valid(t):
                pe.wait_ge(probs_ready, t + 1)
                for g in range(2):
                    at_least(pe, probT_ready, 3 * t - (1 if g == 0 else 1))
                    for h in range(2):
                        pe.transpose(p_t[g][:, h * S:h * S + P], prob0[r][:, 2 * g + h, :], k.ident[:])
                        mm = pe.transpose(p_t[g][:, h * S + P:(h + 1) * S], prob1[r][:, 2 * g + h, 0:P], k.ident[:])
                    mm.then_inc(probs_turned, 1)
            if batch_valid(m):
                pe.wait_ge(sq_ready, n)
                if batch_valid(f):
                    pe.wait_ge(kT_ready, f + 1)
                    pe.wait_ge(qT_ready, f + 1)
                at_least(pe, yT_ready, t)
                for i in range(NT):
                    mm = pe.matmul(p_n[:, i * S:i * S + D + H1], sq[o][:, i * P:(i + 1) * P], k.memz[:],
                                   start=True, stop=True)
                mm.then_inc(a_made, 1)
            if batch_valid(t):
                pe.wait_ge(probT_ready, 3 * t + 1)
                for h in range(H1):
                    mm = pe.transpose(p_t[0][:, h * P:(h + 1) * P], prob1[r][:, h, P:S], k.ident[:])
                mm.then_inc(probs_turned, 1)
                if batch_valid(m):
                    pe.wait_ge(v_ready, m + 1)
                at_least(pe, x_added, t)
                pe.wait_ge(A_ready, t + 1)
                for i in range(NT):
                    mm = pe.transpose(p_m[:, i * P:(i + 1) * P], A[r][:, i].rearrange("p h d -> p (h d)"), k.ident[:])
                mm.then_inc(A_turned, 1)
                pe.wait_ge(probT_ready, 3 * t + 3)
                at_least(pe, OT_ready, t)
                for j, (keys, q0) in enumerate(((probT0, 0), (probT1, P))):
                    for h in range(H1):
                        rows = slice(h * DH1, (h + 1) * DH1)
                        mm = pe.matmul(p_o[rows, q0:S], V[r][:, j, rows], keys[:, h, :], start=(j == 0), stop=(j == 1),
                                       skip_group_check=True)
                mm.then_inc(pv_made, 1)
                if batch_valid(m):
                    pe.wait_ge(A_ready, m + 1)
                pe.wait_ge(OTA_ready, t + 1)
                at_least(pe, yT_ready, t)
                pe.matmul(p_n[:, 0:S], k.w["wo1"][:], OTA[:], start=True, stop=True).then_inc(y_made, 1)

        def act_step(act, n, r):
            f, m, t = n, n - 1, n - 2
            o = (r + 1) % 2
            if batch_valid(f):
                act.wait_ge(ln.xn_turned, f + 1)
                at_least(act, v_made, m)
                act.activation(hT[r][:], p_m[:, 0:S], ACT.Identity, bias=k.mod[:, 1, SA, bass.ds(f, 1)],
                               scale=k.mod[:, 1, CA, bass.ds(f, 1)]).then_inc(hT_ready, 1)
            if batch_valid(m):
                for i, (bank, prob) in enumerate(((p_s0, prob0), (p_s1, prob1))):
                    act.wait_ge(negmax_ready, 2 * m + i + 1)
                    at_least(act, probs_turned, 3 * (t - 1) + 3)
                    at_least(act, rsums_ready, m)
                    for h in range(H1):
                        ins = act.activation(prob[o][:, h, :], bank[:, h, :], ACT.Exp, bias=negmax[:, i, h:h + 1],
                                             accum_out=sums[:, i, h:h + 1])
                    ins.then_inc(exped, 1)
            if batch_valid(f):
                act.wait_ge(qk_made, f + 1)
                at_least(act, q_lo_ready, f)
                at_least(act, sq_ready, f)
                act.activation(qT[:], p_n[:, 0:S], ACT.Copy).then_inc(qT_ready, 1)
                at_least(act, k_lo_ready, f)
                act.activation(kT[:], p_n[:, S:2 * S], ACT.Copy).then_inc(kT_ready, 1)
                act.wait_ge(kT_ready, f + 1)
                at_least(act, scored, 2 * m)
                act.activation(k_hi[r][:], kT[:], ACT.Copy).then_inc(k_hi_ready, 1)
                act.wait_ge(q_min_ready, f + 1)
                at_least(act, sq_ready, f)
                act.activation(q_exp[:], q_min[:], ACT.Exp).then_inc(q_exp_ready, 1)
            if batch_valid(m):
                act.wait_ge(v_made, m + 1)
                at_least(act, pv_made, m - 1)
                act.activation(V[o][:], p_m[:, 0:NT * D].rearrange("p (i d) -> p i d", i=NT), ACT.Copy
                               ).then_inc(v_ready, 1)
            if batch_valid(t):
                for g in range(2):
                    act.wait_ge(probs_turned, 3 * t + g + 1)
                    at_least(act, pv_made, t)
                    act.activation(probT0[:, 2 * g:2 * g + 2, :], p_t[g][:].rearrange("p (h q) -> p h q", h=2), ACT.Copy
                                   ).then_inc(probT_ready, 1)
                act.wait_ge(probs_turned, 3 * t + 3)
                act.activation(probT1[:], p_t[0][:].rearrange("p (h q) -> p h q", h=H1), ACT.Copy).then_inc(probT_ready, 1)
                act.wait_ge(pv_made, t + 1)
                at_least(act, OTA_ready, t)
                act.activation(OT[:], p_o[:, 0:S], ACT.Copy, scale=k.gate_a[:, 0:1]).then_inc(OT_ready, 1)
                act.wait_ge(y_made, t + 1)
                at_least(act, y_turned, t)
                act.activation(yT[:], p_n[:, 0:S], ACT.Identity, bias=k.gbo1[:, bass.ds(t, 1)],
                               scale=k.mod[:, 1, GA, bass.ds(t, 1)]).then_inc(yT_ready, 1)

        def dve_step(dve, n, r):
            f, m, t, y = n, n - 1, n - 2, n - 3
            o = (r + 1) % 2
            if batch_valid(f + 1):
                ln.dve_stats(dve, f + 1)
            if batch_valid(m):
                for i, bank in enumerate((p_s0, p_s1)):
                    dve.wait_ge(scored, 2 * m + i + 1)
                    at_least(dve, exped, 2 * m)
                    dve.tensor_reduce(rowmax[:, i, :], bank[:], AX.X, ALU.max).then_inc(maxed, 1)
                    dve.wait_ge(maxed, 2 * m + i + 1)
                    dve.tensor_scalar(negmax[:, i, :], rowmax[:, i, :], -1.0, None, ALU.mult).then_inc(negmax_ready, 1)
            if batch_valid(y):
                dve.wait_ge(y_turned, y + 1)
                x = k.X[:, bass.ds(y * NT, NT), :]
                dve.tensor_tensor(x, x, p_m[:, 0:S].rearrange("p (i d) -> p i d", i=NT), ALU.add).then_inc(x_added, 1)
            if batch_valid(f):
                dve.wait_ge(qT_ready, f + 1)
                at_least(dve, q_exp_ready, f)
                dve.tensor_scalar(q_min[:], qT[:], 0.0, None, ALU.min).then_inc(q_min_ready, 1)
                at_least(dve, scored, 2 * m)
                for h in range(H1):
                    rows = slice(h * DH1, (h + 1) * DH1)
                    ins = dve.tensor_copy(q_hi[r][rows, h, :], qT[rows, :])
                ins.then_inc(q_hi_ready, 1)
                dve.wait_ge(k_hi_ready, f + 1)
                dve.tensor_tensor(k_lo[r][:], kT[:], k_hi[r][:].bitcast(F32), ALU.subtract).then_inc(k_lo_ready, 1)
                dve.wait_ge(q_hi_ready, f + 1)
                for h in range(H1):
                    rows = slice(h * DH1, (h + 1) * DH1)
                    ins = dve.tensor_tensor(q_lo[r][rows, h, :], qT[rows, :], q_hi[r][rows, h, :].bitcast(F32),
                                            ALU.subtract)
                ins.then_inc(q_lo_ready, 1)
                dve.wait_ge(q_exp_ready, f + 1)
                at_least(dve, a_made, m)
                dve.scalar_tensor_tensor(out=sq[r][:], in0=qT[:], scalar=0.0, in1=q_exp[:], op0=ALU.max, op1=ALU.add
                                         ).then_inc(sq_ready, 1)
            if batch_valid(m):
                dve.wait_ge(exped, 2 * m + 2)
                at_least(dve, probs_ready, m)
                dve.reciprocal(rsums[:], sums[:]).then_inc(rsums_ready, 1)
                dve.wait_ge(a_made, m + 1)
                read = p_n[:].rearrange("p (i c) -> p i c", i=NT)
                dve.tensor_scalar(den[:], read[:, :, D:D + H1], 1e-6, None, ALU.add).then_inc(den_ready, 1)
                dve.wait_ge(den_ready, m + 1)
                dve.reciprocal(rden[:], den[:]).then_inc(rden_ready, 1)
                dve.wait_ge(rden_ready, m + 1)
                at_least(dve, A_turned, m - 1)
                for i in range(NT):
                    ins = dve.tensor_tensor(A[o][:, i], read[:, i, 0:D].rearrange("p (h d) -> p h d", h=H1),
                                            rden[:, i, :].unsqueeze(2).to_broadcast([P, H1, DH1]), ALU.mult)
                ins.then_inc(A_ready, 1)
            if batch_valid(t):
                dve.wait_ge(A_turned, t + 1)
                dve.wait_ge(OT_ready, t + 1)
                at_least(dve, y_made, t)
                dve.tensor_tensor(OTA[:], OT[:], p_m[:, 0:S], ALU.add).then_inc(OTA_ready, 1)
            if batch_valid(f + 1):
                ln.dve_normalise(dve, f + 1)

        def pool_step(pool, n, r):
            m = n - 1
            o = (r + 1) % 2
            if batch_valid(n + 1):
                ln.pool_rstd(pool, n + 1)
            if batch_valid(m):
                wait_apart(pool, k, rsums_ready, m + 1)
                for i, prob in enumerate((prob0, prob1)):
                    for h in range(H1):
                        ins = pool.tensor_scalar(prob[o][:, h, :], prob[o][:, h, :], rsums[:, i, h:h + 1], 0.0,
                                                 ALU.mult, ALU.add)
                ins.then_inc(probs_ready, 1)

        WHOLE0, LOOPS, LAST = 3, 6, B + 3
        block = ctx.enter_context(nc.Block())

        def walk(eng, step, last=LAST):
            for n in range(WHOLE0):
                step(eng, n, n % 2)
            with eng.Fori(0, LOOPS) as turn:
                for r in range(2):
                    step(eng, turn * 2 + (WHOLE0 + r), (WHOLE0 + r) % 2)
            for n in range(WHOLE0 + 2 * LOOPS, last):
                step(eng, n, n % 2)

        @block.gpsimd
        def _(pool):
            for n in range(2):
                pool.memset(q_hi[n][:].bitcast(F32), 0.0)
                ins = pool.memset(q_lo[n][:].bitcast(F32), 0.0)
            ins.then_inc(cleared, 1)
            ln.pool_rstd(pool, 0)
            walk(pool, pool_step, B + 1)

        @block.tensor
        def _(pe):
            pe.wait_ge(cleared, 1)
            walk(pe, pe_step)

        @block.scalar
        def _(act):
            walk(act, act_step)

        @block.vector
        def _(dve):
            dve.wait_ge(cleared, 1)
            ln.dve_stats(dve, 0)
            ln.dve_normalise(dve, 0)
            walk(dve, dve_step)


E = 8
TOP = 2
U = 2 * S
UNITS = B * S // U
UT = U // P
TILES_ALL = B * NT
CP = 3


def moe_weights(nc, k, a, wsb):
    for part in ("hi", "lo"):
        k.w["gu_" + part] = wsb("gu_" + part, [P, E, 2, P], F32R)
        k.w["dn_" + part] = wsb("dn_" + part, [P, E, P], F32R)
    k.wg = wsb("wg", [P, E])
    k.bg = wsb("bg", [P, E])
    k.sel16 = wsb("sel16", [P, E, P], BF16)
    with ExitStack() as ctx:
        sb, ps, sem = tensors(nc, ctx, "moew")
        raw = sb("raw", [P, 3 * E, D])
        raw_g = sb("raw_g", [E, D])
        sel = sb("sel", [P, E])
        ones = sb("ones", [P, P])
        p_t = [ps(f"p_t{n}", [P, 4, P]) for n in range(4)]
        p_g = ps("p_g", [P, 512])
        loaded = [sem(f"loaded{n}") for n in range(2)]
        small_loaded = sem("small_loaded")
        turned = sem("turned")
        hi_ready = sem("hi_ready")
        lo_ready = sem("lo_ready")
        wg_turned = sem("wg_turned")
        sel_step = sem("sel_step")
        GU_GROUPS, GROUPS = 2 * E // 4, 3 * E // 4

        def dest(g, part):
            if g < GU_GROUPS:
                return k.w["gu_" + part][:, 2 * g:2 * g + 2].rearrange("p e c o -> p (e c) o")
            at = 4 * (g - GU_GROUPS)
            return k.w["dn_" + part][:, at:at + 4, :]

        block = ctx.enter_context(nc.Block())

        @block.sync
        def _(sp):
            sp.dma_start(raw_g[:], a["L1_ffn_Wg"]).then_inc(small_loaded, 16)
            sp.dma_start(k.bg[:], a["L1_ffn_bg"].rearrange("(o e) -> o e", o=1).to_broadcast([P, E])
                         ).then_inc(small_loaded, 16)
            sp.dma_start(raw[:, 0:2 * E, :], a["L1_ffn_w1"].rearrange("e (c p) i -> p (e c) i", p=P)
                         ).then_inc(loaded[0], 16)
            sp.dma_start(raw[:, 2 * E:, :], a["L1_ffn_w2"].rearrange("e p f -> p e f")).then_inc(loaded[1], 16)

        @block.tensor
        def _(pe):
            pe.wait_ge(small_loaded, 32)
            pe.transpose(p_g[:, 0:E], raw_g[:], k.ident[0:E, 0:E]).then_inc(wg_turned, 1)
            for g in range(GROUPS):
                pe.wait_ge(loaded[g // GU_GROUPS], 16)
                at_least(pe, lo_ready, g - 3)
                for j in range(4):
                    mm = pe.transpose(p_t[g % 4][:, j, :], raw[:, 4 * g + j, :], k.ident[:])
                mm.then_inc(turned, 1)

        @block.scalar
        def _(act):
            for g in range(GROUPS):
                act.wait_ge(turned, g + 1)
                act.activation(dest(g, "hi"), p_t[g % 4][:], ACT.Copy).then_inc(hi_ready, 1)

        @block.vector
        def _(dve):
            dve.memset(ones[:], 1.0).then_inc(sel_step, 1)
            dve.tensor_reduce(sel[:], k.ident[:, 0:CP * E].rearrange("p (c e) -> p e c", e=E), AX.X, ALU.add
                              ).then_inc(sel_step, 1)
            dve.wait_ge(sel_step, 2)
            for e in range(E):
                dve.tensor_scalar(k.sel16[:, e, :], ones[:], sel[:, e:e + 1], None, ALU.mult)
            dve.wait_ge(wg_turned, 1)
            dve.tensor_copy(k.wg[:], p_g[:, 0:E])
            for g in range(GROUPS):
                dve.wait_ge(hi_ready, g + 1)
                dve.tensor_tensor(dest(g, "lo"), p_t[g % 4][:], dest(g, "hi").bitcast(F32), ALU.subtract
                                  ).then_inc(lo_ready, 1)


def router(nc, k, wsb):
    k.h_hi = wsb("h_hi", [P, B, S], F32R)
    k.h_lo = wsb("h_lo", [P, B, S], F32R)
    k.comb16 = wsb("comb16", [P, TILES_ALL, P], BF16)
    with ExitStack() as ctx:
        sb, ps, sem = tensors(nc, ctx, "router")
        ln = layer_norm_steps(nc, k, sb, sem)
        hT = [sb(f"hT{n}", [P, S]) for n in range(2)]
        logits = sb("logits", [P, TILES_ALL, E])
        top = sb("top", [P, TILES_ALL])
        shifted = sb("shifted", [P, TILES_ALL, E])
        weight = sb("weight", [P, TILES_ALL, E])
        beats = sb("beats", [P, TILES_ALL, E, E])
        rank = sb("rank", [P, TILES_ALL, E])
        total = sb("total", [P, TILES_ALL])
        rtotal = sb("rtotal", [P, TILES_ALL])
        rest = sb("rest", [P, TILES_ALL, E])
        parts = sb("parts", [P, TILES_ALL, CP, E], BF16)
        p_m = ps("p_m", [P, 512])
        p_l = ps("p_l", [P, TILES_ALL, E])
        p_c = [ps(f"p_c{n}", [P, 4, P], BF16) for n in range(2)]
        hT_ready = sem("hT_ready")
        h_hi_ready = sem("h_hi_ready")
        h_lo_ready = sem("h_lo_ready")
        logits_made = sem("logits_made")
        cleared = sem("cleared")
        step = sem("step")
        weight_ready = sem("weight_ready")
        shifted_ready = sem("shifted_ready")
        parts_ready = sem("parts_ready")
        comb_turned = sem("comb_turned")
        comb_ready = sem("comb_ready")
        block = ctx.enter_context(nc.Block())

        def walk(eng, each):
            for b in range(2):
                each(eng, b, b)
            with eng.Fori(0, (B - 4) // 2) as turn:
                for r in range(2):
                    each(eng, turn * 2 + (2 + r), r)
            for b in range(B - 2, B):
                each(eng, b, b % 2)

        @block.gpsimd
        def _(pool):
            pool.memset(k.comb16[:], 0.0).then_inc(cleared, 1)
            with pool.Fori(0, B) as b:
                ln.pool_rstd(pool, b)

        @block.tensor
        def _(pe):
            def each(pe, b, r):
                at_least(pe, h_hi_ready, b)
                ln.pe_turn(pe, b, p_m)
                pe.wait_ge(hT_ready, b + 1)
                for i in range(NT):
                    mm = pe.matmul(p_l[:, bass.ds(b * NT + i, 1), :].rearrange("p o e -> p (o e)"),
                                   hT[r][:, i * P:(i + 1) * P], k.wg[:], start=True, stop=True)
                mm.then_inc(logits_made, 1)
            walk(pe, each)
            pe.wait_ge(parts_ready, 1)
            for g in range(TILES_ALL // 4):
                at_least(pe, comb_ready, g - 1)
                for j in range(4):
                    mm = pe.transpose(p_c[g % 2][0:CP * E, j, :],
                                      parts[:, 4 * g + j].rearrange("p c e -> p (c e)"), k.ident16[:])
                mm.then_inc(comb_turned, 1)

        @block.scalar
        def _(act):
            def each(act, b, r):
                act.wait_ge(ln.xn_turned, b + 1)
                at_least(act, logits_made, b - 1)
                at_least(act, h_lo_ready, b - 1)
                scale, bias = k.mod[:, 1, CB, bass.ds(b, 1)], k.mod[:, 1, SB, bass.ds(b, 1)]
                act.activation(hT[r][:], p_m[:, 0:S], ACT.Identity, bias=bias, scale=scale).then_inc(hT_ready, 1)
                act.activation(k.h_hi[:, bass.ds(b, 1), :].rearrange("p o s -> p (o s)"), p_m[:, 0:S], ACT.Identity,
                               bias=bias, scale=scale).then_inc(h_hi_ready, 1)
            walk(act, each)
            act.wait_ge(shifted_ready, 1)
            act.activation(weight[:], shifted[:], ACT.Exp).then_inc(weight_ready, 1)
            act.wait_ge(cleared, 1)
            for g in range(TILES_ALL // 4):
                act.wait_ge(comb_turned, g + 1)
                act.activation(k.comb16[0:CP * E, 4 * g:4 * g + 4, :], p_c[g % 2][0:CP * E], ACT.Copy
                               ).then_inc(comb_ready, 1)

        @block.vector
        def _(dve):
            ln.dve_stats(dve, 0)
            ln.dve_normalise(dve, 0)

            def each(dve, b, r):
                if not isinstance(b, int) or b + 1 < B:
                    ln.dve_stats(dve, b + 1)
                dve.wait_ge(h_hi_ready, b + 1)
                dve.wait_ge(hT_ready, b + 1)
                at = bass.ds(b, 1)
                dve.tensor_tensor(k.h_lo[:, at, :].rearrange("p o s -> p (o s)"), hT[r][:],
                                  k.h_hi[:, at, :].rearrange("p o s -> p (o s)").bitcast(F32), ALU.subtract
                                  ).then_inc(h_lo_ready, 1)
                if not isinstance(b, int) or b + 1 < B:
                    ln.dve_normalise(dve, b + 1)
            walk(dve, each)

            chain = [0]

            def then(ins):
                chain[0] += 1
                ins.then_inc(step, 1)
                dve.wait_ge(step, chain[0])

            dve.wait_ge(logits_made, B)
            then(dve.tensor_tensor(logits[:], p_l[:], k.bg[:].unsqueeze(1).to_broadcast([P, TILES_ALL, E]), ALU.add))
            then(dve.tensor_reduce(top[:], logits[:], AX.X, ALU.max))
            dve.tensor_tensor(shifted[:], logits[:], top[:].unsqueeze(2).to_broadcast([P, TILES_ALL, E]), ALU.subtract
                              ).then_inc(shifted_ready, 1)
            then(dve.memset(beats[:], 0.0))
            for e in range(E):
                for lo, hi, op in ((0, e, ALU.is_ge), (e + 1, E, ALU.is_gt)):
                    if hi > lo:
                        ins = dve.tensor_tensor(beats[:, :, e, lo:hi], logits[:, :, lo:hi],
                                                logits[:, :, e:e + 1].to_broadcast([P, TILES_ALL, hi - lo]), op)
            then(ins)
            then(dve.tensor_reduce(rank[:], beats[:], AX.X, ALU.add))
            dve.wait_ge(weight_ready, 1)
            then(dve.scalar_tensor_tensor(out=weight[:], in0=rank[:], scalar=TOP - 0.5, in1=weight[:],
                                          op0=ALU.is_lt, op1=ALU.mult))
            then(dve.tensor_reduce(total[:], weight[:], AX.X, ALU.add))
            then(dve.reciprocal(rtotal[:], total[:]))
            then(dve.tensor_tensor(weight[:], weight[:], rtotal[:].unsqueeze(2).to_broadcast([P, TILES_ALL, E]), ALU.mult))
            then(dve.tensor_copy(parts[:, :, 0, :], weight[:]))
            then(dve.tensor_tensor(rest[:], weight[:], parts[:, :, 0, :], ALU.subtract))
            then(dve.tensor_copy(parts[:, :, 1, :], rest[:]))
            dve.tensor_tensor(parts[:, :, 2, :], rest[:], parts[:, :, 1, :], ALU.subtract).then_inc(parts_ready, 1)


def experts(nc, k, out):
    with ExitStack() as ctx:
        sb, ps, sem = tensors(nc, ctx, "moe")
        LAG = 3
        RING = 4
        act_g = [sb(f"act_g{n}", [P, U]) for n in range(2)]
        act_u = [sb(f"act_u{n}", [P, U]) for n in range(2)]
        z = [sb(f"z{n}", [P, U]) for n in range(RING)]
        z_hi = [sb(f"z_hi{n}", [P, U], F32R) for n in range(RING)]
        z_lo = [sb(f"z_lo{n}", [P, U], F32R) for n in range(RING)]
        yT = sb("yT", [P, U])
        p_g = [ps(f"p_g{n}", [P, U]) for n in range(2)]
        p_u = [ps(f"p_u{n}", [P, U]) for n in range(2)]
        p_c = [ps(f"p_c{n}", [P, U]) for n in range(2)]
        p_y = ps("p_y", [P, U])
        p_m = ps("p_m", [P, U])
        c_made = sem("c_made")
        gate_made = sem("gate_made")
        up_made = sem("up_made")
        silu_ready = sem("silu_ready")
        prod_ready = sem("prod_ready")
        z_ready = sem("z_ready")
        z_hi_ready = sem("z_hi_ready")
        z_lo_ready = sem("z_lo_ready")
        down_made = sem("down_made")
        yT_ready = sem("yT_ready")
        y_turned = sem("y_turned")
        x_added = sem("x_added")
        stored = sem("stored")

        def tokens(h, u):
            return h[:, bass.ds(u * 2, 2), :].rearrange("p b s -> p (b s)")

        def pe_down(pe, u, e):
            i = u * E + e
            pe.wait_ge(z_lo_ready, i + 1)
            if e == 0:
                at_least(pe, yT_ready, u)
            r = e % RING
            mm = split_product(pe, p_y[:], (k.w["dn_hi"][:, e, :], k.w["dn_lo"][:, e, :]), (z_hi[r][:], z_lo[r][:]),
                               e == 0, e == E - 1)
            mm.then_inc(down_made, 1)

        def pe_turn(pe, u):
            pe.wait_ge(yT_ready, u + 1)
            at_least(pe, x_added, u)
            for j in range(UT):
                mm = pe.transpose(p_m[:, j * P:(j + 1) * P], yT[:, j * P:(j + 1) * P], k.ident[:])
            mm.then_inc(y_turned, 1)

        def pe_unit(pe, u, first=False):
            for e in range(E):
                i = u * E + e
                at_least(pe, z_ready, i - 1)
                pe.matmul(p_c[e % 2][:], k.sel16[:, e, :],
                          k.comb16[:, bass.ds(u * UT, UT), :].rearrange("p t q -> p (t q)"), start=True, stop=True
                          ).then_inc(c_made, 1)
                for c, bank, made in ((0, p_g[e % 2], gate_made), (1, p_u[e % 2], up_made)):
                    split_product(pe, bank[:], (k.w["gu_hi"][:, e, c, :], k.w["gu_lo"][:, e, c, :]),
                                  (tokens(k.h_hi, u), tokens(k.h_lo, u)), True, True).then_inc(made, 1)
                if e >= LAG:
                    pe_down(pe, u, e - LAG)
                elif not first:
                    pe_down(pe, u - 1, E - LAG + e)
                if e == LAG + 1 and not first:
                    pe_turn(pe, u - 1)

        def act_hi(act, u, e):
            i = u * E + e
            act.wait_ge(z_ready, i + 1)
            at_least(act, down_made, i - RING + 1)
            act.activation(z_hi[e % RING][:], z[e % RING][:], ACT.Copy).then_inc(z_hi_ready, 1)

        def act_y(act, u):
            act.wait_ge(down_made, (u + 1) * E)
            at_least(act, y_turned, u)
            for c in range(2):
                ins = act.activation(yT[:, c * S:(c + 1) * S], p_y[:, c * S:(c + 1) * S], ACT.Copy,
                                     scale=k.mod[:, 1, GB, bass.ds(u * 2 + c, 1)])
            ins.then_inc(yT_ready, 1)

        def act_unit(act, u, first=False):
            for e in range(E):
                i = u * E + e
                act.wait_ge(gate_made, i + 1)
                at_least(act, prod_ready, i - 1)
                act.activation(act_g[e % 2][:], p_g[e % 2][:], ACT.Silu).then_inc(silu_ready, 1)
                if e >= 1:
                    act_hi(act, u, e - 1)
                elif not first:
                    act_hi(act, u - 1, E - 1)
                if e == LAG and not first:
                    act_y(act, u - 1)

        def dve_add(dve, u):
            dve.wait_ge(y_turned, u + 1)
            x = k.X[:, bass.ds(u * UT, UT), :]
            dve.tensor_tensor(x, x, p_m[:].rearrange("p (t d) -> p t d", t=UT), ALU.add).then_inc(x_added, 1)

        def dve_unit(dve, u, first=False):
            for e in range(E):
                i = u * E + e
                dve.wait_ge(silu_ready, i + 1)
                dve.wait_ge(up_made, i + 1)
                dve.tensor_tensor(act_u[e % 2][:], act_g[e % 2][:], p_u[e % 2][:], ALU.mult).then_inc(prod_ready, 1)
                dve.wait_ge(prod_ready, i + 1)
                dve.wait_ge(c_made, i + 1)
                at_least(dve, z_lo_ready, i - RING + 1)
                dve.tensor_tensor(z[e % RING][:], act_u[e % 2][:], p_c[e % 2][:], ALU.mult).then_inc(z_ready, 1)
                if e == LAG + 2 and not first:
                    dve_add(dve, u - 1)

        def pool_unit(pool, u):
            for e in range(E):
                i = u * E + e
                pool.wait_ge(z_hi_ready, i + 1)
                at_least(pool, down_made, i - RING + 1)
                pool.tensor_tensor(z_lo[e % RING][:], z[e % RING][:], z_hi[e % RING][:].bitcast(F32), ALU.subtract
                                   ).then_inc(z_lo_ready, 1)

        x_out = out.rearrange("b (i p) d -> p (b i) d", p=P)
        block = ctx.enter_context(nc.Block())

        @block.gpsimd
        def _(pool):
            pool_unit(pool, 0)
            with pool.Fori(1, UNITS) as u:
                pool_unit(pool, u)

        @block.tensor
        def _(pe):
            pe_unit(pe, 0, first=True)
            with pe.Fori(1, UNITS) as u:
                pe_unit(pe, u)
            for e in range(E - LAG, E):
                pe_down(pe, UNITS - 1, e)
            pe_turn(pe, UNITS - 1)

        @block.scalar
        def _(act):
            act_unit(act, 0, first=True)
            with act.Fori(1, UNITS) as u:
                act_unit(act, u)
            act_hi(act, UNITS - 1, E - 1)
            act_y(act, UNITS - 1)

        @block.vector
        def _(dve):
            dve_unit(dve, 0, first=True)
            with dve.Fori(1, UNITS) as u:
                dve_unit(dve, u)
            dve_add(dve, UNITS - 1)

        @block.sync
        def _(sp):
            with sp.Fori(0, UNITS) as u:
                sp.wait_ge(x_added, u + 1)
                at = bass.ds(u * UT, UT)
                sp.dma_start(x_out[:, at, :], k.X[:, at, :]).then_inc(stored, 16)
            sp.wait_ge(stored, 16 * UNITS)


def build(nc, a, out):
    k = Names()
    k.w = {}
    with ExitStack() as ctx:
        sb, ps, sem = tensors(nc, ctx, "top")
        k.X = sb("X", [P, B * NT, D])
        k.ident = sb("ident", [P, P])
        k.ident16 = sb("ident16", [P, P], BF16)
        k.minus_half = sb("minus_half", [P, 8])
        k.parity = sb("parity", [P, 2])
        k.mod = sb("mod", [P, 2, 6, B])
        k.wq0, k.wk0, k.wv0, k.wo0 = (sb(f"w{x}0", [P, D]) for x in "qkvo")
        k.bq0, k.bk0, k.bo0 = (sb(f"b{x}0", [P, 1]) for x in "qko")
        k.gbo0 = sb("gbo0", [P, B])
        k.ffn_scales = sb("ffn_scales", [P, 4, FB])
        k.ab_scale = sb("ab_scale", [P, FB])
        k.half_s1 = sb("half_s1", [P, FB])
        k.w3_scale = sb("w3_scale", [P, 1])
        k.w3_gate = sb("w3_gate", [P, B])
        k.x_loaded = sem("x_loaded")
        k.waits_passed = sem("waits_passed")
        with ExitStack() as phase:
            wsb, _, _ = tensors(nc, phase, "att0p")
            k.Q = [wsb(f"Q{n}", [P, H0, S], BF16) for n in range(NB)]
            k.K = [wsb(f"K{n}", [P, PAIRS, S], BF16) for n in range(NB)]
            k.V = [wsb(f"V{n}", [P, NT, H0, 32]) for n in range(NB)]
            prepare(nc, k, a)
            attention0(nc, k)
        with ExitStack() as phase:
            wsb, _, _ = tensors(nc, phase, "ffn0")
            ffn_weights(nc, k, a, wsb)
            ffn0(nc, k)
        with ExitStack() as phase:
            wsb, _, _ = tensors(nc, phase, "att1p")
            attention1_weights(nc, k, a, wsb)
            attention1(nc, k)
        with ExitStack() as phase:
            wsb, _, _ = tensors(nc, phase, "moep")
            moe_weights(nc, k, a, wsb)
            router(nc, k, wsb)
            experts(nc, k, out)


_INS = [
    "L0_attn_x", "L0_attn_Wq", "L0_attn_bq", "L0_attn_Wl", "L0_attn_bl", "L0_attn_Wk", "L0_attn_bk", "L0_attn_Wv",
    "L0_attn_bv", "L0_attn_Wo", "L0_attn_bo", "L0_ffn_w1_w", "L0_ffn_w1_s", "L0_ffn_w2_w", "L0_ffn_w2_s",
    "L0_ffn_h1_w", "L0_ffn_h1_s", "L0_ffn_h2_w", "L0_ffn_h2_s", "L0_ffn_w3_w", "L0_ffn_w3_s", "L0_c", "L0_wmod",
    "L1_attn_Wq", "L1_attn_Wk", "L1_attn_Wv", "L1_attn_Wo", "L1_attn_bo", "L1_attn_betas", "L1_attn_mem",
    "L1_attn_z", "L1_ffn_Wg", "L1_ffn_bg", "L1_ffn_w1", "L1_ffn_w2", "L1_c", "L1_wmod",
]


def kernel(**inputs):
    import numpy as np
    import concourse.bacc as bacc
    from concourse.bass_utils import run_bass_kernel_spmd

    nc = bacc.Bacc("TRN2", target_bir_lowering=False, num_devices=1)
    arrays, aps = {}, {}
    for name in _INS:
        array = np.ascontiguousarray(inputs[name])
        arrays[f"in_{name}"] = array
        aps[name] = nc.dram_tensor(f"in_{name}", array.shape, mybir.dt.from_np(array.dtype), kind="ExternalInput").ap()
    out = nc.dram_tensor("out_x", (B, S, D), F32, kind="ExternalOutput").ap()
    build(nc, aps, out)
    result = run_bass_kernel_spmd(nc, [arrays], core_ids=[0])
    return result.results[0]["out_x"]
```

```python
from contextlib import ExitStack

import concourse.bass as bass
from concourse import mybir

F32 = mybir.dt.float32
F32R = mybir.dt.float32r
BF16 = mybir.dt.bfloat16
ALU = mybir.AluOpType
ACT = mybir.ActivationFunctionType
AX = mybir.AxisListType

P = 128
B = 16
S = 256
D = 128
NT = S // P
EPS = 1e-5
SA, CA, GA, SB, CB, GB = range(6)

H0 = 16
DH0 = D // H0
LAT = D // 4
SCALE0 = DH0 ** -0.5
PAIRS = H0 // 2
HROWS = P // 2
TERMS = [(0, 0), (0, 1), (0, 2), (1, 0), (1, 1), (2, 0)]
TROWS = 2 * DH0
NB = 4
MAXROW = len(TERMS) * TROWS
PES = {"ln": 0, "max_turn": 1, "qk": 3, "O0": 5, "v": 8, "O1": 9, "back": 11, "out": 12, "turn_y": 14,
       "pv_s": (11, 15), "pv_t": (3, 7)}
DVE = {"negmax": 0, "stats": 2, "parts": 6, "O0": 6, "parts2": 10, "normalise": 11, "O1": 10, "add": 15}
ACTS = {"hT": 0, "maxT": 0, "qk": 3, "part1": 7, "v": 7, "OTn": 11, "y": 12, "OT_s": (11, 15), "OT_t": (3, 6)}

F = 512
FB = F // P
FFN_PLAN = [("w1", FB, 1, 0), ("w2", FB, 1, FB), ("h1", FB, FB, 2 * FB), ("h2", FB, FB, 2 * FB + FB * FB),
            ("w3", 1, FB, 2 * FB + 2 * FB * FB)]
FFN_BLOCKS = 2 * FB + 2 * FB * FB + FB
H1 = 4
DH1 = D // H1
E = 8
TOP = 2
CP = 3
TILES_ALL = B * NT
EARLY = 12
MOE_GU_GROUPS = 2 * E // 4
LATE_LOADS = 32
LATE_LOADED = 16 * LATE_LOADS
X_LOADS = 4
X_LOADED = 16 * X_LOADS


class Names:
    pass


def batch_valid(b):
    return not isinstance(b, int) or 0 <= b < B


def at_least(eng, sem, value):
    if isinstance(value, int) and value <= 0:
        return
    eng.wait_ge(sem, value)


def wait_apart(eng, k, sem, value):
    eng.wait_ge(sem, value)
    eng.sem_inc(k.waits_passed, 1)


def tensors(nc, ctx, tag):
    def sb(name, shape, dt=F32):
        return ctx.enter_context(nc.sbuf_tensor(f"{tag}_{name}", shape, dt))

    def ps(name, shape, dt=F32):
        return ctx.enter_context(nc.psum_tensor(f"{tag}_{name}", shape, dt))

    mine = []

    def clear():
        if mine:
            nc.clear_and_free_semaphores(mine)
            nc.all_engine_barrier()

    ctx.callback(clear)

    def sem(name):
        mine.append(nc.alloc_semaphore(f"{tag}_s_{name}"))
        return mine[-1]

    return sb, ps, sem


def prepare(nc, k, a):
    with ExitStack() as ctx:
        sb, ps, sem = tensors(nc, ctx, "prep")
        c_nat = sb("c_nat", [B, 2, D])
        wmod = sb("wmod", [P, 2, 6 * D])
        wl = sb("wl", [P, LAT])
        wk = sb("wk", [LAT, D])
        wv = sb("wv", [LAT, D])
        wq = sb("wq", [P, D])
        lat_bias = sb("lat_bias", [LAT, 1])
        cols = sb("cols", [P, 4])
        tanh_c = sb("tanh_c", [P, 2 * B])
        half_c = sb("half_c", [P, 2 * B])
        silu_c = sb("silu_c", [P, 2 * B])
        wlT = sb("wlT", [LAT, P])
        wk_perm = sb("wk_perm", [LAT, D])
        bv_col = sb("bv_col", [P, 1])
        gate_sign = sb("gate_sign", [P, 2, 2, B])
        gate_abs = sb("gate_abs", [P, 2, 2, B])

        p_c = ps("p_c", [P, 512])
        p_mod = ps("p_mod", [P, 512])
        p_w = ps("p_w", [P, 512])
        p_v = ps("p_v", [P, 512])
        p_b = ps("p_b", [P, 512])

        zeroed = sem("zeroed")
        ident_ready = sem("ident_ready")
        small_loaded = sem("small_loaded")
        wmod_loaded = sem("wmod_loaded")
        c_turned = sem("c_turned")
        c_tanh = sem("c_tanh")
        c_half = sem("c_half")
        c_silu = sem("c_silu")
        wl_turned = sem("wl_turned")
        wlT_ready = sem("wlT_ready")
        perm_ready = sem("perm_ready")
        w_made = sem("w_made")
        mod_made = sem("mod_made")
        bias_made = sem("bias_made")
        bv_ready = sem("bv_ready")
        bo_made = sem("bo_made")
        gate_step = sem("gate_step")

        x_view = a["L0_attn_x"].rearrange("b (i p) d -> p (b i) d", p=P)

        block = ctx.enter_context(nc.Block())

        @block.sync
        def _(sp):
            loads = [
                (c_nat[:, 0, :], a["L0_c"]), (c_nat[:, 1, :], a["L1_c"]),
                (wl[:], a["L0_attn_Wl"]), (wk[:], a["L0_attn_Wk"]), (wv[:], a["L0_attn_Wv"]),
                (wq[:], a["L0_attn_Wq"]), (k.wo0[:], a["L0_attn_Wo"]),
                (lat_bias[:], a["L0_attn_bl"].rearrange("(l o) -> l o", o=1)),
            ]
            for to, of in loads:
                sp.dma_start(to, of).then_inc(small_loaded, 16)
            for half in range(2):
                rows = slice(half * HROWS, (half + 1) * HROWS)
                for n, name in enumerate(("L0_attn_bq", "L0_attn_bk")):
                    sp.dma_start(cols[rows, n:n + 1],
                                 a[name].rearrange("(g w d o) -> w d g o", w=2, d=DH0, o=1)[half],
                                 allow_slow_non_contiguous=True).then_inc(small_loaded, 16)
            for n, name in ((2, "L0_attn_bv"), (3, "L0_attn_bo")):
                sp.dma_start(cols[:, n:n + 1], a[name].rearrange("(d o) -> d o", o=1)).then_inc(small_loaded, 16)
            for n, name in enumerate(("L0_wmod", "L1_wmod")):
                sp.dma_start(wmod[:, n, :], a[name]).then_inc(wmod_loaded, 16)
            per = B * NT // X_LOADS
            for n in range(X_LOADS):
                part = slice(n * per, (n + 1) * per)
                sp.dma_start(k.X[:, part, :], x_view[:, part, :]).then_inc(k.x_loaded, 16)
            sp.wait_ge(k.x_loaded, X_LOADED)

        SMALL = 16 * 14

        @block.gpsimd
        def _(pool):
            pool.memset(k.ident[:], 0.0).then_inc(zeroed, 1)
            pool.wait_ge(zeroed, 1)
            pool.affine_select(out=k.ident[:], in_=k.ident[:], compare_op=ALU.not_equal, fill=1.0, base=0,
                               pattern=[[-1, P]], channel_multiplier=1).then_inc(ident_ready, 1)
            pool.wait_ge(ident_ready, 1)
            pool.tensor_copy(k.ident16[:], k.ident[:]).then_inc(ident_ready, 1)
            pool.memset(k.minus_half[:], -0.5)
            pool.memset(k.memz[:], 0.0)
            for r in range(NB):
                pool.memset(k.V[r][:, :, :, DH0 + 1:], 0.0)
                if r >= 2:
                    pool.memset(k.Q[r][:], 0.0)
                    pool.memset(k.K[r][:], 1.0)

        @block.tensor
        def _(pe):
            pe.wait_ge(ident_ready, 1)
            pe.wait_ge(small_loaded, SMALL)
            for n in range(2):
                mm = pe.transpose(p_c[:, n * B:(n + 1) * B], c_nat[:, n, :], k.ident[0:B, 0:B])
            mm.then_inc(c_turned, 1)
            pe.transpose(p_w[0:LAT, 0:P], wl[:], k.ident[:]).then_inc(wl_turned, 1)
            pe.wait_ge(wlT_ready, 1)
            pe.wait_ge(perm_ready, 2)
            pe.matmul(p_v[:, 0:D], wlT[:], wk_perm[:], start=True, stop=True)
            pe.matmul(p_v[:, D:2 * D], wlT[:], wv[:], start=True, stop=True).then_inc(w_made, 1)
            pe.matmul(p_b[:, 0:1], wk_perm[:], lat_bias[:], start=True, stop=True)
            pe.matmul(p_b[:, 1:2], wv[:], lat_bias[:], start=True, stop=True).then_inc(bias_made, 1)
            pe.wait_ge(c_silu, 1)
            pe.wait_ge(wmod_loaded, 32)
            for n in range(2):
                for j in range(6):
                    at = (n * 6 + j) * B
                    mm = pe.matmul(p_mod[:, at:at + B], wmod[:, n, j * D:(j + 1) * D],
                                   silu_c[:, n * B:(n + 1) * B], start=True, stop=True)
            mm.then_inc(mod_made, 1)
            pe.wait_ge(bv_ready, 1)
            pe.matmul(p_c[:, 0:1], k.wo0[:], bv_col[:], start=True, stop=True).then_inc(bo_made, 1)

        @block.scalar
        def _(act):
            act.wait_ge(c_turned, 1)
            act.activation(tanh_c[:], p_c[:, 0:2 * B], ACT.Tanh, scale=0.5).then_inc(c_tanh, 1)

        @block.vector
        def _(dve):
            for r in range(NB):
                dve.memset(k.V[r][:, :, :, DH0:DH0 + 1], 1.0)
                if r < 2:
                    dve.memset(k.Q[r][:], 0.0)
                    dve.memset(k.K[r][:], 1.0)
            dve.wait_ge(small_loaded, SMALL)
            dve.wait_ge(ident_ready, 1)
            dve.tensor_reduce(k.parity[:], k.ident[:].rearrange("p (t w d) -> p w t d", w=2, d=DH0), AX.XY, ALU.add)
            for to, of in ((k.wq0[:], wq[:]), (wk_perm[:], wk[:])):
                dve.tensor_copy(to.rearrange("p (w d g) -> p w d g", w=2, d=DH0),
                                of.rearrange("p (g w d) -> p w d g", w=2, d=DH0)).then_inc(perm_ready, 1)
            dve.wait_ge(wl_turned, 1)
            dve.tensor_copy(wlT[:], p_w[0:LAT, 0:P]).then_inc(wlT_ready, 1)
            dve.wait_ge(c_tanh, 1)
            dve.tensor_scalar(half_c[:], p_c[:, 0:2 * B], 0.5, None, ALU.mult).then_inc(c_half, 1)
            dve.wait_ge(c_half, 1)
            dve.scalar_tensor_tensor(out=silu_c[:], in0=tanh_c[:], scalar=1.0, in1=half_c[:],
                                     op0=ALU.add, op1=ALU.mult).then_inc(c_silu, 1)
            dve.wait_ge(w_made, 1)
            dve.tensor_copy(k.wk0[:], p_v[:, 0:D])
            dve.tensor_copy(k.wv0[:], p_v[:, D:2 * D])
            dve.wait_ge(bias_made, 1)
            dve.tensor_scalar(k.bq0[:], cols[:, 0:1], SCALE0, None, ALU.mult)
            dve.tensor_tensor(k.bk0[:], p_b[:, 0:1], cols[:, 1:2], ALU.add)
            dve.tensor_tensor(bv_col[:], p_b[:, 1:2], cols[:, 2:3], ALU.add).then_inc(bv_ready, 1)
            dve.wait_ge(bo_made, 1)
            dve.tensor_tensor(k.bo0[:], p_c[:, 0:1], cols[:, 3:4], ALU.add).then_inc(gate_step, 1)
            dve.wait_ge(mod_made, 1)
            dve.tensor_copy(k.mod[:], p_mod[:, 0:2 * 6 * B].rearrange("p (n j b) -> p n j b", n=2, j=6)).then_inc(gate_step, 1)
            dve.wait_ge(gate_step, 2)
            one_plus = k.mod[:, :, CA::CB - CA, :]
            dve.tensor_scalar(one_plus, one_plus, 1.0, None, ALU.add)
            g = k.mod[:, :, GA::GB - GA, :]
            dve.tensor_scalar(gate_sign[:], g, 0.0, 2.0, ALU.is_ge, ALU.mult)
            dve.scalar_tensor_tensor(out=gate_abs[:], in0=g, scalar=-1.0, in1=g, op0=ALU.mult, op1=ALU.max
                                     ).then_inc(gate_step, 1)
            dve.wait_ge(gate_step, 3)
            dve.tensor_scalar(gate_abs[:], gate_abs[:], 0.25, None, ALU.max).then_inc(gate_step, 1)
            dve.wait_ge(gate_step, 4)
            dve.scalar_tensor_tensor(out=g, in0=gate_sign[:], scalar=-1.0, in1=gate_abs[:],
                                     op0=ALU.add, op1=ALU.mult).then_inc(gate_step, 1)
            dve.wait_ge(gate_step, 5)
            dve.tensor_scalar(k.gbo0[:], k.mod[:, 0, GA, :], k.bo0[:, 0:1], None, ALU.mult)


def late_loads(k, a):
    loads = []
    for name, ob, ib, at in FFN_PLAN:
        loads.append((k.raw_ffn[:, at:at + ob * ib, :].rearrange("p (o i) d -> p o (i d)", o=ob),
                      a[f"L0_ffn_{name}_w"].rearrange("(o p) i -> p o i", p=P)))
    loads.append((k.raw_moe[:, 0:2 * E, :], a["L1_ffn_w1"].rearrange("e (c p) i -> p (e c) i", p=P)))
    loads.append((k.raw_moe[:, 2 * E:, :], a["L1_ffn_w2"].rearrange("e p f -> p e f")))
    for n, name in enumerate(("w1", "w2", "h1", "h2")):
        loads.append((k.ffn_scales[:, n, :], a[f"L0_ffn_{name}_s"].rearrange("(m p) -> p m", p=P)))
    loads.append((k.w3_scale[:], a["L0_ffn_w3_s"].rearrange("(p o) -> p o", o=1)))
    for n, name in enumerate(("Wq", "Wk", "Wv", "Wo")):
        loads.append((k.raw_att1[:, n, :], a[f"L1_attn_{name}"]))
    loads.append((k.bo1[:], a["L1_attn_bo"].rearrange("(d o) -> d o", o=1)))
    for h in range(H1):
        rows = slice(h * DH1, (h + 1) * DH1)
        loads.append((k.beta[rows, 0:1], a["L1_attn_betas"][0, h].to_broadcast([DH1, 1])))
        loads.append((k.memz[rows, rows], a["L1_attn_mem"][h]))
        loads.append((k.memz[rows, D + h:D + h + 1], a["L1_attn_z"][h]))
    loads.append((k.beta[:, 1:], a["L1_attn_betas"].rearrange("a h b c -> a (h b c)").to_broadcast([P, H1])))
    loads.append((k.raw_g[:], a["L1_ffn_Wg"]))
    loads.append((k.bg[:], a["L1_ffn_bg"].rearrange("(o e) -> o e", o=1).to_broadcast([P, E])))
    return loads


def attention0(nc, k, a):
    with ExitStack() as ctx:
        sb, ps, sem = tensors(nc, ctx, "att0")
        Q, K, V = k.Q, k.K, k.V
        stats = sb("stats", [P, NT, 6])
        meanvar = sb("meanvar", [P, NT, 2])
        var_eps = sb("var_eps", [P, NT])
        rstd = sb("rstd", [P, NT])
        xn = sb("xn", [P, NT, D])
        hT = sb("hT", [P, S])
        qk = sb("qk", [P, 2, S])
        rest = sb("rest", [P, 2, S])
        parts = [sb(f"parts{n}", [P, 3, 2, S], BF16) for n in range(2)]
        Qall = [sb(f"Qall{n}", [P, PAIRS, S], BF16) for n in range(2)]
        rowmax = sb("rowmax", [P, NT, PAIRS, 2])
        negmax = sb("negmax", [P, NT, 2, PAIRS])
        negrest = sb("negrest", [P, NT, 2, PAIRS])
        negparts = sb("negparts", [P, NT, 2, 3, PAIRS], BF16)
        maxT = sb("maxT", [2 * 3 * PAIRS, S], BF16)
        probs = [sb(f"probs{n}", [P, 2, 2, NT, S]) for n in range(2)]
        OT = [sb(f"OT{n}", [P, S]) for n in range(4)]
        recip = sb("recip", [P, 2, NT, 4])
        O = sb("O", [P, NT, H0, DH0])
        OTn = sb("OTn", [P, S])
        yT = sb("yT", [P, S])

        p_max = [ps(f"p_max{n}", [P, 2, S]) for n in range(2)]
        p_sT = [ps(f"p_sT{n}", [P, 2, NT, S]) for n in range(2)]
        p_o = ps("p_o", [P, 512])
        p_m = ps("p_m", [P, 512])
        p_m16 = p_m[:].bitcast(BF16)

        stats_step = sem("stats_step")
        var_ready = sem("var_ready")
        rstd_ready = sem("rstd_ready")
        xn_ready = sem("xn_ready")
        xn_turned = sem("xn_turned")
        hT_ready = sem("hT_ready")
        qk_made = sem("qk_made")
        qk_ready = sem("qk_ready")
        part0_ready = sem("part0_ready")
        rest_ready = sem("rest_ready")
        part1_ready = sem("part1_ready")
        part2_ready = sem("part2_ready")
        v_made = sem("v_made")
        v_ready = sem("v_ready")
        stacked = sem("stacked")
        Q_ready = sem("Q_ready")
        scored = sem("scored")
        maxed = sem("maxed")
        negmax_ready = sem("negmax_ready")
        neg_step = sem("neg_step")
        neg_ready = sem("neg_ready")
        max_turned = sem("max_turned")
        maxT_ready = sem("maxT_ready")
        max_stacked = sem("max_stacked")
        scoredT = sem("scoredT")
        exped = sem("exped")
        pv_made = sem("pv_made")
        OT_ready = sem("OT_ready")
        O_turned = sem("O_turned")
        recip_ready = sem("recip_ready")
        O_ready = sem("O_ready")
        OTn_turned = sem("OTn_turned")
        OTn_ready = sem("OTn_ready")
        y_made = sem("y_made")
        yT_ready = sem("yT_ready")
        y_turned = sem("y_turned")
        x_added = sem("x_added")

        TILES = 2 * PAIRS
        STACK_DMAS = 2 * len(TERMS)

        def pe_ln(pe, b):
            pe.wait_ge(xn_ready, b + 1)
            at_least(pe, v_ready, b)
            at_least(pe, x_added, b - 4)
            for i in range(NT):
                mm = pe.transpose(p_m[:, i * P:(i + 1) * P], xn[:, i, :], k.ident[:])
            mm.then_inc(xn_turned, 1)

        def pe_qk(pe, b):
            pe.wait_ge(hT_ready, b + 1)
            at_least(pe, maxT_ready, b - 2)
            pe.matmul(p_m[:, 0:S], k.wq0[:], hT[:], start=True, stop=True)
            pe.matmul(p_m[:, S:2 * S], k.wk0[:], hT[:], start=True, stop=True).then_inc(qk_made, 1)

        def pe_v(pe, b):
            pe.wait_ge(qk_ready, b + 1)
            at_least(pe, O_ready, 2 * (b - 4) + 1)
            for i in range(NT):
                mm = pe.matmul(p_m[:, i * D:(i + 1) * D], hT[:, i * P:(i + 1) * P], k.wv0[:], start=True, stop=True)
            mm.then_inc(v_made, 1)

        def pe_max_tile(pe, b, r, t):
            if t == 0:
                pe.wait_ge(stacked, 16 * STACK_DMAS * (b + 1))
                pe.wait_ge(Q_ready, b + 1)
            at_least(pe, maxed, TILES * b + t - 1)
            pair, i = t // NT, t % NT
            for w in range(2):
                mm = pe.matmul(p_max[t % 2][:, w, :], Q[r][0:MAXROW, 2 * pair + w, i * P:(i + 1) * P],
                               K[r][0:MAXROW, pair, :],
                               start=True, stop=True)
            mm.then_inc(scored, 1)

        def pe_max_turn(pe, b):
            pe.wait_ge(neg_ready, b + 1)
            if not isinstance(b, int) or b + 3 < B:
                wait_apart(pe, k, hT_ready, b + 4)
            else:
                at_least(pe, x_added, b - 1)
            for i in range(NT):
                mm = pe.transpose(p_m16[0:6 * PAIRS, i * P:(i + 1) * P],
                                  negparts[:, i].rearrange("p w t g -> p (w t g)"), k.ident16[:])
            mm.then_inc(max_turned, 1)

        def pe_scoreT(pe, b, r, t):
            if t == 0:
                pe.wait_ge(max_stacked, 32 * (b + 1))
            at_least(pe, exped, PAIRS * b + t - 1)
            for w in range(2):
                for j in range(NT):
                    mm = pe.matmul(p_sT[t % 2][:, w, j, :], K[r][:, t, j * P:(j + 1) * P], Q[r][:, 2 * t + w, :],
                                   start=True, stop=True)
            mm.then_inc(scoredT, 1)

        def pe_pv(pe, b, r, g):
            if g == 0:
                pe.wait_ge(v_ready, b + 1)
            pe.wait_ge(exped, PAIRS * b + 2 * g + 2)
            at_least(pe, OT_ready, 4 * b + g)
            for j in range(NT):
                for h in range(4):
                    mm = pe.matmul(p_o[32 * h:32 * h + 32, 0:S], V[r][:, j, 4 * g + h, :],
                                   probs[g % 2][:, h // 2, h % 2, j, :], start=(j == 0), stop=(j == NT - 1))
            mm.then_inc(pv_made, 1)

        def pe_turn_O(pe, b, u, p_m_free):
            p_m_free()
            pe.wait_ge(OT_ready, 4 * b + 2 * u + 2)
            for g in range(2):
                for i in range(NT):
                    at = (g * NT + i) * P
                    mm = pe.transpose(p_m[:, at:at + P], OT[2 * u + g][:, i * P:(i + 1) * P], k.ident[:])
            mm.then_inc(O_turned, 1)

        def pe_turn_back(pe, b):
            pe.wait_ge(O_ready, 2 * b + 2)
            for i in range(NT):
                mm = pe.transpose(p_m[:, i * P:(i + 1) * P], O[:, i].rearrange("p h d -> p (h d)"), k.ident[:])
            mm.then_inc(OTn_turned, 1)

        def pe_out(pe, b):
            pe.wait_ge(OTn_ready, b + 1)
            pe.matmul(p_m[:, 0:S], k.wo0[:], OTn[:], start=True, stop=True).then_inc(y_made, 1)

        def pe_turn_y(pe, b):
            pe.wait_ge(yT_ready, b + 1)
            for i in range(NT):
                mm = pe.transpose(p_m[:, i * P:(i + 1) * P], yT[:, i * P:(i + 1) * P], k.ident[:])
            mm.then_inc(y_turned, 1)

        def pe_step(pe, n, r):
            f, m, s, t = n, n - 2, n - 3, n - 4
            rm, rs, rt = (r - 2) % NB, (r - 3) % NB, r
            for slot in range(TILES):
                if slot == PES["ln"] and batch_valid(f):
                    pe_ln(pe, f)
                if slot == PES["max_turn"] and batch_valid(s):
                    pe_max_turn(pe, s)
                if slot == PES["qk"] and batch_valid(f):
                    pe_qk(pe, f)
                if slot == PES["v"] and batch_valid(f):
                    pe_v(pe, f)
                if batch_valid(m):
                    pe_max_tile(pe, m, rm, slot)
                if slot >= 6 and slot % 2 == 0 and batch_valid(s):
                    pe_scoreT(pe, s, rs, (slot - 6) // 2)
                if slot in (0, 2, 4) and batch_valid(t):
                    pe_scoreT(pe, t, rt, 5 + slot // 2)
                if slot in PES["pv_s"] and batch_valid(s):
                    pe_pv(pe, s, rs, PES["pv_s"].index(slot))
                if slot in PES["pv_t"] and batch_valid(t):
                    pe_pv(pe, t, rt, 2 + PES["pv_t"].index(slot))
                if slot == PES["O0"] and batch_valid(t):
                    def after_qk():
                        if batch_valid(f):
                            pe.wait_ge(qk_ready, f + 1)
                        elif batch_valid(s):
                            pe.wait_ge(maxT_ready, s + 1)
                        at_least(pe, x_added, t)
                    pe_turn_O(pe, t, 0, after_qk)
                if slot == PES["O1"] and batch_valid(t):
                    def after_v():
                        if batch_valid(f):
                            pe.wait_ge(v_ready, f + 1)
                        pe.wait_ge(O_ready, 2 * t + 1)
                    pe_turn_O(pe, t, 1, after_v)
                if slot == PES["back"] and batch_valid(t):
                    pe_turn_back(pe, t)
                if slot == PES["out"] and batch_valid(t):
                    pe_out(pe, t)
                if slot == PES["turn_y"] and batch_valid(t):
                    pe_turn_y(pe, t)

        def dve_stats(dve, b):
            at_least(dve, xn_ready, b)
            for i in range(NT):
                dve.bn_stats(stats[:, i, :], k.X[:, bass.ds(b * NT + i, 1), :]).then_inc(stats_step, 1)
            wait_apart(dve, k, stats_step, 3 * b + 2)
            for i in range(NT):
                ins = dve.bn_aggr(meanvar[:, i, :], stats[:, i, :])
            ins.then_inc(stats_step, 1)
            dve.wait_ge(stats_step, 3 * b + 3)
            at_least(dve, rstd_ready, b)
            dve.tensor_scalar(var_eps[:], meanvar[:, :, 1], EPS, None, ALU.add).then_inc(var_ready, 1)

        def dve_normalise(dve, b):
            dve.wait_ge(rstd_ready, b + 1)
            at_least(dve, xn_turned, b)
            for i in range(NT):
                ins = dve.tensor_scalar(xn[:, i, :], k.X[:, bass.ds(b * NT + i, 1), :].rearrange("p o d -> p (o d)"),
                                        meanvar[:, i, 0:1], rstd[:, i:i + 1], ALU.subtract, ALU.mult)
            ins.then_inc(xn_ready, 1)

        def dve_parts(dve, b, r):
            dve.wait_ge(part0_ready, b + 1)
            dve.tensor_tensor(rest[:], qk[:], parts[r % 2][:, 0], ALU.subtract).then_inc(rest_ready, 1)

        def dve_parts2(dve, b, r):
            dve.wait_ge(part1_ready, b + 1)
            dve.tensor_tensor(parts[r % 2][:, 2], rest[:], parts[r % 2][:, 1], ALU.subtract).then_inc(part2_ready, 1)

        def dve_max_tile(dve, b, t):
            pair, i = t // NT, t % NT
            if t == 0:
                at_least(dve, negmax_ready, b)
            dve.wait_ge(scored, TILES * b + t + 1)
            dve.tensor_reduce(rowmax[:, i, pair, :], p_max[t % 2][:], AX.X, ALU.max).then_inc(maxed, 1)

        def dve_negmax(dve, b):
            dve.wait_ge(maxed, TILES * (b + 1))
            dve.tensor_scalar(negmax[:].rearrange("p i w g -> p i g w"), rowmax[:], -1.0, None, ALU.mult
                              ).then_inc(negmax_ready, 1)
            dve.wait_ge(negmax_ready, b + 1)
            at_least(dve, max_turned, b)
            dve.tensor_copy(negparts[:, :, :, 0, :], negmax[:]).then_inc(neg_step, 1)
            dve.wait_ge(neg_step, 3 * b + 1)
            dve.tensor_tensor(negrest[:], negmax[:], negparts[:, :, :, 0, :], ALU.subtract).then_inc(neg_step, 1)
            dve.wait_ge(neg_step, 3 * b + 2)
            dve.tensor_copy(negparts[:, :, :, 1, :], negrest[:]).then_inc(neg_step, 1)
            dve.wait_ge(neg_step, 3 * b + 3)
            dve.tensor_tensor(negparts[:, :, :, 2, :], negrest[:], negparts[:, :, :, 1, :], ALU.subtract
                              ).then_inc(neg_ready, 1)

        def dve_normalise_O(dve, b, u):
            dve.wait_ge(O_turned, 2 * b + u + 1)
            if u == 0:
                at_least(dve, OTn_turned, b)
            heads = p_m[:].rearrange("p (g i h c) -> p g i h c", g=2, i=NT, h=4)
            at_least(dve, O_ready, 2 * b + u)
            dve.reciprocal(recip[:].rearrange("p g i h -> p (g i h)"),
                           p_m[:].rearrange("p (n c) -> p n c", c=32)[:, :, DH0]).then_inc(recip_ready, 1)
            dve.wait_ge(recip_ready, 2 * b + u + 1)
            for i in range(NT):
                ins = dve.tensor_tensor(O[:, i, 8 * u:8 * u + 8, :].rearrange("p (g h) d -> p g h d", g=2),
                                        heads[:, :, i, :, 0:DH0],
                                        recip[:, :, i, :].unsqueeze(3).to_broadcast([P, 2, 4, DH0]), ALU.mult)
            ins.then_inc(O_ready, 1)

        def dve_add(dve, b):
            dve.wait_ge(y_turned, b + 1)
            x = k.X[:, bass.ds(b * NT, NT), :]
            dve.tensor_tensor(x, x, p_m[:, 0:S].rearrange("p (i d) -> p i d", i=NT), ALU.add).then_inc(x_added, 1)

        def dve_step(dve, n, r):
            f, m, s, t = n, n - 2, n - 3, n - 4
            for slot in range(TILES):
                if slot == DVE["negmax"] and batch_valid(s):
                    dve_negmax(dve, s)
                if slot == DVE["O0"] and batch_valid(t):
                    dve_normalise_O(dve, t, 0)
                if slot == DVE["O1"] and batch_valid(t):
                    dve_normalise_O(dve, t, 1)
                if slot == DVE["parts"] and batch_valid(f):
                    dve_parts(dve, f, r)
                if slot == DVE["parts2"] and batch_valid(f):
                    dve_parts2(dve, f, r)
                if batch_valid(m):
                    dve_max_tile(dve, m, slot)
                if slot == DVE["stats"] and batch_valid(f + 1):
                    dve_stats(dve, f + 1)
                if slot == DVE["normalise"] and batch_valid(f + 1):
                    dve_normalise(dve, f + 1)
                if slot == DVE["add"] and batch_valid(t):
                    dve_add(dve, t)

        def act_hT(act, b):
            act.wait_ge(xn_turned, b + 1)
            at_least(act, v_made, b)
            act.activation(hT[:], p_m[:, 0:S], ACT.Identity, bias=k.mod[:, 0, SA, bass.ds(b, 1)],
                           scale=k.mod[:, 0, CA, bass.ds(b, 1)]).then_inc(hT_ready, 1)

        def act_qk(act, b, r):
            act.wait_ge(qk_made, b + 1)
            at_least(act, rest_ready, b)
            act.activation(qk[:, 0, :], p_m[:, 0:S], ACT.Identity, bias=k.bq0[:, 0:1], scale=SCALE0)
            act.activation(qk[:, 1, :], p_m[:, S:2 * S], ACT.Identity, bias=k.bk0[:, 0:1]).then_inc(qk_ready, 1)
            act.wait_ge(qk_ready, b + 1)
            at_least(act, stacked, 16 * STACK_DMAS * (b - 1))
            act.activation(parts[r % 2][:, 0], qk[:], ACT.Copy).then_inc(part0_ready, 1)

        def act_part1(act, b, r):
            act.wait_ge(rest_ready, b + 1)
            act.activation(parts[r % 2][:, 1], rest[:], ACT.Copy).then_inc(part1_ready, 1)

        def act_v(act, b, r):
            act.wait_ge(v_made, b + 1)
            at_least(act, pv_made, 4 * (b - NB) + 4)
            act.activation(V[r][:, :, :, 0:DH0], p_m[:, 0:NT * D].rearrange("p (i h d) -> p i h d", i=NT, h=H0),
                           ACT.Copy).then_inc(v_ready, 1)

        def act_maxT(act, b):
            act.wait_ge(max_turned, b + 1)
            at_least(act, max_stacked, 32 * b)
            act.activation(maxT[:], p_m16[0:6 * PAIRS, 0:S], ACT.Copy).then_inc(maxT_ready, 1)

        def act_exp(act, b, t):
            g = t // 2
            act.wait_ge(scoredT, PAIRS * b + t + 1)
            if t % 2 == 0:
                at_least(act, pv_made, 4 * b + g - 1)
            act.activation(probs[g % 2][:, t % 2], p_sT[t % 2][:], ACT.Exp).then_inc(exped, 1)

        def act_OT(act, b, g):
            act.wait_ge(pv_made, 4 * b + g + 1)
            at_least(act, O_turned, 2 * (b - 1) + g // 2 + 1)
            act.activation(OT[g][:], p_o[:, 0:S], ACT.Copy).then_inc(OT_ready, 1)

        def act_OTn(act, b):
            act.wait_ge(OTn_turned, b + 1)
            at_least(act, y_made, b)
            act.activation(OTn[:], p_m[:, 0:S], ACT.Copy).then_inc(OTn_ready, 1)

        def act_y(act, b):
            act.wait_ge(y_made, b + 1)
            at_least(act, y_turned, b)
            act.activation(yT[:], p_m[:, 0:S], ACT.Identity, bias=k.gbo0[:, bass.ds(b, 1)],
                           scale=k.mod[:, 0, GA, bass.ds(b, 1)]).then_inc(yT_ready, 1)

        def act_step(act, n, r):
            f, m, s, t = n, n - 2, n - 3, n - 4
            for slot in range(TILES):
                if slot == ACTS["hT"] and batch_valid(f):
                    act_hT(act, f)
                if slot == ACTS["maxT"] and batch_valid(s):
                    act_maxT(act, s)
                if slot == ACTS["qk"] and batch_valid(f):
                    act_qk(act, f, r)
                if slot == ACTS["part1"] and batch_valid(f):
                    act_part1(act, f, r)
                if slot == ACTS["v"] and batch_valid(f):
                    act_v(act, f, r)
                if slot == ACTS["OTn"] and batch_valid(t):
                    act_OTn(act, t)
                if slot == ACTS["y"] and batch_valid(t):
                    act_y(act, t)
                if slot >= 6 and slot % 2 == 0 and batch_valid(s):
                    act_exp(act, s, (slot - 6) // 2)
                if slot in (0, 2, 4) and batch_valid(t):
                    act_exp(act, t, 5 + slot // 2)
                if slot in ACTS["OT_s"] and batch_valid(s):
                    act_OT(act, s, ACTS["OT_s"].index(slot))
                if slot in ACTS["OT_t"] and batch_valid(t):
                    act_OT(act, t, 2 + ACTS["OT_t"].index(slot))

        def sp_max(sp, b, r):
            wait_apart(sp, k, maxT_ready, b + 1)
            wait_apart(sp, k, scored, TILES * (b + 1))
            for w in range(2):
                sp.dma_start(Q[r][MAXROW:MAXROW + 3, w::2, :], maxT[w * 3 * PAIRS:(w + 1) * 3 * PAIRS, :]
                             ).then_inc(max_stacked, 16)

        def sp_stack(sp, b, r):
            if not isinstance(b, int) or b >= NB:
                wait_apart(sp, k, scoredT, PAIRS * (b - NB + 1))
            if not isinstance(b, int) or b >= 1:
                wait_apart(sp, k, stacked, 16 * STACK_DMAS * b)
            if not isinstance(b, int) or b >= 2:
                wait_apart(sp, k, Q_ready, b - 1)
            for part, ready in enumerate((part0_ready, part1_ready, part2_ready)):
                sp.wait_ge(ready, b + 1)
                for n, (q_part, k_part) in enumerate(TERMS):
                    rows = slice(n * TROWS, (n + 1) * TROWS)
                    if q_part == part:
                        sp.dma_start(Qall[r % 2][rows, :, :], parts[r % 2][:, part, 0, :]).then_inc(stacked, 16)
                    if k_part == part:
                        sp.dma_start(K[r][rows, :, :], parts[r % 2][:, part, 1, :]).then_inc(stacked, 16)

        def sp_step(sp, n, r):
            if batch_valid(n - 3):
                sp_max(sp, n - 3, (r - 3) % NB)
            if batch_valid(n):
                sp_stack(sp, n, r)

        def pool_rstd(pool, b):
            pool.wait_ge(var_ready, b + 1)
            at_least(pool, xn_ready, b)
            pool.tensor_tensor(rstd[:], var_eps[:], k.minus_half[:, 0:NT], ALU.pow).then_inc(rstd_ready, 1)

        def pool_Q(pool, b, r):
            pool.wait_ge(stacked, 16 * STACK_DMAS * (b + 1))
            if not isinstance(b, int) or b >= NB:
                wait_apart(pool, k, scoredT, PAIRS * (b - NB + 1))
            for w in range(2):
                ins = pool.tensor_scalar(Q[r][0:MAXROW, w::2, :], Qall[r % 2][0:MAXROW], k.parity[0:MAXROW, w:w + 1], 0.0,
                                         ALU.mult, ALU.add)
            ins.then_inc(Q_ready, 1)

        def pool_step(pool, n, r):
            if batch_valid(n + 1):
                pool_rstd(pool, n + 1)
            pool_Q(pool, n, r)

        LOOPS = (B - 1 - 4) // NB
        WHOLE = range(4, 4 + NB * LOOPS)
        LAST = B + 4

        block = ctx.enter_context(nc.Block())

        @block.sync
        def _(sp):
            for n in range(WHOLE.start):
                sp_step(sp, n, n % NB)
            with sp.Fori(0, LOOPS) as turn:
                for r in range(NB):
                    sp_step(sp, turn * NB + (WHOLE.start + r), r)
            late = late_loads(k, a)
            assert len(late) == LATE_LOADS
            per_step = -(-len(late) // (LAST - WHOLE.stop))
            for n in range(WHOLE.stop, LAST):
                sp_step(sp, n, n % NB)
                for to, of in late[:per_step]:
                    sp.dma_start(to, of, allow_slow_non_contiguous=True).then_inc(k.late_loaded, 16)
                late = late[per_step:]

        @block.gpsimd
        def _(pool):
            pool_rstd(pool, 0)
            for n in range(WHOLE.start):
                pool_step(pool, n, n % NB)
            with pool.Fori(0, LOOPS) as turn:
                for r in range(NB):
                    pool_step(pool, turn * NB + (WHOLE.start + r), r)
            for n in range(WHOLE.stop, B):
                pool_step(pool, n, n % NB)

        @block.tensor
        def _(pe):
            for n in range(WHOLE.start):
                pe_step(pe, n, n % NB)
            with pe.Fori(0, LOOPS) as turn:
                for r in range(NB):
                    pe_step(pe, turn * NB + (WHOLE.start + r), r)
            for n in range(WHOLE.stop, LAST):
                pe_step(pe, n, n % NB)

        @block.scalar
        def _(act):
            for n in range(WHOLE.start):
                act_step(act, n, n % NB)
            with act.Fori(0, LOOPS) as turn:
                for r in range(NB):
                    act_step(act, turn * NB + (WHOLE.start + r), r)
            for n in range(WHOLE.stop, LAST):
                act_step(act, n, n % NB)

        @block.vector
        def _(dve):
            dve_stats(dve, 0)
            dve_normalise(dve, 0)
            for n in range(WHOLE.start):
                dve_step(dve, n, n % NB)
            with dve.Fori(0, LOOPS) as turn:
                for r in range(NB):
                    dve_step(dve, turn * NB + (WHOLE.start + r), r)
            for n in range(WHOLE.stop, LAST):
                dve_step(dve, n, n % NB)



def ffn_weights(nc, k, sb):
    for name, blocks, width in (("w1", 1, F), ("w2", 1, F), ("h1", FB, F), ("h2", FB, F), ("w3", FB, D)):
        for part in ("hi", "lo"):
            k.w[f"{name}_{part}"] = sb(f"{name}_{part}", [P, blocks, width], F32R)
    k.rows_inexact = sb("rows_inexact", [1, 1], mybir.dt.int32)
    with ExitStack() as ctx:
        sbt, ps, sem = tensors(nc, ctx, "ffn0w")
        lo_abs = sbt("lo_abs", [P, F])
        lo_sums = sbt("lo_sums", [P, 11])
        lo_sum = sbt("lo_sum", [P, 1])
        inexact = sbt("inexact", [P, 1])
        ones = sbt("ones", [P, 1])
        p_count = ps("p_count", [P, 512])
        ones_ready = sem("ones_ready")
        lo_summed = sem("lo_summed")
        lo_summed_dve = sem("lo_summed_dve")
        inexact_step = sem("inexact_step")
        counted = sem("counted")
        raw = k.raw_ffn
        scales = k.ffn_scales
        p_t = [ps(f"p_t{n}", [P, 4, P]) for n in range(4)]
        turned = sem("turned")
        hi_ready = sem("hi_ready")
        lo_ready = sem("lo_ready")

        groups = []
        for n, (name, ob, ib, at) in enumerate(FFN_PLAN):
            if name == "w3":
                groups.append((n, [at + i for i in range(FB)], name, None))
            else:
                for i in range(ib):
                    groups.append((n, [at + o * ib + i for o in range(FB)], name, i))

        def dest(name, i, part):
            w = k.w[f"{name}_{part}"]
            return w[:, :, :].rearrange("p i d -> p (i d)") if i is None else w[:, i, :]

        block = ctx.enter_context(nc.Block())

        @block.tensor
        def _(pe):
            for g, (n, of, name, i) in enumerate(groups):
                pe.wait_ge(k.late_loaded, LATE_LOADED)
                at_least(pe, lo_ready, g - 3)
                for j, o in enumerate(of):
                    mm = pe.transpose(p_t[g % 4][:, j, :], raw[:, o, :], k.ident[:])
                mm.then_inc(turned, 1)
            pe.wait_ge(ones_ready, 1)
            pe.wait_ge(inexact_step, 2)
            pe.matmul(p_count[0:1, 0:1], inexact[:], ones[:], start=True, stop=True).then_inc(counted, 1)

        @block.gpsimd
        def _(pool):
            pool.memset(ones[:], 1.0).then_inc(ones_ready, 1)

        @block.scalar
        def _(act):
            def sum_lo(g):
                n, of, name, i = groups[g]
                act.wait_ge(lo_ready, g + 1)
                at_least(act, lo_summed, g // 2)
                act.activation(lo_abs[:], dest(name, i, "lo").bitcast(F32), ACT.Abs, accum_out=lo_sums[:, g:g + 1]
                               ).then_inc(lo_summed, 1)

            for g, (n, of, name, i) in enumerate(groups):
                act.wait_ge(turned, g + 1)
                act.activation(dest(name, i, "hi"), p_t[g % 4][:].rearrange("p j d -> p (j d)"), ACT.Copy
                               ).then_inc(hi_ready, 1)
                if g % 2 == 0 and g >= 2:
                    sum_lo(g - 1)

        @block.vector
        def _(dve):
            for g, (n, of, name, i) in enumerate(groups):
                dve.wait_ge(hi_ready, g + 1)
                dve.tensor_tensor(dest(name, i, "lo"), p_t[g % 4][:].rearrange("p j d -> p (j d)"),
                                  dest(name, i, "hi").bitcast(F32), ALU.subtract).then_inc(lo_ready, 1)
                if g % 2 == 0:
                    dve.wait_ge(lo_ready, g + 1)
                    dve.tensor_reduce(lo_sums[:, g:g + 1], dest(name, i, "lo").bitcast(F32), AX.X, ALU.add,
                                      apply_absolute_value=True).then_inc(lo_summed_dve, 1)
            dve.wait_ge(lo_summed_dve, (len(groups) + 1) // 2)
            dve.wait_ge(lo_summed, len(groups) // 2)
            dve.tensor_reduce(lo_sum[:], lo_sums[:], AX.X, ALU.add).then_inc(inexact_step, 1)
            dve.wait_ge(inexact_step, 1)
            dve.tensor_scalar(inexact[:], lo_sum[:], 0.0, None, ALU.not_equal).then_inc(inexact_step, 1)
            dve.wait_ge(counted, 1)
            dve.tensor_copy(k.rows_inexact[:], p_count[0:1, 0:1])
            dve.wait_ge(k.late_loaded, LATE_LOADED)
            dve.scalar_tensor_tensor(out=k.ab_scale[:], in0=scales[:, 0, :], scalar=0.5, in1=scales[:, 1, :],
                                     op0=ALU.mult, op1=ALU.mult)
            dve.tensor_scalar(k.half_s1[:], scales[:, 0, :], 0.5, None, ALU.mult)
            dve.tensor_scalar(k.w3_gate[:], k.mod[:, 0, GB, :], k.w3_scale[:, 0:1], None, ALU.mult)


def split_product(pe, out, hi_lo_w, hi_lo_x, first, last, w_lo_is_zero=False):
    (w_hi, w_lo), (x_hi, x_lo) = hi_lo_w, hi_lo_x
    pe.matmul(out, w_hi, x_hi, start=first, stop=False)
    mm = pe.matmul(out, w_hi, x_lo, start=False, stop=last and w_lo_is_zero)
    if w_lo_is_zero:
        return mm
    return pe.matmul(out, w_lo, x_hi, start=False, stop=last)


def layer_norm_steps(nc, k, sb, sem, tag=""):
    n = Names()
    n.stats = sb(tag + "stats", [P, NT, 6])
    n.meanvar = sb(tag + "meanvar", [P, NT, 2])
    n.var_eps = sb(tag + "var_eps", [P, NT])
    n.rstd = sb(tag + "rstd", [P, NT])
    n.xn = sb(tag + "xn", [P, NT, D])
    n.stats_step = sem(tag + "stats_step")
    n.var_ready = sem(tag + "var_ready")
    n.rstd_ready = sem(tag + "rstd_ready")
    n.xn_ready = sem(tag + "xn_ready")
    n.xn_turned = sem(tag + "xn_turned")

    def dve_stats(dve, b):
        if not isinstance(b, int) or b >= 1:
            wait_apart(dve, k, n.xn_ready, b)
        for i in range(NT):
            dve.bn_stats(n.stats[:, i, :], k.X[:, bass.ds(b * NT + i, 1), :]).then_inc(n.stats_step, 1)
        wait_apart(dve, k, n.stats_step, 3 * b + 2)
        for i in range(NT):
            ins = dve.bn_aggr(n.meanvar[:, i, :], n.stats[:, i, :])
        ins.then_inc(n.stats_step, 1)
        dve.wait_ge(n.stats_step, 3 * b + 3)
        at_least(dve, n.rstd_ready, b)
        dve.tensor_scalar(n.var_eps[:], n.meanvar[:, :, 1], EPS, None, ALU.add).then_inc(n.var_ready, 1)

    def dve_normalise(dve, b):
        dve.wait_ge(n.rstd_ready, b + 1)
        at_least(dve, n.xn_turned, b)
        for i in range(NT):
            ins = dve.tensor_scalar(n.xn[:, i, :], k.X[:, bass.ds(b * NT + i, 1), :].rearrange("p o d -> p (o d)"),
                                    n.meanvar[:, i, 0:1], n.rstd[:, i:i + 1], ALU.subtract, ALU.mult)
        ins.then_inc(n.xn_ready, 1)

    def pool_rstd(pool, b):
        pool.wait_ge(n.var_ready, b + 1)
        at_least(pool, n.xn_ready, b)
        pool.tensor_tensor(n.rstd[:], n.var_eps[:], k.minus_half[:, 0:NT], ALU.pow).then_inc(n.rstd_ready, 1)

    def pe_turn(pe, b, p_m):
        pe.wait_ge(n.xn_ready, b + 1)
        for i in range(NT):
            mm = pe.transpose(p_m[:, i * P:(i + 1) * P], n.xn[:, i, :], k.ident[:])
        mm.then_inc(n.xn_turned, 1)

    n.dve_stats, n.dve_normalise, n.pool_rstd, n.pe_turn = dve_stats, dve_normalise, pool_rstd, pe_turn
    return n


def ffn0(nc, k):
    with ExitStack() as ctx:
        sb, ps, sem = tensors(nc, ctx, "ffn0s")
        ln = layer_norm_steps(nc, k, sb, sem)
        HB = FB // 2
        hT = sb("hT", [P, S])
        h_hi = [sb(f"h_hi{n}", [P, S], F32R) for n in range(2)]
        h_lo = [sb(f"h_lo{n}", [P, S], F32R) for n in range(2)]
        tanh_a = [sb(f"tanh_a{n}", [P, 2, S]) for n in range(HB)]
        gated = [sb(f"gated{n}", [P, 2, S]) for n in range(HB)]
        u = [sb(f"u{n}", [P, 2, S]) for n in range(2)]
        u_hi, u_lo, g1_hi, g1_lo, g2_hi, g2_lo = (
            [sb(f"{name}{n}", [P, FB, S], F32R) for n in range(2)]
            for name in ("u_hi", "u_lo", "g1_hi", "g1_lo", "g2_hi", "g2_lo"))
        g = [sb(f"g{n}", [P, 2, S]) for n in range(2)]
        yT = sb("yT", [P, S])

        p_a = [ps(f"p_a{n}", [P, 2, S]) for n in range(HB)]
        p_b = [ps(f"p_b{n}", [P, 2, S]) for n in range(HB)]
        p_h = [ps(f"p_h{n}", [P, 2, S]) for n in range(HB)]
        p_m = ps("p_m", [P, 512])
        p_y = ps("p_y", [P, 512])

        hT_ready = sem("hT_ready")
        h_hi_ready = sem("h_hi_ready")
        h_lo_ready = sem("h_lo_ready")
        a_made = sem("a_made")
        b_made = sem("b_made")
        tanh_ready = sem("tanh_ready")
        gated_ready = sem("gated_ready")
        u_ready = sem("u_ready")
        u_hi_ready = sem("u_hi_ready")
        u_lo_ready = sem("u_lo_ready")
        h1_made = sem("h1_made")
        g1_ready = sem("g1_ready")
        g1_lo_ready = sem("g1_lo_ready")
        h2_made = sem("h2_made")
        g2_ready = sem("g2_ready")
        g2_lo_ready = sem("g2_lo_ready")
        y_made = sem("y_made")
        yT_ready = sem("yT_ready")
        y_turned = sem("y_turned")
        x_added = sem("x_added")

        moe = moe_weight_steps(k, sem, [bank[:] for bank in (*p_a, *p_b)])
        moe_groups = {B + 1: (0, 1), B + 2: (2, 3), B + 3: (4,), B + 4: (5,)}

        def groups_of(n):
            return moe_groups.get(n, ()) if isinstance(n, int) else ()

        def pe_ab(pe, b, r, exact):
            pe.wait_ge(h_lo_ready, b + 1)
            for q in range(HB):
                for bank, name, made in ((p_a[q], "w1", a_made), (p_b[q], "w2", b_made)):
                    at_least(pe, u_ready, HB * (b - 1) + q + 1)
                    w = k.w[name + "_hi"], k.w[name + "_lo"]
                    for m in range(2):
                        cols = slice((2 * q + m) * P, (2 * q + m + 1) * P)
                        mm = split_product(pe, bank[:, m, :], [x[:, 0, cols] for x in w], (h_hi[r][:], h_lo[r][:]),
                                           True, True, exact)
                    mm.then_inc(made, 1)

        def pe_hidden(pe, b, r, exact, name, x_hi, x_lo, x_ready, before, made):
            w = k.w[name + "_hi"], k.w[name + "_lo"]
            for q in range(HB):
                before(q)
                for m in range(2):
                    cols = slice((2 * q + m) * P, (2 * q + m + 1) * P)
                    for i in range(FB):
                        if q == m == 0 and i % 2 == 0:
                            pe.wait_ge(x_ready, HB * b + i // 2 + 1)
                        mm = split_product(pe, p_h[q][:, m, :], [x[:, i, cols] for x in w],
                                           (x_hi[r][:, i, :], x_lo[r][:, i, :]), i == 0, i == FB - 1, exact)
                mm.then_inc(made, 1)

        def pe_w3(pe, b, r, exact):
            pe.wait_ge(g2_lo_ready, HB * (b + 1))
            at_least(pe, yT_ready, b)
            for i in range(FB):
                mm = split_product(pe, p_y[:, 0:S], (k.w["w3_hi"][:, i, :], k.w["w3_lo"][:, i, :]),
                                   (g2_hi[r][:, i, :], g2_lo[r][:, i, :]), i == 0, i == FB - 1, exact)
            mm.then_inc(y_made, 1)

        def pe_step(pe, n, r, exact):
            if batch_valid(n - 2):
                def free1(q):
                    at_least(pe, g2_ready, HB * (n - 4) + q + 1)
                pe_hidden(pe, n - 2, r, exact, "h1", u_hi, u_lo, u_lo_ready, free1, h1_made)
            if batch_valid(n - 5):
                pe.wait_ge(yT_ready, n - 4)
                if batch_valid(n - 1):
                    pe.wait_ge(h_hi_ready, n)
                at_least(pe, x_added, n - 5)
                for i in range(NT):
                    mm = pe.transpose(p_m[:, i * P:(i + 1) * P], yT[:, i * P:(i + 1) * P], k.ident[:])
                mm.then_inc(y_turned, 1)
            if batch_valid(n - 1):
                pe_ab(pe, n - 1, (r + 1) % 2, exact)
            if batch_valid(n - 4):
                pe_w3(pe, n - 4, r, exact)
            if batch_valid(n):
                at_least(pe, x_added, n - 4)
                ln.pe_turn(pe, n, p_m)
            if batch_valid(n - 3):
                def free2(q):
                    if batch_valid(n - 2):
                        pe.wait_ge(g1_ready, HB * (n - 2) + q + 1)
                    else:
                        at_least(pe, g2_ready, HB * (n - 4) + q + 1)
                pe_hidden(pe, n - 3, (r + 1) % 2, exact, "h2", g1_hi, g1_lo, g1_lo_ready, free2, h2_made)
            for group in groups_of(n):
                pe.wait_ge(u_ready, HB * B)
                moe.pe_group(pe, group)

        def act_h(act, b, r):
            act.wait_ge(ln.xn_turned, b + 1)
            at_least(act, h_lo_ready, b)
            scale, bias = k.mod[:, 0, CB, bass.ds(b, 1)], k.mod[:, 0, SB, bass.ds(b, 1)]
            act.activation(hT[:], p_m[:, 0:S], ACT.Identity, bias=bias, scale=scale).then_inc(hT_ready, 1)
            if not isinstance(b, int) or b >= 2:
                wait_apart(act, k, b_made, HB * (b - 1))
            act.activation(h_hi[r][:], p_m[:, 0:S], ACT.Identity, bias=bias, scale=scale).then_inc(h_hi_ready, 1)

        def act_tanh(act, b, q):
            act.wait_ge(a_made, HB * b + q + 1)
            at_least(act, gated_ready, HB * (b - 1) + q + 1)
            for m in range(2):
                ins = act.activation(tanh_a[q][:, m, :], p_a[q][:, m, :], ACT.Tanh,
                                     scale=k.half_s1[:, 2 * q + m:2 * q + m + 1])
            ins.then_inc(tanh_ready, 1)

        def act_u_hi(act, b, r, q):
            act.wait_ge(u_ready, HB * b + q + 1)
            at_least(act, h1_made, HB * (b - 1))
            act.activation(u_hi[r][:, 2 * q:2 * q + 2, :], u[q][:], ACT.Copy).then_inc(u_hi_ready, 1)

        def act_gelu(act, b, r, q, layer, made, g_hi, g_ready, g_lo_ready, g_read, g_used):
            act.wait_ge(made, HB * b + q + 1)
            g_used(q)
            for m in range(2):
                act.activation(g[q][:, m, :], p_h[q][:, m, :], ACT.Gelu,
                               scale=k.ffn_scales[:, layer, 2 * q + m:2 * q + m + 1])
            at_least(act, g_read, (b - 1) * HB if layer == 2 else b - 1)
            for m in range(2):
                ins = act.activation(g_hi[r][:, 2 * q + m, :], p_h[q][:, m, :], ACT.Gelu,
                                     scale=k.ffn_scales[:, layer, 2 * q + m:2 * q + m + 1])
            ins.then_inc(g_ready, 1)

        def act_step(act, n, r):
            if batch_valid(n - 2):
                def used1(q):
                    at_least(act, g2_lo_ready, HB * (n - 4) + q + 1)
                for q in range(HB):
                    act_gelu(act, n - 2, r, q, 2, h1_made, g1_hi, g1_ready, g1_lo_ready, h2_made, used1)
            if batch_valid(n - 1):
                for q in range(HB):
                    act_tanh(act, n - 1, q)
            if batch_valid(n - 1):
                act_u_hi(act, n - 1, (r + 1) % 2, 0)
            if batch_valid(n - 3):
                def used2(q):
                    if batch_valid(n - 2):
                        act.wait_ge(g1_lo_ready, HB * (n - 2) + q + 1)
                    else:
                        at_least(act, g2_lo_ready, HB * (n - 4) + q + 1)
                act_gelu(act, n - 3, (r + 1) % 2, 0, 3, h2_made, g2_hi, g2_ready, g2_lo_ready, y_made, used2)
            if batch_valid(n - 1):
                act_u_hi(act, n - 1, (r + 1) % 2, 1)
            if batch_valid(n):
                act_h(act, n, r)
            if batch_valid(n - 3):
                act_gelu(act, n - 3, (r + 1) % 2, 1, 3, h2_made, g2_hi, g2_ready, g2_lo_ready, y_made, used2)
            if batch_valid(n - 4):
                act.wait_ge(y_made, n - 3)
                at_least(act, y_turned, n - 4)
                act.activation(yT[:], p_y[:, 0:S], ACT.Copy, scale=k.w3_gate[:, bass.ds(n - 4, 1)]
                               ).then_inc(yT_ready, 1)
            for group in groups_of(n):
                moe.act_group(act, group)

        def dve_u(dve, b, r, q):
            dve.wait_ge(tanh_ready, HB * b + q + 1)
            at_least(dve, u_ready, HB * (b - 1) + q + 1)
            dve.scalar_tensor_tensor(out=gated[q][:], in0=tanh_a[q][:], scalar=1.0, in1=p_a[q][:],
                                     op0=ALU.add, op1=ALU.mult).then_inc(gated_ready, 1)
            dve.wait_ge(gated_ready, HB * b + q + 1)
            dve.wait_ge(b_made, HB * b + q + 1)
            at_least(dve, u_lo_ready, HB * (b - 1) + q + 1)
            for m in range(2):
                ins = dve.scalar_tensor_tensor(out=u[q][:, m, :], in0=p_b[q][:, m, :],
                                               scalar=k.ab_scale[:, 2 * q + m:2 * q + m + 1], in1=gated[q][:, m, :],
                                               op0=ALU.mult, op1=ALU.mult)
            ins.then_inc(u_ready, 1)

        def dve_lo(dve, b, r, q, ready, read, read_at, lo, hi, g_buf, lo_ready):
            dve.wait_ge(ready, HB * b + q + 1)
            at_least(dve, read, read_at)
            dve.tensor_tensor(lo[r][:, 2 * q:2 * q + 2, :], g_buf[q][:], hi[r][:, 2 * q:2 * q + 2, :].bitcast(F32),
                              ALU.subtract).then_inc(lo_ready, 1)

        def dve_step(dve, n, r):
            o = (r + 1) % 2
            if batch_valid(n + 1):
                ln.dve_stats(dve, n + 1)
            if batch_valid(n - 2):
                for q in range(HB):
                    dve_lo(dve, n - 2, r, q, g1_ready, h2_made, HB * (n - 3), g1_lo, g1_hi, g, g1_lo_ready)
            if batch_valid(n - 5):
                dve.wait_ge(y_turned, n - 4)
                x = k.X[:, bass.ds((n - 5) * NT, NT), :]
                dve.tensor_tensor(x, x, p_m[:, 0:S].rearrange("p (i d) -> p i d", i=NT), ALU.add
                                  ).then_inc(x_added, 1)
            if batch_valid(n - 1):
                for q in range(HB):
                    dve_u(dve, n - 1, o, q)
                for q in range(HB):
                    dve_lo(dve, n - 1, o, q, u_hi_ready, h1_made, HB * (n - 2), u_lo, u_hi, u, u_lo_ready)
            if batch_valid(n):
                dve.wait_ge(h_hi_ready, n + 1)
                dve.wait_ge(hT_ready, n + 1)
                at_least(dve, b_made, HB * (n - 1))
                dve.tensor_tensor(h_lo[r][:], hT[:], h_hi[r][:].bitcast(F32), ALU.subtract).then_inc(h_lo_ready, 1)
            if batch_valid(n + 1):
                ln.dve_normalise(dve, n + 1)
            if batch_valid(n - 3):
                for q in range(HB):
                    dve_lo(dve, n - 3, o, q, g2_ready, y_made, n - 4, g2_lo, g2_hi, g, g2_lo_ready)
            for group in groups_of(n):
                moe.dve_group(dve, group)

        WHOLE0, LOOPS, LAST = 5, 5, B + 5

        block = ctx.enter_context(nc.Block())

        @block.gpsimd
        def _(pool):
            ln.pool_rstd(pool, 0)
            with pool.Fori(1, B) as b:
                ln.pool_rstd(pool, b)

        def pe_program(pe, exact):
            for n in range(WHOLE0):
                pe_step(pe, n, n % 2, exact)
            with pe.Fori(0, LOOPS) as turn:
                for r in range(2):
                    pe_step(pe, turn * 2 + (WHOLE0 + r), (WHOLE0 + r) % 2, exact)
            for n in range(WHOLE0 + 2 * LOOPS, LAST):
                pe_step(pe, n, n % 2, exact)

        @block.tensor
        def _(pe):
            rows_inexact = pe.value_load(k.rows_inexact[0:1, 0:1], min_val=0, max_val=P)
            with pe.If(rows_inexact == 0):
                pe_program(pe, exact=True)
            with pe.Else():
                pe_program(pe, exact=False)

        @block.scalar
        def _(act):
            for n in range(WHOLE0):
                act_step(act, n, n % 2)
            with act.Fori(0, LOOPS) as turn:
                for r in range(2):
                    act_step(act, turn * 2 + (WHOLE0 + r), (WHOLE0 + r) % 2)
            for n in range(WHOLE0 + 2 * LOOPS, LAST):
                act_step(act, n, n % 2)

        @block.vector
        def _(dve):
            ln.dve_stats(dve, 0)
            ln.dve_normalise(dve, 0)
            for n in range(WHOLE0):
                dve_step(dve, n, n % 2)
            with dve.Fori(0, LOOPS) as turn:
                for r in range(2):
                    dve_step(dve, turn * 2 + (WHOLE0 + r), (WHOLE0 + r) % 2)
            for n in range(WHOLE0 + 2 * LOOPS, LAST):
                dve_step(dve, n, n % 2)


MASKED = -1e30


def attention1_weights(nc, k, wsb):
    k.wg = wsb("wg", [P, E])
    k.sel16 = wsb("sel16", [P, E, P], BF16)
    for name in ("wq1", "wk1", "wv1", "wo1"):
        k.w[name] = wsb(name, [P, D])
    k.gate_m = wsb("gate_m", [P, 1])
    k.gbo1 = wsb("gbo1", [P, B])
    k.mask16 = wsb("mask16", [P, P], BF16)
    with ExitStack() as ctx:
        sb, ps, sem = tensors(nc, ctx, "att1w")
        raw, beta, bo = k.raw_att1, k.beta, k.bo1
        tanh_b = sb("tanh_b", [P, 1 + H1])
        gate_a = sb("gate_a", [P, H1])
        sel = sb("sel", [P, E])
        ones = sb("ones", [P, P])
        p_t = ps("p_t", [P, 4, D])
        p_g = ps("p_g", [P, 512])
        wg_turned = sem("wg_turned")
        sel_step = sem("sel_step")
        turned = sem("turned")
        tanh_ready = sem("tanh_ready")
        gate_ready = sem("gate_ready")
        mask_ready = sem("mask_ready")
        block = ctx.enter_context(nc.Block())

        @block.gpsimd
        def _(pool):
            pool.memset(k.mask16[:], 0.0).then_inc(mask_ready, 1)
            pool.wait_ge(mask_ready, 1)
            pool.affine_select(out=k.mask16[:], in_=k.mask16[:], compare_op=ALU.is_ge, fill=MASKED, base=0,
                               pattern=[[-1, P]], channel_multiplier=1).then_inc(mask_ready, 1)

        @block.tensor
        def _(pe):
            pe.wait_ge(k.late_loaded, LATE_LOADED)
            for n in range(4):
                mm = pe.transpose(p_t[:, n, :], raw[:, n, :], k.ident[:])
            mm.then_inc(turned, 1)
            pe.transpose(p_g[:, 0:E], k.raw_g[:], k.ident[0:E, 0:E]).then_inc(wg_turned, 1)

        @block.scalar
        def _(act):
            act.wait_ge(k.late_loaded, LATE_LOADED)
            act.activation(tanh_b[:], beta[:], ACT.Tanh, scale=0.5).then_inc(tanh_ready, 1)

        @block.vector
        def _(dve):
            dve.wait_ge(tanh_ready, 1)
            dve.tensor_scalar(k.gate_m[:], tanh_b[:, 0:1], 0.5, 0.5, ALU.mult, ALU.add)
            dve.tensor_scalar(gate_a[:], tanh_b[:, 1:], -0.5, 0.5, ALU.mult, ALU.add).then_inc(gate_ready, 1)
            dve.wait_ge(k.late_loaded, LATE_LOADED)
            dve.wait_ge(gate_ready, 1)
            dve.tensor_scalar(k.memz[:, 0:D], k.memz[:, 0:D], k.gate_m[:, 0:1], None, ALU.mult)
            dve.tensor_scalar(k.gbo1[:], k.mod[:, 1, GA, :], bo[:, 0:1], None, ALU.mult)
            dve.wait_ge(turned, 1)
            for n, name in enumerate(("wq1", "wk1", "wv1", "wo1")):
                if name == "wv1":
                    dve.tensor_tensor(k.w[name][:].rearrange("p (h d) -> p h d", h=H1),
                                      p_t[:, n, :].rearrange("p (h d) -> p h d", h=H1),
                                      gate_a[:].unsqueeze(2).to_broadcast([P, H1, DH1]), ALU.mult)
                else:
                    dve.tensor_copy(k.w[name][:], p_t[:, n, :])
            dve.memset(ones[:], 1.0).then_inc(sel_step, 1)
            dve.tensor_reduce(sel[:], k.ident[:, 0:CP * E].rearrange("p (c e) -> p e c", e=E), AX.X, ALU.add
                              ).then_inc(sel_step, 1)
            dve.wait_ge(sel_step, 2)
            for e in range(E):
                dve.tensor_scalar(k.sel16[:, e, :], ones[:], sel[:, e:e + 1], None, ALU.mult)
            dve.wait_ge(wg_turned, 1)
            dve.tensor_copy(k.wg[:], p_g[:, 0:E])


def attention1(nc, k):
    with ExitStack() as ctx:
        sb, ps, sem = tensors(nc, ctx, "att1")
        ln = layer_norm_steps(nc, k, sb, sem)
        ln2 = layer_norm_steps(nc, k, sb, sem, "ffn_")
        hT2 = sb("hT2", [P, S])
        gating = gating_steps(k, sem, 0, EARLY * NT)
        hT = [sb(f"hT{n}", [P, S]) for n in range(2)]
        qT = sb("qT", [P, S])
        kT = sb("kT", [P, S])
        q_hi = [sb(f"q_hi{n}", [P, H1, S], F32R) for n in range(2)]
        q_lo = [sb(f"q_lo{n}", [P, H1, S], F32R) for n in range(2)]
        k_hi = [sb(f"k_hi{n}", [P, S], F32R) for n in range(2)]
        k_lo = [sb(f"k_lo{n}", [P, S], F32R) for n in range(2)]
        q_min = sb("q_min", [P, S])
        q_exp = sb("q_exp", [P, S])
        sq = [sb(f"sq{n}", [P, S]) for n in range(2)]
        V = [sb(f"V{n}", [P, NT, D]) for n in range(2)]
        rowmax = sb("rowmax", [P, NT, H1])
        negmax = sb("negmax", [P, NT, H1])
        sums = sb("sums", [P, NT, H1])
        rsums = sb("rsums", [P, NT, H1])
        prob0 = [sb(f"prob0_{n}", [P, H1, P]) for n in range(2)]
        prob1 = [sb(f"prob1_{n}", [P, H1, S]) for n in range(2)]
        probT0 = sb("probT0", [P, H1, S])
        probT1 = sb("probT1", [P, H1, P])
        den = sb("den", [P, NT, H1])
        rden = sb("rden", [P, NT, H1])
        A = [sb(f"A{n}", [P, NT, H1, DH1]) for n in range(2)]
        OT = sb("OT", [P, S])
        yT = sb("yT", [P, S])

        p_s0 = ps("p_s0", [P, H1, P])
        p_s1 = ps("p_s1", [P, H1, S])
        p_t = [ps(f"p_t{n}", [P, 512]) for n in range(2)]
        p_o = ps("p_o", [P, 512])
        p_m = ps("p_m", [P, 512])
        p_n = ps("p_n", [P, 512])

        cleared = sem("cleared")
        hT_ready = sem("hT_ready")
        qk_made = sem("qk_made")
        qT_ready = sem("qT_ready")
        kT_ready = sem("kT_ready")
        k_hi_ready = sem("k_hi_ready")
        k_lo_ready = sem("k_lo_ready")
        q_hi_ready = sem("q_hi_ready")
        q_lo_ready = sem("q_lo_ready")
        q_min_ready = sem("q_min_ready")
        q_exp_ready = sem("q_exp_ready")
        sq_ready = sem("sq_ready")
        v_made = sem("v_made")
        v_ready = sem("v_ready")
        scored = sem("scored")
        maxed = sem("maxed")
        negmax_ready = sem("negmax_ready")
        exped = sem("exped")
        rsums_ready = sem("rsums_ready")
        probs_ready = sem("probs_ready")
        probs_turned = sem("probs_turned")
        probT_ready = sem("probT_ready")
        pv_made = sem("pv_made")
        a_made = sem("a_made")
        den_ready = sem("den_ready")
        rden_ready = sem("rden_ready")
        A_ready = sem("A_ready")
        OT_ready = sem("OT_ready")
        y_made = sem("y_made")
        yT_ready = sem("yT_ready")
        y_turned = sem("y_turned")
        x_added = sem("x_added")
        hT2_ready = sem("hT2_ready")
        beats_cleared = sem("beats_cleared")
        h_hi_ready = sem("h_hi_ready")
        h_lo_ready = sem("h_lo_ready")
        logits_made = sem("logits_made")
        logits_ready = sem("logits_ready")

        def of_batches(x):
            return min(x, B) if isinstance(x, int) else x

        def pe_scores(pe, m, o, i, bank, keys):
            pe.wait_ge(k_lo_ready, m + 1)
            pe.wait_ge(q_lo_ready, m + 1)
            at_least(pe, exped, 2 * m - 1 + i)
            rows = slice(i * P, (i + 1) * P)
            for h in range(H1):
                out = bank[:, h, :]
                pe.matmul(out, q_hi[o][:, h, rows], k_hi[o][:, 0:keys], start=True, stop=False, skip_group_check=True)
                pe.matmul(out, q_hi[o][:, h, rows], k_lo[o][:, 0:keys], start=False, stop=False, skip_group_check=True)
                pe.matmul(out, q_lo[o][:, h, rows], k_hi[o][:, 0:keys], start=False, stop=False, skip_group_check=True)
                mm = pe.matmul(bank[:, h, keys - P:keys], k.ident16[:], k.mask16[:], start=False, stop=True,
                               skip_group_check=True)
            mm.then_inc(scored, 1)

        def pe_step(pe, n, r):
            f, m, t, y, w = n, n - 1, n - 3, n - 4, n - 6
            o = (r + 1) % 2
            if batch_valid(t):
                pe.wait_ge(probs_ready, t + 1)
                for g in range(2):
                    at_least(pe, probT_ready, 3 * t - g)
                    if g == 1:
                        at_least(pe, logits_ready, w)
                    for h in range(2):
                        pe.transpose(p_t[g][:, h * S:h * S + P], prob0[o][:, 2 * g + h, :], k.ident[:])
                        mm = pe.transpose(p_t[g][:, h * S + P:(h + 1) * S], prob1[o][:, 2 * g + h, 0:P], k.ident[:])
                    mm.then_inc(probs_turned, 1)
            if batch_valid(y):
                pe.wait_ge(OT_ready, y + 1)
                if batch_valid(n - 2):
                    pe.wait_ge(A_ready, m)
                pe.matmul(p_n[:, 0:S], k.w["wo1"][:], OT[:], start=True, stop=True).then_inc(y_made, 1)
            if batch_valid(f):
                at_least(pe, v_ready, m)
                ln.pe_turn(pe, f, p_m)
            if batch_valid(m):
                pe_scores(pe, m, o, 0, p_s0, P)
            if batch_valid(w):
                if batch_valid(f):
                    pe.wait_ge(hT_ready, f + 1)
                else:
                    pe.wait_ge(v_ready, of_batches(m))
                    pe.wait_ge(x_added, of_batches(y))
                ln2.pe_turn(pe, w, p_m)
            if batch_valid(f):
                pe.wait_ge(hT_ready, f + 1)
                at_least(pe, A_ready, m)
                at_least(pe, yT_ready, y + 1)
                pe.matmul(p_n[:, 0:S], k.w["wq1"][:], hT[r][:], start=True, stop=True)
                pe.matmul(p_n[:, S:2 * S], k.w["wk1"][:], hT[r][:], start=True, stop=True).then_inc(qk_made, 1)
            if batch_valid(t):
                pe.wait_ge(probT_ready, 3 * t + 1)
                for h in range(H1):
                    mm = pe.transpose(p_t[0][:, h * P:(h + 1) * P], prob1[o][:, h, P:S], k.ident[:])
                mm.then_inc(probs_turned, 1)
            if batch_valid(m):
                pe_scores(pe, m, o, 1, p_s1, S)
            if batch_valid(t):
                pe.wait_ge(A_ready, t + 1)
                at_least(pe, OT_ready, t)
                for i in range(NT):
                    pe.matmul(p_o[:, i * P:(i + 1) * P], A[o][:, i].rearrange("p h d -> p (h d)"), k.ident[:],
                              start=(i == 0), stop=False, skip_group_check=True)
                pe.wait_ge(probT_ready, 3 * t + 3)
                pe.wait_ge(v_ready, t + 1)
                for j, (keys, q0) in enumerate(((probT0, 0), (probT1, P))):
                    for h in range(H1):
                        rows = slice(h * DH1, (h + 1) * DH1)
                        mm = pe.matmul(p_o[rows, q0:S], V[o][:, j, rows], keys[:, h, :], start=False, stop=(j == 1),
                                       skip_group_check=True)
                mm.then_inc(pv_made, 1)
            if batch_valid(m):
                pe.wait_ge(sq_ready, n)
                if batch_valid(f):
                    pe.wait_ge(kT_ready, f + 1)
                    pe.wait_ge(qT_ready, f + 1)
                at_least(pe, yT_ready, y + 1)
                for i in range(NT):
                    mm = pe.matmul(p_n[:, i * S:i * S + D + H1], sq[o][:, i * P:(i + 1) * P], k.memz[:],
                                   start=True, stop=True)
                mm.then_inc(a_made, 1)
            if batch_valid(y):
                if batch_valid(f):
                    pe.wait_ge(hT_ready, f + 1)
                elif batch_valid(n - 2):
                    pe.wait_ge(v_ready, m)
                at_least(pe, x_added, y)
                if batch_valid(w):
                    pe.wait_ge(h_hi_ready, w + 1)
                pe.wait_ge(yT_ready, y + 1)
                for i in range(NT):
                    mm = pe.transpose(p_m[:, i * P:(i + 1) * P], yT[:, i * P:(i + 1) * P], k.ident[:])
                mm.then_inc(y_turned, 1)
            if batch_valid(w):
                pe.wait_ge(hT2_ready, w + 1)
                pe.wait_ge(probT_ready, 3 * of_batches(t + 1) - (1 if batch_valid(t) else 0))
                at_least(pe, logits_ready, w)
                for i in range(NT):
                    mm = pe.matmul(p_t[1][:, i * E:(i + 1) * E], hT2[:, i * P:(i + 1) * P], k.wg[:],
                                   start=True, stop=True)
                mm.then_inc(logits_made, 1)
            if batch_valid(m):
                if batch_valid(f):
                    pe.wait_ge(hT_ready, f + 1)
                at_least(pe, x_added, y + 1)
                for i in range(NT):
                    mm = pe.matmul(p_m[:, i * D:(i + 1) * D], hT[o][:, i * P:(i + 1) * P], k.w["wv1"][:],
                                   start=True, stop=True)
                mm.then_inc(v_made, 1)

        def act_exp(act, m, o, i, bank, prob):
            act.wait_ge(negmax_ready, 2 * m + i + 1)
            at_least(act, probs_turned, 3 * (m - 2) + 2 + i)
            at_least(act, rsums_ready, m)
            for h in range(H1):
                ins = act.activation(prob[o][:, h, :], bank[:, h, :], ACT.Exp, bias=negmax[:, i, h:h + 1],
                                     accum_out=sums[:, i, h:h + 1])
            ins.then_inc(exped, 1)

        def act_step(act, n, r):
            f, m, t, y, w = n, n - 1, n - 3, n - 4, n - 6
            o = (r + 1) % 2
            if batch_valid(t):
                for g in range(2):
                    act.wait_ge(probs_turned, 3 * t + g + 1)
                    at_least(act, pv_made, t)
                    act.activation(probT0[:, 2 * g:2 * g + 2, :], p_t[g][:].rearrange("p (h q) -> p h q", h=2), ACT.Copy
                                   ).then_inc(probT_ready, 1)
            if batch_valid(y):
                act.wait_ge(y_made, y + 1)
                at_least(act, y_turned, y)
                act.activation(yT[:], p_n[:, 0:S], ACT.Identity, bias=k.gbo1[:, bass.ds(y, 1)],
                               scale=k.mod[:, 1, GA, bass.ds(y, 1)]).then_inc(yT_ready, 1)
            if batch_valid(f):
                act.wait_ge(ln.xn_turned, f + 1)
                at_least(act, v_made, m)
                act.activation(hT[r][:], p_m[:, 0:S], ACT.Identity, bias=k.mod[:, 1, SA, bass.ds(f, 1)],
                               scale=k.mod[:, 1, CA, bass.ds(f, 1)]).then_inc(hT_ready, 1)
                act.wait_ge(qk_made, f + 1)
                at_least(act, q_lo_ready, f)
                at_least(act, sq_ready, f)
                act.activation(qT[:], p_n[:, 0:S], ACT.Copy).then_inc(qT_ready, 1)
                at_least(act, k_lo_ready, f)
                act.activation(kT[:], p_n[:, S:2 * S], ACT.Copy).then_inc(kT_ready, 1)
            if isinstance(n, int) and n == EARLY + 7:
                gating.act_exp(act)
            if batch_valid(t):
                act.wait_ge(probs_turned, 3 * t + 3)
                act.activation(probT1[:], p_t[0][:].rearrange("p (h q) -> p h q", h=H1), ACT.Copy).then_inc(probT_ready, 1)
            if batch_valid(m):
                act_exp(act, m, o, 0, p_s0, prob0)
            if batch_valid(w):
                act.wait_ge(ln2.xn_turned, w + 1)
                at_least(act, logits_made, w)
                at_least(act, h_lo_ready, w)
                scale, bias = k.mod[:, 1, CB, bass.ds(w, 1)], k.mod[:, 1, SB, bass.ds(w, 1)]
                act.activation(hT2[:], p_m[:, 0:S], ACT.Identity, bias=bias, scale=scale).then_inc(hT2_ready, 1)
                act.activation(k.h_hi[:, bass.ds(w, 1), :].rearrange("p o s -> p (o s)"), p_m[:, 0:S], ACT.Identity,
                               bias=bias, scale=scale).then_inc(h_hi_ready, 1)
            if batch_valid(f):
                act.wait_ge(kT_ready, f + 1)
                at_least(act, scored, 2 * m)
                act.activation(k_hi[r][:], kT[:], ACT.Copy).then_inc(k_hi_ready, 1)
                act.wait_ge(q_min_ready, f + 1)
                at_least(act, sq_ready, f)
                act.activation(q_exp[:], q_min[:], ACT.Exp).then_inc(q_exp_ready, 1)
            if batch_valid(t):
                act.wait_ge(pv_made, t + 1)
                at_least(act, y_made, t)
                act.activation(OT[:], p_o[:, 0:S], ACT.Copy).then_inc(OT_ready, 1)
            if batch_valid(m):
                act_exp(act, m, o, 1, p_s1, prob1)
                act.wait_ge(v_made, m + 1)
                at_least(act, pv_made, n - 2)
                act.activation(V[o][:], p_m[:, 0:NT * D].rearrange("p (i d) -> p i d", i=NT), ACT.Copy
                               ).then_inc(v_ready, 1)

        def dve_max(dve, m, i, bank):
            dve.wait_ge(scored, 2 * m + i + 1)
            at_least(dve, exped, 2 * m)
            dve.tensor_reduce(rowmax[:, i, :], bank[:], AX.X, ALU.max).then_inc(maxed, 1)
            dve.wait_ge(maxed, 2 * m + i + 1)
            dve.tensor_scalar(negmax[:, i, :], rowmax[:, i, :], -1.0, None, ALU.mult).then_inc(negmax_ready, 1)

        def dve_step(dve, n, r):
            f, m, s, y, z, w = n, n - 1, n - 2, n - 4, n - 5, n - 6
            o = (r + 1) % 2
            if batch_valid(s):
                dve.wait_ge(exped, 2 * s + 2)
                at_least(dve, probs_ready, s)
                dve.reciprocal(rsums[:], sums[:]).then_inc(rsums_ready, 1)
            if batch_valid(f + 1):
                ln.dve_stats(dve, f + 1)
            if batch_valid(z):
                wait_apart(dve, k, x_added, z + 1)
                ln2.dve_stats(dve, z)
            if batch_valid(m):
                dve_max(dve, m, 0, p_s0)
            if batch_valid(f):
                dve.wait_ge(qT_ready, f + 1)
                at_least(dve, q_exp_ready, f)
                dve.tensor_scalar(q_min[:], qT[:], 0.0, None, ALU.min).then_inc(q_min_ready, 1)
                at_least(dve, scored, 2 * m)
                for h in range(H1):
                    rows = slice(h * DH1, (h + 1) * DH1)
                    ins = dve.tensor_copy(q_hi[r][rows, h, :], qT[rows, :])
                ins.then_inc(q_hi_ready, 1)
            if batch_valid(f + 1):
                ln.dve_normalise(dve, f + 1)
            if batch_valid(m):
                dve_max(dve, m, 1, p_s1)
            if batch_valid(f):
                dve.wait_ge(k_hi_ready, f + 1)
                dve.tensor_tensor(k_lo[r][:], kT[:], k_hi[r][:].bitcast(F32), ALU.subtract).then_inc(k_lo_ready, 1)
            if batch_valid(w):
                dve.wait_ge(h_hi_ready, w + 1)
                dve.wait_ge(hT2_ready, w + 1)
                at = bass.ds(w, 1)
                dve.tensor_tensor(k.h_lo[:, at, :].rearrange("p o s -> p (o s)"), hT2[:],
                                  k.h_hi[:, at, :].rearrange("p o s -> p (o s)").bitcast(F32), ALU.subtract
                                  ).then_inc(h_lo_ready, 1)
            read = p_n[:].rearrange("p (i c) -> p i c", i=NT)
            if batch_valid(m):
                dve.wait_ge(a_made, m + 1)
                dve.tensor_scalar(den[:], read[:, :, D:D + H1], 1e-6, None, ALU.add).then_inc(den_ready, 1)
            if batch_valid(y):
                dve.wait_ge(y_turned, y + 1)
                x = k.X[:, bass.ds(y * NT, NT), :]
                dve.tensor_tensor(x, x, p_m[:, 0:S].rearrange("p (i d) -> p i d", i=NT), ALU.add).then_inc(x_added, 1)
            if batch_valid(m):
                dve.wait_ge(den_ready, m + 1)
                dve.reciprocal(rden[:], den[:]).then_inc(rden_ready, 1)
            if batch_valid(w):
                dve.wait_ge(logits_made, w + 1)
                dve.tensor_tensor(k.logits[:, bass.ds(w * NT, NT), :],
                                  p_t[1][:, 0:NT * E].rearrange("p (i e) -> p i e", i=NT),
                                  k.bg[:].unsqueeze(1).to_broadcast([P, NT, E]), ALU.add).then_inc(logits_ready, 1)
            if batch_valid(m):
                dve.wait_ge(rden_ready, m + 1)
                at_least(dve, pv_made, n - 2)
                for i in range(NT):
                    ins = dve.tensor_tensor(A[o][:, i], read[:, i, 0:D].rearrange("p (h d) -> p h d", h=H1),
                                            rden[:, i, :].unsqueeze(2).to_broadcast([P, H1, DH1]), ALU.mult)
                ins.then_inc(A_ready, 1)
            if batch_valid(f):
                dve.wait_ge(q_hi_ready, f + 1)
                for h in range(H1):
                    rows = slice(h * DH1, (h + 1) * DH1)
                    ins = dve.tensor_tensor(q_lo[r][rows, h, :], qT[rows, :], q_hi[r][rows, h, :].bitcast(F32),
                                            ALU.subtract)
                ins.then_inc(q_lo_ready, 1)
            if batch_valid(z):
                ln2.dve_normalise(dve, z)
            if batch_valid(f):
                dve.wait_ge(q_exp_ready, f + 1)
                at_least(dve, a_made, m)
                dve.scalar_tensor_tensor(out=sq[r][:], in0=qT[:], scalar=0.0, in1=q_exp[:], op0=ALU.max, op1=ALU.add
                                         ).then_inc(sq_ready, 1)
            if isinstance(n, int) and n == EARLY + 6:
                dve.wait_ge(logits_ready, EARLY)
                dve.wait_ge(beats_cleared, 1)
                gating.dve_rank(dve)
            if isinstance(n, int) and n == EARLY + 7:
                gating.dve_weigh(dve)
            if isinstance(n, int) and n == EARLY + 8:
                gating.dve_split(dve)

        def pool_step(pool, n, r):
            s, z = n - 2, n - 5
            if batch_valid(n + 1):
                ln.pool_rstd(pool, n + 1)
            if batch_valid(z):
                ln2.pool_rstd(pool, z)
            if batch_valid(s):
                wait_apart(pool, k, rsums_ready, s + 1)
                for i, prob in enumerate((prob0, prob1)):
                    for h in range(H1):
                        ins = pool.tensor_scalar(prob[r][:, h, :], prob[r][:, h, :], rsums[:, i, h:h + 1], 0.0,
                                                 ALU.mult, ALU.add)
                ins.then_inc(probs_ready, 1)

        WHOLE0, LOOPS, LAST = 6, 4, B + 6
        block = ctx.enter_context(nc.Block())

        def walk(eng, step, last=LAST):
            for n in range(WHOLE0):
                step(eng, n, n % 2)
            with eng.Fori(0, LOOPS) as turn:
                for r in range(2):
                    step(eng, turn * 2 + (WHOLE0 + r), (WHOLE0 + r) % 2)
            for n in range(WHOLE0 + 2 * LOOPS, last):
                step(eng, n, n % 2)

        @block.gpsimd
        def _(pool):
            for n in range(2):
                pool.memset(q_hi[n][:].bitcast(F32), 0.0)
                ins = pool.memset(q_lo[n][:].bitcast(F32), 0.0)
            ins.then_inc(cleared, 1)
            ln.pool_rstd(pool, 0)
            pool.memset(k.beats[:], 0.0).then_inc(beats_cleared, 1)
            pool.memset(k.comb16[:], 0.0)
            walk(pool, pool_step, B + 5)

        @block.tensor
        def _(pe):
            pe.wait_ge(cleared, 1)
            walk(pe, pe_step)

        @block.scalar
        def _(act):
            walk(act, act_step)

        @block.vector
        def _(dve):
            dve.wait_ge(cleared, 1)
            ln.dve_stats(dve, 0)
            ln.dve_normalise(dve, 0)
            walk(dve, dve_step)


U = 2 * S
UNITS = B * S // U
UT = U // P


def moe_weight_steps(k, sem, banks):
    w = Names()
    turned = sem("moe_turned")
    hi_ready = sem("moe_hi_ready")
    lo_ready = sem("moe_lo_ready")

    def dest(g, part):
        if g < MOE_GU_GROUPS:
            return k.w["gu_" + part][:, 2 * g:2 * g + 2].rearrange("p e c o -> p (e c) o")
        at = 4 * (g - MOE_GU_GROUPS)
        return k.w["dn_" + part][:, at:at + 4, :]

    def bank(g):
        return banks[g % len(banks)].rearrange("p m s -> p (m s)").rearrange("p (j d) -> p j d", j=4)

    def pe_group(pe, g):
        pe.wait_ge(k.late_loaded, LATE_LOADED)
        at_least(pe, lo_ready, g - len(banks) + 1)
        for j in range(4):
            mm = pe.transpose(bank(g)[:, j, :], k.raw_moe[:, 4 * g + j, :], k.ident[:])
        mm.then_inc(turned, 1)

    def act_group(act, g):
        act.wait_ge(turned, g + 1)
        act.activation(dest(g, "hi"), bank(g), ACT.Copy).then_inc(hi_ready, 1)

    def dve_group(dve, g):
        dve.wait_ge(hi_ready, g + 1)
        dve.tensor_tensor(dest(g, "lo"), bank(g), dest(g, "hi").bitcast(F32), ALU.subtract).then_inc(lo_ready, 1)

    w.pe_group, w.act_group, w.dve_group = pe_group, act_group, dve_group
    return w


def gating_tensors(k, wsb):
    k.top = wsb("top", [P, TILES_ALL])
    k.shifted = wsb("shifted", [P, TILES_ALL, E])
    k.weight = wsb("weight", [P, TILES_ALL, E])
    k.beats = wsb("beats", [P, TILES_ALL, E, E])
    k.rank = wsb("rank", [P, TILES_ALL, E])
    k.total = wsb("total", [P, TILES_ALL])
    k.rtotal = wsb("rtotal", [P, TILES_ALL])
    k.wrest = wsb("wrest", [P, TILES_ALL, E])
    k.wparts = wsb("wparts", [P, TILES_ALL, CP, E], BF16)
    k.comb16 = wsb("comb16", [P, TILES_ALL, P], BF16)


def gating_steps(k, sem, t0, t1):
    g = Names()
    g.chain = sem("gating_chain")
    g.shifted_ready = sem("gating_shifted_ready")
    g.weight_ready = sem("gating_weight_ready")
    g.parts_ready = sem("gating_parts_ready")
    g.count = 0
    tiles = slice(t0, t1)
    shape = [P, t1 - t0, E]
    logits, top, shifted, weight, rank = (x[:, tiles] for x in (k.logits, k.top, k.shifted, k.weight, k.rank))

    def then(dve, ins):
        g.count += 1
        ins.then_inc(g.chain, 1)
        dve.wait_ge(g.chain, g.count)

    def dve_rank(dve):
        then(dve, dve.tensor_reduce(top, logits, AX.X, ALU.max))
        dve.tensor_tensor(shifted, logits, top.unsqueeze(2).to_broadcast(shape), ALU.subtract
                          ).then_inc(g.shifted_ready, 1)
        for e in range(E):
            for lo, hi, op in ((0, e, ALU.is_ge), (e + 1, E, ALU.is_gt)):
                if hi > lo:
                    ins = dve.tensor_tensor(k.beats[:, tiles, e, lo:hi], logits[:, :, lo:hi],
                                            logits[:, :, e:e + 1].to_broadcast([P, t1 - t0, hi - lo]), op)
        then(dve, ins)
        then(dve, dve.tensor_reduce(rank, k.beats[:, tiles], AX.X, ALU.add))

    def act_exp(act):
        act.wait_ge(g.shifted_ready, 1)
        act.activation(weight, shifted, ACT.Exp).then_inc(g.weight_ready, 1)

    def dve_weigh(dve):
        total, rtotal = k.total[:, tiles], k.rtotal[:, tiles]
        dve.wait_ge(g.weight_ready, 1)
        then(dve, dve.scalar_tensor_tensor(out=weight, in0=rank, scalar=TOP - 0.5, in1=weight,
                                           op0=ALU.is_lt, op1=ALU.mult))
        then(dve, dve.tensor_reduce(total, weight, AX.X, ALU.add))
        then(dve, dve.reciprocal(rtotal, total))
        then(dve, dve.tensor_tensor(weight, weight, rtotal.unsqueeze(2).to_broadcast(shape), ALU.mult))

    def dve_split(dve):
        rest, parts = k.wrest[:, tiles], k.wparts[:, tiles]
        then(dve, dve.tensor_copy(parts[:, :, 0, :], weight))
        then(dve, dve.tensor_tensor(rest, weight, parts[:, :, 0, :], ALU.subtract))
        then(dve, dve.tensor_copy(parts[:, :, 1, :], rest))
        dve.tensor_tensor(parts[:, :, 2, :], rest, parts[:, :, 1, :], ALU.subtract).then_inc(g.parts_ready, 1)

    g.dve_rank, g.act_exp, g.dve_weigh, g.dve_split = dve_rank, act_exp, dve_weigh, dve_split
    return g


def router(nc, k, wsb):
    with ExitStack() as ctx:
        sb, ps, sem = tensors(nc, ctx, "router")
        g = gating_steps(k, sem, EARLY * NT, TILES_ALL)
        p_c = [ps(f"p_c{n}", [P, 4, P], BF16) for n in range(2)]
        comb_turned = sem("comb_turned")
        comb_ready = sem("comb_ready")
        block = ctx.enter_context(nc.Block())

        @block.tensor
        def _(pe):
            for u in range(TILES_ALL // 4):
                if 4 * u + 4 > EARLY * NT:
                    pe.wait_ge(g.parts_ready, 1)
                at_least(pe, comb_ready, u - 1)
                for j in range(4):
                    mm = pe.transpose(p_c[u % 2][0:CP * E, j, :],
                                      k.wparts[:, 4 * u + j].rearrange("p c e -> p (c e)"), k.ident16[:])
                mm.then_inc(comb_turned, 1)

        @block.scalar
        def _(act):
            g.act_exp(act)
            for u in range(TILES_ALL // 4):
                act.wait_ge(comb_turned, u + 1)
                act.activation(k.comb16[0:CP * E, 4 * u:4 * u + 4, :], p_c[u % 2][0:CP * E], ACT.Copy
                               ).then_inc(comb_ready, 1)

        @block.vector
        def _(dve):
            g.dve_rank(dve)
            g.dve_weigh(dve)
            g.dve_split(dve)


def experts(nc, k, out):
    with ExitStack() as ctx:
        sb, ps, sem = tensors(nc, ctx, "moe")
        LAG = 3
        RING = 4
        act_g = [sb(f"act_g{n}", [P, U]) for n in range(2)]
        act_u = [sb(f"act_u{n}", [P, U]) for n in range(2)]
        z = [sb(f"z{n}", [P, U]) for n in range(RING)]
        z_hi = [sb(f"z_hi{n}", [P, U], F32R) for n in range(RING)]
        z_lo = [sb(f"z_lo{n}", [P, U], F32R) for n in range(RING)]
        yT = sb("yT", [P, U])
        p_g = [ps(f"p_g{n}", [P, U]) for n in range(2)]
        p_u = [ps(f"p_u{n}", [P, U]) for n in range(2)]
        p_c = [ps(f"p_c{n}", [P, U]) for n in range(2)]
        p_y = ps("p_y", [P, U])
        p_m = ps("p_m", [P, U])
        c_made = sem("c_made")
        gate_made = sem("gate_made")
        up_made = sem("up_made")
        silu_ready = sem("silu_ready")
        prod_ready = sem("prod_ready")
        z_ready = sem("z_ready")
        z_hi_ready = sem("z_hi_ready")
        z_lo_ready = sem("z_lo_ready")
        down_made = sem("down_made")
        yT_ready = sem("yT_ready")
        y_turned = sem("y_turned")
        x_added = sem("x_added")
        stored = sem("stored")

        def tokens(h, u):
            return h[:, bass.ds(u * 2, 2), :].rearrange("p b s -> p (b s)")

        def pe_down(pe, u, e):
            i = u * E + e
            pe.wait_ge(z_lo_ready, i + 1)
            if e == 0:
                at_least(pe, yT_ready, u)
            r = e % RING
            mm = split_product(pe, p_y[:], (k.w["dn_hi"][:, e, :], k.w["dn_lo"][:, e, :]), (z_hi[r][:], z_lo[r][:]),
                               e == 0, e == E - 1)
            mm.then_inc(down_made, 1)

        def pe_turn(pe, u):
            pe.wait_ge(yT_ready, u + 1)
            at_least(pe, x_added, u)
            for j in range(UT):
                mm = pe.transpose(p_m[:, j * P:(j + 1) * P], yT[:, j * P:(j + 1) * P], k.ident[:])
            mm.then_inc(y_turned, 1)

        def pe_unit(pe, u, first=False):
            for e in range(E):
                i = u * E + e
                at_least(pe, z_ready, i - 1)
                pe.matmul(p_c[e % 2][:], k.sel16[:, e, :],
                          k.comb16[:, bass.ds(u * UT, UT), :].rearrange("p t q -> p (t q)"), start=True, stop=True
                          ).then_inc(c_made, 1)
                for c, bank, made in ((0, p_g[e % 2], gate_made), (1, p_u[e % 2], up_made)):
                    split_product(pe, bank[:], (k.w["gu_hi"][:, e, c, :], k.w["gu_lo"][:, e, c, :]),
                                  (tokens(k.h_hi, u), tokens(k.h_lo, u)), True, True).then_inc(made, 1)
                if e >= LAG:
                    pe_down(pe, u, e - LAG)
                elif not first:
                    pe_down(pe, u - 1, E - LAG + e)
                if e == LAG + 1 and not first:
                    pe_turn(pe, u - 1)

        def act_hi(act, u, e):
            i = u * E + e
            act.wait_ge(z_ready, i + 1)
            at_least(act, down_made, i - RING + 1)
            act.activation(z_hi[e % RING][:], z[e % RING][:], ACT.Copy).then_inc(z_hi_ready, 1)

        def act_y(act, u):
            act.wait_ge(down_made, (u + 1) * E)
            at_least(act, y_turned, u)
            for c in range(2):
                ins = act.activation(yT[:, c * S:(c + 1) * S], p_y[:, c * S:(c + 1) * S], ACT.Copy,
                                     scale=k.mod[:, 1, GB, bass.ds(u * 2 + c, 1)])
            ins.then_inc(yT_ready, 1)

        def act_unit(act, u, first=False):
            for e in range(E):
                i = u * E + e
                if e == LAG and not first:
                    act_y(act, u - 1)
                act.wait_ge(gate_made, i + 1)
                at_least(act, prod_ready, i - 1)
                act.activation(act_g[e % 2][:], p_g[e % 2][:], ACT.Silu).then_inc(silu_ready, 1)
                if e >= 1:
                    act_hi(act, u, e - 1)
                elif not first:
                    act_hi(act, u - 1, E - 1)

        def dve_add(dve, u):
            dve.wait_ge(y_turned, u + 1)
            x = k.X[:, bass.ds(u * UT, UT), :]
            dve.tensor_tensor(x, x, p_m[:].rearrange("p (t d) -> p t d", t=UT), ALU.add).then_inc(x_added, 1)

        def dve_unit(dve, u, first=False):
            for e in range(E):
                i = u * E + e
                dve.wait_ge(silu_ready, i + 1)
                dve.wait_ge(up_made, i + 1)
                dve.tensor_tensor(act_u[e % 2][:], act_g[e % 2][:], p_u[e % 2][:], ALU.mult).then_inc(prod_ready, 1)
                dve.wait_ge(prod_ready, i + 1)
                dve.wait_ge(c_made, i + 1)
                at_least(dve, z_lo_ready, i - RING + 1)
                dve.tensor_tensor(z[e % RING][:], act_u[e % 2][:], p_c[e % 2][:], ALU.mult).then_inc(z_ready, 1)
                if e == LAG + 2 and not first:
                    dve_add(dve, u - 1)

        def pool_unit(pool, u):
            for e in range(E):
                i = u * E + e
                pool.wait_ge(z_hi_ready, i + 1)
                at_least(pool, down_made, i - RING + 1)
                pool.tensor_tensor(z_lo[e % RING][:], z[e % RING][:], z_hi[e % RING][:].bitcast(F32), ALU.subtract
                                   ).then_inc(z_lo_ready, 1)

        x_out = out.rearrange("b (i p) d -> p (b i) d", p=P)
        block = ctx.enter_context(nc.Block())

        @block.gpsimd
        def _(pool):
            pool_unit(pool, 0)
            with pool.Fori(1, UNITS) as u:
                pool_unit(pool, u)

        @block.tensor
        def _(pe):
            pe_unit(pe, 0, first=True)
            with pe.Fori(1, UNITS) as u:
                pe_unit(pe, u)
            for e in range(E - LAG, E):
                pe_down(pe, UNITS - 1, e)
            pe_turn(pe, UNITS - 1)

        @block.scalar
        def _(act):
            act_unit(act, 0, first=True)
            with act.Fori(1, UNITS) as u:
                act_unit(act, u)
            act_hi(act, UNITS - 1, E - 1)
            act_y(act, UNITS - 1)

        @block.vector
        def _(dve):
            dve_unit(dve, 0, first=True)
            with dve.Fori(1, UNITS) as u:
                dve_unit(dve, u)
            dve_add(dve, UNITS - 1)

        @block.sync
        def _(sp):
            with sp.Fori(0, UNITS) as u:
                sp.wait_ge(x_added, u + 1)
                at = bass.ds(u * UT, UT)
                sp.dma_start(x_out[:, at, :], k.X[:, at, :]).then_inc(stored, 16)
            sp.wait_ge(stored, 16 * UNITS)


def build(nc, a, out):
    k = Names()
    k.w = {}
    with ExitStack() as ctx:
        sb, ps, sem = tensors(nc, ctx, "top")
        k.X = sb("X", [P, B * NT, D])
        k.ident = sb("ident", [P, P])
        k.ident16 = sb("ident16", [P, P], BF16)
        k.minus_half = sb("minus_half", [P, 8])
        k.parity = sb("parity", [P, 2])
        k.mod = sb("mod", [P, 2, 6, B])
        k.wq0, k.wk0, k.wv0, k.wo0 = (sb(f"w{x}0", [P, D]) for x in "qkvo")
        k.bq0, k.bk0, k.bo0 = (sb(f"b{x}0", [P, 1]) for x in "qko")
        k.gbo0 = sb("gbo0", [P, B])
        k.ffn_scales = sb("ffn_scales", [P, 4, FB])
        k.ab_scale = sb("ab_scale", [P, FB])
        k.half_s1 = sb("half_s1", [P, FB])
        k.w3_scale = sb("w3_scale", [P, 1])
        k.w3_gate = sb("w3_gate", [P, B])
        k.raw_ffn = sb("raw_ffn", [P, FFN_BLOCKS, D])
        k.raw_att1 = sb("raw_att1", [P, 4, D])
        k.raw_moe = sb("raw_moe", [P, 3 * E, D])
        k.raw_g = sb("raw_g", [E, D])
        k.bg = sb("bg", [P, E])
        k.bo1 = sb("bo1", [P, 1])
        k.beta = sb("beta", [P, 1 + H1])
        k.memz = sb("memz", [P, D + H1])
        k.x_loaded = sem("x_loaded")
        k.late_loaded = sem("late_loaded")
        k.waits_passed = sem("waits_passed")
        with ExitStack() as phase:
            wsb, _, _ = tensors(nc, phase, "att0p")
            k.Q = [wsb(f"Q{n}", [P, H0, S], BF16) for n in range(NB)]
            k.K = [wsb(f"K{n}", [P, PAIRS, S], BF16) for n in range(NB)]
            k.V = [wsb(f"V{n}", [P, NT, H0, 32]) for n in range(NB)]
            prepare(nc, k, a)
            attention0(nc, k, a)
        wsb, _, _ = tensors(nc, ctx, "w")
        attention1_weights(nc, k, wsb)
        for part in ("hi", "lo"):
            k.w["gu_" + part] = wsb("gu_" + part, [P, E, 2, P], F32R)
            k.w["dn_" + part] = wsb("dn_" + part, [P, E, P], F32R)
        with ExitStack() as phase:
            fsb, _, _ = tensors(nc, phase, "ffn0")
            ffn_weights(nc, k, fsb)
            ffn0(nc, k)
        k.h_hi = wsb("h_hi", [P, B, S], F32R)
        k.h_lo = wsb("h_lo", [P, B, S], F32R)
        k.logits = wsb("logits", [P, B * NT, E])
        gating_tensors(k, wsb)
        attention1(nc, k)
        router(nc, k, wsb)
        experts(nc, k, out)


_INS = [
    "L0_attn_x", "L0_attn_Wq", "L0_attn_bq", "L0_attn_Wl", "L0_attn_bl", "L0_attn_Wk", "L0_attn_bk", "L0_attn_Wv",
    "L0_attn_bv", "L0_attn_Wo", "L0_attn_bo", "L0_ffn_w1_w", "L0_ffn_w1_s", "L0_ffn_w2_w", "L0_ffn_w2_s",
    "L0_ffn_h1_w", "L0_ffn_h1_s", "L0_ffn_h2_w", "L0_ffn_h2_s", "L0_ffn_w3_w", "L0_ffn_w3_s", "L0_c", "L0_wmod",
    "L1_attn_Wq", "L1_attn_Wk", "L1_attn_Wv", "L1_attn_Wo", "L1_attn_bo", "L1_attn_betas", "L1_attn_mem",
    "L1_attn_z", "L1_ffn_Wg", "L1_ffn_bg", "L1_ffn_w1", "L1_ffn_w2", "L1_c", "L1_wmod",
]


def kernel(**inputs):
    import numpy as np
    import concourse.bacc as bacc
    from concourse.bass_utils import run_bass_kernel_spmd

    nc = bacc.Bacc("TRN2", target_bir_lowering=False, num_devices=1)
    arrays, aps = {}, {}
    for name in _INS:
        array = np.ascontiguousarray(inputs[name])
        arrays[f"in_{name}"] = array
        aps[name] = nc.dram_tensor(f"in_{name}", array.shape, mybir.dt.from_np(array.dtype), kind="ExternalInput").ap()
    out = nc.dram_tensor("out_x", (B, S, D), F32, kind="ExternalOutput").ap()
    build(nc, aps, out)
    result = run_bass_kernel_spmd(nc, [arrays], core_ids=[0])
    return result.results[0]["out_x"]
```
